# Optimizing a Trainium2 kernel written in Bass

```python
import numpy as np
import jax
import jax.numpy as jnp

def _softmax(x, axis=-1):
    return jax.nn.softmax(x, axis=axis)

def _gelu(x):
    return jax.nn.gelu(x, approximate=True)

def _silu(x):
    return jax.nn.silu(x)

def _sigmoid(x):
    return jax.nn.sigmoid(x)

def _layernorm(x, axis=-1, eps=1e-05):
    m = jnp.mean(x, axis=axis, keepdims=True)
    v = jnp.var(x, axis=axis, keepdims=True)
    return (x - m) / jnp.sqrt(v + eps)

def _scatter_add(tgt, idx, src, axis=0):
    return tgt.at[idx].add(src)

def _segment_sum(src, seg, n):
    return jax.ops.segment_sum(src, seg, n)
kernel_name = 'mk_seq_postln_d1_jaxref_r8_f273ab'

def setup_inputs(seed: int=0):
    np.random.seed(seed)
    _w = jnp.asarray

    def _L0_attn_setup():
        import jax, jax.numpy as jnp
        import numpy as np
        H, DK, DV = (6, 32, 64)
        HID = 256
        CONV = 4
        NORM_EPS = 1e-05

        def causal_dwconv_silu(x, w):
            K = w.shape[1]
            xp = jnp.pad(x, ((0, 0), (K - 1, 0), (0, 0)))
            y = jax.lax.conv_general_dilated(jnp.transpose(xp, (0, 2, 1)), w[:, None, :], (1,), 'VALID', feature_group_count=w.shape[0])
            return jax.nn.silu(jnp.transpose(y, (0, 2, 1)))

        def l2norm(x, eps=1e-06):
            return x * jax.lax.rsqrt(jnp.sum(x * x, axis=-1, keepdims=True) + eps)
        key = jax.random.key(seed)
        ks = jax.random.split(key, 16)
        B, T = (2, 512)
        s = HID ** (-0.5)
        return dict(hidden_states=jax.random.normal(ks[0], (B, T, HID), jnp.float32), Wq=jax.random.normal(ks[1], (H * DK, HID), jnp.float32) * s, Wk=jax.random.normal(ks[2], (H * DK, HID), jnp.float32) * s, Wv=jax.random.normal(ks[3], (H * DV, HID), jnp.float32) * s, Wb=jax.random.normal(ks[4], (H, HID), jnp.float32) * s, Wa=jax.random.normal(ks[5], (H, HID), jnp.float32) * s, A_log=jnp.log(jax.random.uniform(ks[6], (H,), jnp.float32, 0.5, 16.0)), dt_bias=jax.random.normal(ks[7], (H,), jnp.float32) * 0.1, conv_wq=jax.random.normal(ks[8], (H * DK, CONV), jnp.float32) * 0.5, conv_wk=jax.random.normal(ks[9], (H * DK, CONV), jnp.float32) * 0.5, conv_wv=jax.random.normal(ks[10], (H * DV, CONV), jnp.float32) * 0.5, Wg=jax.random.normal(ks[11], (H * DV, HID), jnp.float32) * s, norm_w=jnp.ones((DV,), jnp.float32), Wo=jax.random.normal(ks[12], (HID, H * DV), jnp.float32) * (H * DV) ** (-0.5))
    _L0_attn_in = _L0_attn_setup()

    def _L0_ffn_setup():
        import jax, jax.numpy as jnp
        import numpy as np

        def ternary_quantize(t, threshold, scale):
            return jnp.where(t > threshold, scale, jnp.where(t < -threshold, -scale, 0.0)).astype(t.dtype)
        key = jax.random.key(seed)
        k1, k2, k3 = jax.random.split(key, 3)
        B, S, D = (4, 512, 256)
        x = jax.random.normal(k1, (B, S, D), dtype=jnp.float32)
        weight = jax.random.normal(k2, (D, D), dtype=jnp.float32) * 0.02
        rram_variation = jax.random.normal(k3, (D, D), dtype=jnp.float32) * 0.05
        return {'x': x, 'weight': weight, 'rram_variation': rram_variation}
    _L0_ffn_in = _L0_ffn_setup()
    _d = {'L0_attn_hidden_states': _L0_attn_in['hidden_states'], 'L0_attn_Wq': _L0_attn_in['Wq'], 'L0_attn_Wk': _L0_attn_in['Wk'], 'L0_attn_Wv': _L0_attn_in['Wv'], 'L0_attn_Wb': _L0_attn_in['Wb'], 'L0_attn_Wa': _L0_attn_in['Wa'], 'L0_attn_A_log': _L0_attn_in['A_log'], 'L0_attn_dt_bias': _L0_attn_in['dt_bias'], 'L0_attn_conv_wq': _L0_attn_in['conv_wq'], 'L0_attn_conv_wk': _L0_attn_in['conv_wk'], 'L0_attn_conv_wv': _L0_attn_in['conv_wv'], 'L0_attn_Wg': _L0_attn_in['Wg'], 'L0_attn_norm_w': _L0_attn_in['norm_w'], 'L0_attn_Wo': _L0_attn_in['Wo'], 'L0_ffn_weight': _L0_ffn_in['weight'], 'L0_ffn_rram_variation': _L0_ffn_in['rram_variation']}
    _x0 = _d['L0_attn_hidden_states']
    _d['L0_attn_hidden_states'] = jax.random.normal(jax.random.fold_in(jax.random.key(seed), 1), (8, 256, 256), dtype=_x0.dtype)
    del _x0
    return _d

def reference(L0_attn_hidden_states, L0_attn_Wq, L0_attn_Wk, L0_attn_Wv, L0_attn_Wb, L0_attn_Wa, L0_attn_A_log, L0_attn_dt_bias, L0_attn_conv_wq, L0_attn_conv_wk, L0_attn_conv_wv, L0_attn_Wg, L0_attn_norm_w, L0_attn_Wo, L0_ffn_weight, L0_ffn_rram_variation):

    def _L0_attn_ref(hidden_states, Wq, Wk, Wv, Wb, Wa, A_log, dt_bias, conv_wq, conv_wk, conv_wv, Wg, norm_w, Wo):
        import jax, jax.numpy as jnp
        import numpy as np
        H, DK, DV = (6, 32, 64)
        HID = 256
        CONV = 4
        NORM_EPS = 1e-05

        def causal_dwconv_silu(x, w):
            K = w.shape[1]
            xp = jnp.pad(x, ((0, 0), (K - 1, 0), (0, 0)))
            y = jax.lax.conv_general_dilated(jnp.transpose(xp, (0, 2, 1)), w[:, None, :], (1,), 'VALID', feature_group_count=w.shape[0])
            return jax.nn.silu(jnp.transpose(y, (0, 2, 1)))

        def l2norm(x, eps=1e-06):
            return x * jax.lax.rsqrt(jnp.sum(x * x, axis=-1, keepdims=True) + eps)
        x = hidden_states
        B, T, _ = x.shape
        q = causal_dwconv_silu(x @ Wq.T, conv_wq).reshape(B, T, H, DK)
        k = causal_dwconv_silu(x @ Wk.T, conv_wk).reshape(B, T, H, DK)
        v = causal_dwconv_silu(x @ Wv.T, conv_wv).reshape(B, T, H, DV)
        beta = jax.nn.sigmoid(x @ Wb.T)
        g = -jnp.exp(A_log) * jax.nn.softplus(x @ Wa.T + dt_bias)
        q = l2norm(q) * DK ** (-0.5)
        k = l2norm(k)

        def step(S, inp):
            qt, kt, vt, gt, bt = inp
            S = S * jnp.exp(gt)[..., None, None]
            v_new = vt - jnp.einsum('bhk,bhkv->bhv', kt, S)
            S = S + bt[..., None, None] * (kt[..., :, None] * v_new[..., None, :])
            o = jnp.einsum('bhk,bhkv->bhv', qt, S)
            return (S, o)
        S0 = jnp.zeros((B, H, DK, DV), x.dtype)
        tm = lambda a: jnp.moveaxis(a, 1, 0)
        _, o = jax.lax.scan(step, S0, (tm(q), tm(k), tm(v), tm(g), tm(beta)))
        o = jnp.moveaxis(o, 0, 1)
        var = jnp.mean(jnp.square(o.astype(jnp.float32)), axis=-1, keepdims=True)
        o = o * jax.lax.rsqrt(var + NORM_EPS).astype(o.dtype) * norm_w
        gate = (x @ Wg.T).reshape(B, T, H, DV)
        o = o * jax.nn.silu(gate)
        return o.reshape(B, T, H * DV) @ Wo.T

    def _L0_ffn_ref(x, weight, rram_variation):
        import jax, jax.numpy as jnp
        import numpy as np

        def ternary_quantize(t, threshold, scale):
            return jnp.where(t > threshold, scale, jnp.where(t < -threshold, -scale, 0.0)).astype(t.dtype)
        TH_X, SC_X = (0.33, 0.5)
        TH_W, SC_W = (0.2, 0.6)
        x_q = ternary_quantize(x, TH_X, SC_X)
        w_q = ternary_quantize(weight, TH_W, SC_W)
        w_rram = w_q + rram_variation
        return jnp.einsum('bsd,od->bso', x_q, w_rram)
    x = L0_attn_hidden_states
    x = _layernorm(x + _L0_attn_ref(x, L0_attn_Wq, L0_attn_Wk, L0_attn_Wv, L0_attn_Wb, L0_attn_Wa, L0_attn_A_log, L0_attn_dt_bias, L0_attn_conv_wq, L0_attn_conv_wk, L0_attn_conv_wv, L0_attn_Wg, L0_attn_norm_w, L0_attn_Wo), axis=-1)
    x = _layernorm(x + _L0_ffn_ref(x, L0_ffn_weight, L0_ffn_rram_variation), axis=-1)
    return x

_drawn_inputs = setup_inputs


def setup_inputs(seed=0):
    import zlib

    import numpy as np

    out = dict(_drawn_inputs(seed))
    spreads = {'L0_attn_norm_w': (1.0, 0.2)}
    factors = {}
    for name, (base, spread) in spreads.items():
        noise = np.random.default_rng([zlib.crc32(name.encode()), seed]).standard_normal(out[name].shape)
        drawn = base * np.exp(spread * noise) if base else spread * noise
        out[name] = jnp.asarray(drawn.astype(out[name].dtype))
    for name, factor in factors.items():
        out[name] = (out[name] * factor).astype(out[name].dtype)
    return out
```

```python
from contextlib import ExitStack

import concourse.bass as bass
from concourse import mybir

ALU = mybir.AluOpType
ACT = mybir.ActivationFunctionType
AX = mybir.AxisListType
F32 = mybir.dt.float32
I32 = mybir.dt.int32
BF16 = mybir.dt.bfloat16

P = 128
B, T, HID = 8, 256, 256
H, DK, DV, TAPS = 6, 32, 64, 4
CH = 32
NC = T // CH
PAIRS = B // 2
G3 = 3
U = G3 * NC
TOK = 2 * T
TT = TOK // P
KT = HID // P
CONV_TILES, GATE_TILES = 6, 3
VTILE_LO, VTILE_HI, VTILE_B = 3, 4, 5
HALF = CH // 2
CONV_DEPTH = 4
UH = U // 2

EPS_K = 4e-6
EPS_O = 1e-5 * DK
EPS_LN = 1e-5
TH_X, TH_W, SC_W = 0.33, 0.2, 0.6
RSQRT_MAGIC = 0x5F3759DF

C_QUARTER, C_REP, C_TRI, C_STRICT, C_ONES, C_IDENT = 0, 4, 132, 260, 388, 516
C_UPPER, C_LOWER, C_EYE16, C_ROWA, C_ROWB, C_END = 644, 676, 708, 724, 725, 726

VEC_OWN_FIRST, VEC_OWN_TURN = 229, 141


class OwnResults:

    def __init__(self, eng, sem):
        self.eng, self.sem, self.base, self.n = eng, sem, 0, 0

    def start(self, base):
        self.base, self.n = base, 0

    def __call__(self, instruction, wait=None):
        self.n += 1
        instruction.then_inc(self.sem, 1)
        if wait:
            wait(self.eng, self.sem, self.base + self.n)
        else:
            self.eng.wait_ge(self.sem, self.base + self.n)


def program(nc, x, x_t, w_proj, w_conv, w_ab, a_log, dt_bias, norm_w, w_out, w_ffn, w_rram, consts, out):
    ctx = ExitStack()
    with ctx:
        def sb(name, shape, dt=F32):
            return ctx.enter_context(nc.sbuf_tensor(name, shape, dt))

        def pb(name, shape, dt=F32):
            return ctx.enter_context(nc.psum_tensor(name, shape, dt))

        def sem(name):
            return ctx.enter_context(nc.semaphore(name))

        def view(flat, start, *sizes, dt=F32):
            n = 1
            for size in sizes:
                n *= size
            words = n if dt == F32 else n // 2
            v = flat[:, start:start + words]
            if dt != F32:
                v = v.bitcast(dt)
            names = "abcde"[:len(sizes)]
            return v.rearrange(f"p ({' '.join(names)}) -> p {' '.join(names)}",
                               **dict(zip(names[1:], sizes[1:])))

        cst = sb("cst", [P, C_END])
        xt = sb("xt", [P, KT, B * T])
        wproj = sb("wproj", [P, KT, (CONV_TILES + GATE_TILES) * P])
        wconv = sb("wconv", [P, CONV_TILES, TAPS])
        wab = sb("wab", [P, KT, 2 * H])
        alog = sb("alog", [P, H])
        dtb = sb("dtb", [P, H])
        nw = sb("nw", [P, GATE_TILES])
        nwh = sb("nwh", [P, GATE_TILES])
        wout = sb("wout", [P, GATE_TILES, HID])
        wsplit = sb("wsplit", [P, 3, KT, HID], BF16)
        identb = sb("identb", [P, P], BF16)
        par = sb("par", [P, 5, PAIRS * U])
        park = sb("park", [P, 5, U])
        conv_buf = sb("conv_buf", [P, CONV_DEPTH * TOK])
        tok_buf = sb("tok_buf", [P, G3 * 2 * T])
        gate_buf = sb("gate_buf", [P, GATE_TILES * TOK])
        chunk_buf = sb("chunk_buf", [P, U * CH])
        sub_buf = sb("sub_buf", [P, U * CH])
        hid_buf = sb("hid_buf", [P, TT * HID])
        x1_buf = sb("x1_buf", [P, G3 * 2 * T])
        n_tiles = B * T // P
        rep_rhs = view(gate_buf, 0, n_tiles, 2 * H, 4)
        ab = view(x1_buf, 512, n_tiles, 2 * H)
        abt = view(x1_buf, 512 + n_tiles * 2 * H, n_tiles, 2 * H)
        wf = view(hid_buf, 0, KT, HID)
        wr = view(hid_buf, KT * HID, KT, HID)
        wtmp = view(x1_buf, 0, KT, HID)
        raw = sb("raw", [P, CONV_DEPTH, 2, T + TAPS - 1])
        conv = view(conv_buf, 0, CONV_DEPTH, 2, T)
        kq = sb("kq", [P, G3, 2, T])
        kq_tok = view(tok_buf, 0, G3, 2, NC, DK)
        sq_tok = view(gate_buf, 0, G3, 2, NC, DK)
        ss = sb("ss", [P, G3, 2, NC])
        v_ch = view(x1_buf, 0, G3, 2, T)
        v_tok = sb("v_tok", [P, G3, NC, 2, DV // 2])
        kk = sb("kk", [P, U])
        r2 = sb("r2", [P, U])
        rt = sb("rt", [P, U])
        c2 = sb("c2", [P, U])
        bv = sb("bv", [P, U])
        nceg = sb("nceg", [P, U])
        kc_tok = view(chunk_buf, 0, U, DK)
        qe_tok = view(sub_buf, 0, U, DK)
        kg_tok = sb("kg_tok", [P, U, DK])
        kc_ch = sb("kc_ch", [P, U, CH])
        qe_ch = sb("qe_ch", [P, U, CH])
        gm = sb("gm", [P, U, CH])
        dexp = gm
        dt_m = sb("dt_m", [P, U, CH])
        d_m = view(chunk_buf, 0, U, CH)
        cm = gm
        gd = d_m
        lo = d_m
        a_t = sb("a_t", [P, U, CH])
        l16 = sb("l16", [P, U, HALF])
        l21 = sb("l21", [P, U, CH])
        x16 = sb("x16", [P, U, HALF])
        b16 = view(sub_buf, 0, U, HALF)
        p16 = view(sub_buf, U * HALF, U, HALF)
        x32 = dt_m
        y32 = gm
        t_t = view(chunk_buf, 0, U, CH)
        front_bd = sb("front_bd", [P, U, P])
        p_bd = front_bd
        kc_bd = sb("kc_bd", [P, U, P])
        qe_bd = sb("qe_bd", [P, U, P])
        kg_bd = sb("kg_bd", [P, U, P])
        t_bd = sb("t_bd", [P, U, P])
        a_bd = sb("a_bd", [P, U, P])
        rv = sb("rv", [P, G3, NC, DV])
        decay = sb("decay", [P, G3, NC])
        eps_o = sb("eps_o", [P, G3, NC])
        r_sb = sb("r_sb", [P, G3, DV])
        u_sb = sb("u_sb", [P, G3, DV])
        s_sb = sb("s_sb", [P, G3, DV])
        s_dec = sb("s_dec", [P, G3, DV])
        o_all = sb("o_all", [P, G3, NC, DV])
        o_sq = view(x1_buf, 0, U, DV)
        thg = view(x1_buf, 0, TOK)
        gate = view(gate_buf, 0, GATE_TILES, TOK)
        m_o = sb("m_o", [P, U])
        v_o = sb("v_o", [P, U])
        r_o = sb("r_o", [P, U])
        t_o = sb("t_o", [P, U])
        o_ch = view(conv_buf, 0, GATE_TILES, TOK)
        hid = view(hid_buf, 0, TT, HID)
        res = hid
        x1 = view(x1_buf, 0, TT, HID)
        pos = view(tok_buf, 0, TT, HID, dt=BF16)
        xq = view(tok_buf, TT * HID // 2, TT, HID, dt=BF16)
        xq_t = view(tok_buf, TT * HID, TT, KT, P, dt=BF16)
        stats = sb("stats", [P, TT, 6])
        mv = sb("mv", [P, TT, 2])
        v_n = sb("v_n", [P, TT])
        r_n = sb("r_n", [P, TT])
        t_n = sb("t_n", [P, TT])
        y_out = hid

        pj = pb("pj", [P, 2, 512])
        fr = pb("fr", [P, 3, 512])
        pc = pb("pc", [P, 512])
        po = pb("po", [P, 512])
        pg = pb("pg", [P, 512])

        ld_const, ld_x0, ld_x, ld_wproj, ld_small, ld_wout, ld_ffn, ld_res, st_out = (
            sem(n) for n in ("ld_const", "ld_x0", "ld_x", "ld_wproj", "ld_small", "ld_wout", "ld_ffn",
                             "ld_res", "st_out"))
        zeroed, vec_own, act_own, ffn_ready = (sem(n) for n in ("zeroed", "vec_own", "act_own", "ffn_ready"))
        proj_done, tile_out, tanh_done, silu_done, kc_part, on_scaled = (
            sem(n) for n in ("proj_done", "tile_out", "tanh_done", "silu_done", "kc_part", "on_scaled"))
        conv_done = [sem(f"conv_done{j}") for j in range(CONV_TILES)]
        ab_done, ab_in, abt_pos, abt_abs, soft_done, alog_exp, rep_in, rep_done, par_in, cum_done, par_done = (
            sem(n) for n in ("ab_done", "ab_in", "abt_pos", "abt_abs", "soft_done", "alog_exp", "rep_in",
                             "rep_done", "par_in", "cum_done", "par_done"))
        kq_tok_done, sq_done, park_done, gm_done, dexp_mm, dexp_done, dt_done, c2_done, cm_done, bv_done = (
            sem(n) for n in ("kq_tok_done", "sq_done", "park_done", "gm_done", "dexp_mm", "dexp_done",
                             "dt_done", "c2_done", "cm_done", "bv_done"))
        v_tok_done, qe_done, kg_done, kbd_done, ga_mm, at_done, l21_done, y32_done = (
            sem(n) for n in ("v_tok_done", "qe_done", "kg_done", "kbd_done", "ga_mm", "at_done",
                             "l21_done", "y32_done"))
        p_mm, pbd_done, merge_mm, tt_done = (sem(n) for n in ("p_mm", "pbd_done", "merge_mm", "tt_done"))
        rv_done, vbd_done, abd_done = (sem(n) for n in ("rv_done", "vbd_done", "abd_done"))
        ks_mm, r_done, u_mm, u_done, s_mm, s_done, sdec_done, o_mm, o_out = (
            sem(n) for n in ("ks_mm", "r_done", "u_mm", "u_done", "s_mm", "s_done", "sdec_done", "o_mm",
                             "o_out"))
        gate_mm, gate_tanh, gate_done = (sem(n) for n in ("gate_mm", "gate_tanh", "gate_done"))
        osq_done, on_done, og_done, y_mm, y_in, xq_done, xqt_mm, xqt_done, ffn_mm, ffn_in, out_done = (
            sem(n) for n in ("osq_done", "on_done", "og_done", "y_mm", "y_in", "xq_done", "xqt_mm",
                             "xqt_done", "ffn_mm", "ffn_in", "out_done"))

        N_SMALL = 5
        block = ctx.enter_context(nc.Block())

        def per_unit(t):
            return t.unsqueeze(2)

        def after(eng, semaphore, count, k, per_pair):
            eng.wait_ge(semaphore, k * per_pair + count)

        def wait_apart(eng, semaphore, value):
            if not isinstance(value, int):
                eng.compute_val(value)
                eng.wait_ge(ld_const, 16)
            eng.wait_ge(semaphore, value)

        def first(k):
            return isinstance(k, int) and k == 0

        def last(k):
            return isinstance(k, int) and k == PAIRS - 1

        @block.sync
        def _(sp):
            sp.dma_start(wproj[:, :, 0:P], w_proj.rearrange("k p n -> p k n")[:, :, 0:P]).then_inc(ld_wproj, 16)
            sp.dma_start(xt[:, :, 0:TOK], x_t.rearrange("k p n -> p k n")[:, :, 0:TOK]).then_inc(ld_x0, 16)
            sp.dma_start(wproj[:, :, P:], w_proj.rearrange("k p n -> p k n")[:, :, P:]).then_inc(ld_wproj, 16)
            sp.dma_start(wab[:, :, :], w_ab.rearrange("k p n -> p k n")).then_inc(ld_small, 16)
            sp.dma_start(xt[:, :, TOK:], x_t.rearrange("k p n -> p k n")[:, :, TOK:]).then_inc(ld_x, 16)
            sp.dma_start(wf[:, :, :], w_ffn.rearrange("k p n -> p k n")).then_inc(ld_ffn, 16)
            sp.dma_start(wr[:, :, :], w_rram.rearrange("k p n -> p k n")).then_inc(ld_ffn, 16)
            sp.dma_start(wout[:, :, :], w_out.rearrange("k p n -> p k n")).then_inc(ld_wout, 16)
            x_pairs = x.rearrange("(q b) t c -> q (b t) c", b=2)
            out_pairs = out.rearrange("(q b) t c -> q (b t) c", b=2)

            def move_pair(k):
                if first(k):
                    sp.wait_ge(ffn_ready, 1)
                else:
                    sp.wait_ge(st_out, k * 32)
                sp.dma_start(res[:, :, :], x_pairs[bass.ds(k, 1), :, :].rearrange(
                    "q (n p) c -> p (q n) c", p=P)).then_inc(ld_res, 16)
                for n in range(2):
                    after(sp, out_done, n + 1, k, 2)
                    sp.dma_start(out_pairs[bass.ds(k, 1), n * T:(n + 1) * T, :].rearrange(
                        "q (n p) c -> p (q n) c", p=P), y_out[:, 2 * n:2 * n + 2, :]).then_inc(st_out, 16)

            move_pair(0)
            with sp.Fori(1, PAIRS) as k:
                move_pair(k)
            sp.wait_ge(st_out, 16 * 2 * PAIRS)

        @block.tensor
        def _(pe):
            def project(k, j):
                if not first(k):
                    if j < 2:
                        after(pe, dexp_done, 0, k, 1)
                if not (first(k) and j < 2):
                    after(pe, tile_out, j - 1, k, CONV_TILES)
                for t in range(KT):
                    mm = pe.matmul(pj[:, j % 2, :], wproj[:, t, j * P:(j + 1) * P],
                                   xt[:, t, bass.ds(k * TOK, TOK)], start=(t == 0), stop=(t == KT - 1))
                mm.then_inc(proj_done, 1)

            def gates(k, j):
                if not first(k) or j > 0:
                    after(pe, gate_done, j, k, GATE_TILES)
                if not first(k) and j == 0:
                    after(pe, xqt_done, 0, k, 1)
                for t in range(KT):
                    w = CONV_TILES + j
                    mm = pe.matmul(pg[:, :], wproj[:, t, w * P:(w + 1) * P],
                                   xt[:, t, bass.ds(k * TOK, TOK)], start=(t == 0), stop=(t == KT - 1))
                mm.then_inc(gate_mm, 1)

            def exponents(k):
                after(pe, gm_done, 1, k, 1)
                after(pe, tile_out, CONV_TILES, k, CONV_TILES)
                for n in range(2):
                    mm = pe.matmul(pj[:, n, 0:UH * CH], cst[:, C_STRICT:C_STRICT + P],
                                   gm[:, n * UH:(n + 1) * UH, :].rearrange("p u t -> p (u t)"),
                                   start=True, stop=True)
                mm.then_inc(dexp_mm, 1)

            def chunk_products(k, g):
                if g == 0:
                    after(pe, kbd_done, 1, k, 1)
                    after(pe, silu_done, 3, k, CONV_TILES)
                    if not first(k):
                        after(pe, tt_done, 0, k, 2)
                        after(pe, ffn_in, 0, k - 1, 2)
                for c in range(NC):
                    mm = pe.matmul(fr[:, g, c * 2 * CH:(c + 1) * 2 * CH], front_bd[:, g * NC + c, :],
                                   kq[:, g, :, c * CH:(c + 1) * CH], start=True, stop=True)
                if g == G3 - 1:
                    mm.then_inc(ga_mm, 1)

            def merge(k):
                after(pe, l21_done, 1, k, 1)
                after(pe, y32_done, 1, k, 1)
                after(pe, at_done, 1, k, 1)
                for n in range(2):
                    for u in range(UH):
                        mm = pe.matmul(fr[:, n, u * CH:(u + 1) * CH], front_bd[:, n * UH + u, :],
                                       x32[:, n * UH + u, :], start=True, stop=True)
                    mm.then_inc(p_mm, 1)
                for n in range(2):
                    after(pe, pbd_done, n + 1, k, 2)
                    for u in range(UH):
                        mm = pe.matmul(fr[:, (2, 0)[n], u * CH:(u + 1) * CH], p_bd[:, n * UH + u, :],
                                       y32[:, n * UH + u, :], start=True, stop=True)
                    mm.then_inc(merge_mm, 1)

            def from_state(k, c):
                if c == 0:
                    return
                after(pe, s_done, c, k, NC - 1)
                for g in range(G3):
                    mm = pe.matmul(pc[:, g * DV:(g + 1) * DV], kc_bd[:, g * NC + c, :], s_sb[:, g, :],
                                   start=True, stop=True)
                mm.then_inc(ks_mm, 1)
                after(pe, o_out, c, k, NC)
                for g in range(G3):
                    pe.matmul(po[:, g * DV:(g + 1) * DV], qe_bd[:, g * NC + c, :], s_sb[:, g, :],
                              start=(g == 0), stop=False, skip_group_check=True)

            def solve(k, c):
                if c == 0:
                    after(pe, vbd_done, 2, k, 2)
                    after(pe, abd_done, 3, k, 3)
                    after(pe, rv_done, 1, k, 1)
                else:
                    after(pe, r_done, c, k, NC - 1)
                for g in range(G3):
                    mm = pe.matmul(pc[:, g * DV:(g + 1) * DV], t_bd[:, g * NC + c, :],
                                   rv[:, g, 0, :] if c == 0 else r_sb[:, g, :], start=True, stop=True)
                mm.then_inc(u_mm, 1)

            def to_state(k, c):
                after(pe, u_done, c + 1, k, NC)
                if c < NC - 1:
                    for g in range(G3):
                        mm = pe.matmul(pc[:, g * DV:(g + 1) * DV], kg_bd[:, g * NC + c, :], u_sb[:, g, :],
                                       start=True, stop=True)
                    mm.then_inc(s_mm, 1)
                if c == 0 and not first(k):
                    after(pe, o_out, 0, k, NC)
                for g in range(G3):
                    mm = pe.matmul(po[:, g * DV:(g + 1) * DV], a_bd[:, g * NC + c, :], u_sb[:, g, :],
                                   start=(c == 0 and g == 0), stop=True, skip_group_check=True)
                mm.then_inc(o_mm, 1)

            def project_out(k):
                after(pe, og_done, GATE_TILES, k, GATE_TILES)
                if not last(k):
                    after(pe, tt_done, 2, k + 1, 2)
                for n in range(TT):
                    for j in range(GATE_TILES):
                        mm = pe.matmul(fr[:, n // 2, (n % 2) * HID:(n % 2 + 1) * HID],
                                       o_ch[:, j, n * P:(n + 1) * P], wout[:, j, :],
                                       start=(j == 0), stop=(j == GATE_TILES - 1))
                    if n % 2:
                        mm.then_inc(y_mm, 1)

            def feed_forward(k):
                after(pe, xq_done, 1, k, 1)
                after(pe, gate_done, GATE_TILES, k, GATE_TILES)
                for n in range(TT):
                    for t in range(KT):
                        mm = pe.transpose(pg[:, :].bitcast(BF16)[:, (n * KT + t) * P:(n * KT + t + 1) * P],
                                          xq[:, n, t * P:(t + 1) * P], identb[:, :])
                mm.then_inc(xqt_mm, 1)

            def feed_forward_products(k):
                after(pe, xqt_done, 1, k, 1)
                after(pe, y_in, 2, k, 2)
                for n in range(TT):
                    for t in range(KT):
                        for w in range(3):
                            mm = pe.matmul(fr[:, n // 2, (n % 2) * HID:(n % 2 + 1) * HID], xq_t[:, n, t, :],
                                           wsplit[:, w, t, :], start=(t == 0 and w == 0),
                                           stop=(t == KT - 1 and w == 2))
                    if n % 2:
                        mm.then_inc(ffn_mm, 1)

            def turn(k, front, tail):
                if tail:
                    project_out(k - 1)
                for c in range(NC):
                    from_state(k, c)
                    if tail and c == 2:
                        feed_forward_products(k - 1)
                    if front and c < 3:
                        project(k + 1, 2 * c)
                    if front and c == 5:
                        chunk_products(k + 1, 0)
                        chunk_products(k + 1, 1)
                    if 5 <= c < 8:
                        gates(k, c - 5)
                    solve(k, c)
                    if tail and c == 1:
                        feed_forward(k - 1)
                    if front and c < 3:
                        project(k + 1, 2 * c + 1)
                    if front and c == 4:
                        exponents(k + 1)
                    if front and c == 5:
                        chunk_products(k + 1, 2)
                    to_state(k, c)
                if front:
                    merge(k + 1)

            pe.wait_ge(ld_wproj, 32)
            pe.wait_ge(ld_x0, 16)
            for j in range(CONV_TILES):
                project(0, j)
            pe.wait_ge(ld_x, 16)
            pe.wait_ge(ld_small, 16 * N_SMALL)
            for n in range(B * T // P):
                for t in range(KT):
                    mm = pe.matmul(fr[:, 0, n * 2 * H:(n + 1) * 2 * H], xt[:, t, n * P:(n + 1) * P],
                                   wab[:, t, :], start=(t == 0), stop=(t == KT - 1))
            mm.then_inc(ab_done, 1)
            pe.wait_ge(ld_const, 16)
            pe.wait_ge(rep_in, 1)
            half = B * T // P // 2
            for n in range(2):
                mm = pe.matmul(fr[:, 1 + n, 0:half * 8 * H], cst[:, C_REP:C_REP + P],
                               rep_rhs[:, n * half:(n + 1) * half, :, :].rearrange("p n h c -> p (n h c)"),
                               start=True, stop=True)
            mm.then_inc(rep_done, 1)
            pe.wait_ge(par_in, 1)
            for n, col in enumerate((C_TRI, C_STRICT, C_ONES)):
                mm = pe.matmul(fr[:, 0, n * PAIRS * U:(n + 1) * PAIRS * U], cst[:, col:col + P],
                               par[:, 0, :], start=True, stop=True)
            mm.then_inc(cum_done, 1)
            exponents(0)
            pe.wait_ge(par_done, 3)
            for g in range(G3):
                chunk_products(0, g)
            merge(0)
            pe.wait_ge(ld_wout, 16)
            turn(0, True, False)
            with pe.Fori(1, PAIRS - 1) as k:
                turn(k, True, True)
            turn(PAIRS - 1, False, True)
            project_out(PAIRS - 1)
            feed_forward(PAIRS - 1)
            feed_forward_products(PAIRS - 1)

        @block.scalar
        def _(act):
            act.dma_start(cst[:, :], consts).then_inc(ld_const, 16)
            act.dma_start(wconv[:, :, :], w_conv.rearrange("j p m -> p j m")).then_inc(ld_small, 16)
            act.dma_start(nw[:, :], norm_w).then_inc(ld_small, 16)
            act.dma_start(alog[:, :], a_log.to_broadcast([P, H])).then_inc(ld_small, 16)
            act.dma_start(dtb[:, :], dt_bias.to_broadcast([P, H])).then_inc(ld_small, 16)

            def tile_out_of_psum(k, j):
                after(act, proj_done, j + 1, k, CONV_TILES)
                if not first(k) or j >= CONV_DEPTH:
                    after(act, silu_done, j + 1 - CONV_DEPTH if j >= CONV_DEPTH else 0, k, CONV_TILES)
                if not first(k) and j == 0:
                    after(act, y_mm, 0, k - 1, 2)
                bank = pj[:, j % 2, :].rearrange("p (b t) -> p b t", b=2)
                act.activation(raw[:, j % CONV_DEPTH, :, TAPS - 1:], bank, ACT.Copy)
                act.activation(conv[:, j % CONV_DEPTH, :, :], bank, ACT.Identity,
                               scale=wconv[:, j, TAPS - 1:TAPS]).then_inc(tile_out, 1)

            def tanh(k, j):
                after(act, conv_done[j], 1, k, 1)
                d = j % CONV_DEPTH
                act.activation(raw[:, d, :, TAPS - 1:], conv[:, d, :, :], ACT.Tanh, scale=0.5).then_inc(tanh_done, 1)

            def exp_d(k):
                after(act, dexp_mm, 1, k, 1)
                for n in range(2):
                    e = act.activation(dexp[:, n * UH:(n + 1) * UH, :].rearrange("p u t -> p (u t)"),
                                       pj[:, n, 0:UH * CH], ACT.Exp)
                e.then_inc(dexp_done, 1)

            def to_bd(dst, src, done):
                for h in range(4):
                    rows = slice(32 * h, 32 * h + 32)
                    e = act.activation(dst[rows, :, 32 * h:32 * h + 32], src[rows, :, :], ACT.Copy)
                e.then_inc(done, 1)

            def k_bd(k):
                after(act, silu_done, 3, k, CONV_TILES)
                if not first(k):
                    after(act, merge_mm, 0, k, 2)
                for h in range(4):
                    rows = slice(32 * h, 32 * h + 32)
                    e = act.activation(
                        front_bd[rows, :, 32 * h:32 * h + 32].rearrange("p (g c) t -> p g c t", g=G3),
                        kq[rows, :, 0, :].rearrange("p g (c t) -> p g c t", c=NC), ACT.Copy)
                e.then_inc(kbd_done, 1)

            def square(k):
                after(act, kq_tok_done, 1, k, 1)
                if not first(k):
                    after(act, og_done, 0, k - 1, GATE_TILES)
                act.activation(sq_tok[:, :, :, :, :].rearrange("p g k c d -> p (g k c d)"),
                               kq_tok[:, :, :, :, :].rearrange("p g k c d -> p (g k c d)"),
                               ACT.Square).then_inc(sq_done, 1)

            def merge_bd(k):
                after(act, p_mm, 2, k, 2)
                for n in range(2):
                    units = slice(n * UH, (n + 1) * UH)
                    for h in range(4):
                        rows = slice(32 * h, 32 * h + 32)
                        e = act.activation(p_bd[rows, units, 32 * h:32 * h + 32],
                                           fr[rows, n, 0:UH * CH].rearrange("p (u t) -> p u t", u=UH), ACT.Copy)
                    e.then_inc(pbd_done, 1)

            def handoff(k):
                if not first(k):
                    after(act, o_mm, 0, k, NC)
                after(act, at_done, 1, k, 1)
                to_bd(a_bd, a_t, abd_done)
                merge_bd(k)
                after(act, kg_done, 1, k, 1)
                to_bd(kg_bd, kg_tok, abd_done)
                after(act, qe_done, 1, k, 1)
                to_bd(qe_bd, qe_ch, abd_done)

            def u_out(k, c):
                after(act, u_mm, c + 1, k, NC)
                act.activation(u_sb[:, :, :].rearrange("p g v -> p (g v)"), pc[:, 0:G3 * DV],
                               ACT.Copy).then_inc(u_done, 1)

            def o_out_of_psum(k, c):
                after(act, o_mm, c + 1, k, NC)
                if c == 0 and not first(k):
                    after(act, on_done, 0, k, 1)
                act.activation(o_all[:, :, c, :], po[:, 0:G3 * DV].rearrange("p (g v) -> p g v", g=G3),
                               ACT.Copy).then_inc(o_out, 1)

            def gate_tanh_(k, j):
                after(act, gate_mm, j + 1, k, GATE_TILES)
                if not first(k) and j == 0:
                    after(act, ffn_in, 0, k, 2)
                act.activation(thg[:, :], pg[:, :], ACT.Tanh, scale=0.5).then_inc(gate_tanh, 1)

            def o_square(k, front):
                after(act, o_out, NC, k, NC)
                after(act, gate_done, GATE_TILES, k, GATE_TILES)
                if front:
                    after(act, v_tok_done, 1, k + 1, 1)
                act.activation(o_sq.rearrange("p u v -> p (u v)"),
                               o_all[:, :, :, :].rearrange("p g c v -> p (g c v)"),
                               ACT.Square).then_inc(osq_done, 1)

            def ternary_out(k):
                after(act, xqt_mm, 1, k, 1)
                act.activation(xq_t.rearrange("p n t q -> p (n t q)"),
                               pg[:, :].bitcast(BF16), ACT.Copy).then_inc(xqt_done, 1)

            def turn(k, front, tail):
                for c in range(NC):
                    if front and c < 3:
                        tile_out_of_psum(k + 1, 2 * c)
                    if front and c == 5:
                        square(k + 1)
                    if 5 <= c < 8:
                        gate_tanh_(k, c - 5)
                    u_out(k, c)
                    if tail and c == 1:
                        ternary_out(k - 1)
                    if front and 1 <= c < 4:
                        tanh(k + 1, 2 * c - 2)
                    if front and c < 3:
                        tile_out_of_psum(k + 1, 2 * c + 1)
                    o_out_of_psum(k, c)
                    if front and 1 <= c < 4:
                        tanh(k + 1, 2 * c - 1)
                    if front and c == 3:
                        k_bd(k + 1)
                    if front and c == 4:
                        exp_d(k + 1)
                        after(act, v_tok_done, 1, k + 1, 1)
                o_square(k, front)
                if front:
                    handoff(k + 1)

            act.wait_ge(ld_small, 16 * N_SMALL)
            act.wait_ge(zeroed, 3)
            for j in range(CONV_DEPTH):
                tile_out_of_psum(0, j)
            for j in range(CONV_DEPTH, CONV_TILES):
                tanh(0, j - CONV_DEPTH)
                tile_out_of_psum(0, j)
            act.activation(alog[:, :], alog[:, :], ACT.Exp).then_inc(alog_exp, 1)
            act.wait_ge(abt_abs, 1)
            act.activation(abt[:, :, 0:H], abt[:, :, 0:H], ACT.Exp).then_inc(act_own, 1)
            act.wait_ge(act_own, 1)
            act.activation(abt[:, :, 0:H], abt[:, :, 0:H], ACT.Ln, bias=1.0).then_inc(soft_done, 1)
            act.activation(abt[:, :, H:2 * H], ab[:, :, H:2 * H], ACT.Tanh, scale=0.5).then_inc(soft_done, 1)
            for j in range(CONV_TILES - CONV_DEPTH, CONV_TILES):
                tanh(0, j)
            act.wait_ge(cum_done, 1)
            for n in range(3):
                act.activation(par[:, 2 + n, :], fr[:, 0, n * PAIRS * U:(n + 1) * PAIRS * U],
                               ACT.Exp).then_inc(par_done, 1)
            exp_d(0)
            square(0)
            k_bd(0)
            handoff(0)
            turn(0, True, False)
            with act.Fori(1, PAIRS - 1) as k:
                turn(k, True, True)
            turn(PAIRS - 1, False, True)
            ternary_out(PAIRS - 1)

        @block.gpsimd
        def _(pool):
            pool.memset(raw[:, :, :, 0:TAPS - 1], 0.0).then_inc(zeroed, 1)
            pool.memset(front_bd[:, :, :], 0.0).then_inc(zeroed, 1)
            pool.memset(l21[:, :, :], 0.0).then_inc(zeroed, 1)
            for t in (qe_bd, kg_bd, a_bd, kc_bd, t_bd):
                pool.memset(t[:, :, :], 0.0).then_inc(zeroed, 1)

            upper = cst[:, C_UPPER:C_UPPER + CH].unsqueeze(1).to_broadcast([P, U, CH])
            lower = cst[:, C_LOWER:C_LOWER + CH].unsqueeze(1).to_broadcast([P, U, CH])

            def units(v):
                return v.unsqueeze(2).to_broadcast([P, U, CH])

            def g_masked(k):
                after(pool, park_done, 1, k, 1)
                if not first(k):
                    after(pool, tt_done, 0, k, 2)
                pool.tensor_tensor(gm[:, :, :], units(park[:, 0, :]), upper, ALU.mult).then_inc(gm_done, 1)

            def d_masked(k):
                after(pool, dexp_done, 1, k, 1)
                pool.tensor_tensor(dt_m[:, :, :], dexp[:, :, :], upper, ALU.mult).then_inc(dt_done, 1)

            def c_masked(k):
                after(pool, dt_done, 1, k, 1)
                after(pool, c2_done, 1, k, 1)
                pool.tensor_tensor(cm[:, :, :], units(c2[:, :]), lower, ALU.mult).then_inc(cm_done, 1)

            def k_decayed(k):
                if not first(k):
                    after(pool, abd_done, 0, k, 3)
                after(pool, kq_tok_done, 1, k, 1)
                for g in range(G3):
                    e = pool.tensor_tensor(kg_tok[:, g * NC:(g + 1) * NC, :], kq_tok[:, g, 0, :, :],
                                           park[:, 3, g * NC:(g + 1) * NC].unsqueeze(2).to_broadcast([P, NC, DK]),
                                           ALU.mult)
                e.then_inc(kg_done, 1)

            def v_scaled(k):
                wait_apart(pool, bv_done, k + 1)
                after(pool, v_tok_done, 1, k, 1)
                if not first(k):
                    after(pool, r_done, 0, k, NC - 1)
                    wait_apart(pool, u_mm, k * NC)
                pool.tensor_copy(decay[:, :, :].rearrange("p g c -> p (g c)"), park[:, 4, :])
                pool.tensor_tensor(rv[:, :, :, :].rearrange("p g c v -> p (g c) v"),
                                   v_tok[:, :, :, :, :].rearrange("p g c h v -> p (g c) (h v)"),
                                   bv[:, :].unsqueeze(2).to_broadcast([P, U, DV]), ALU.mult).then_inc(rv_done, 1)

            def decay_state(k, c):
                after(pool, s_done, c, k, NC - 1)
                after(pool, rv_done, 1, k, 1)
                pool.tensor_tensor(s_dec[:, :, :], s_sb[:, :, :],
                                   decay[:, :, c:c + 1].to_broadcast([P, G3, DV]),
                                   ALU.mult).then_inc(sdec_done, 1)

            def turn(k, front):
                for c in range(NC):
                    if 1 <= c < NC - 1:
                        decay_state(k, c)
                    if front and c == 2:
                        g_masked(k + 1)
                    if front and c == 4:
                        k_decayed(k + 1)
                        d_masked(k + 1)
                        c_masked(k + 1)
                if front:
                    v_scaled(k + 1)

            pool.wait_ge(ld_const, 16)
            g_masked(0)
            d_masked(0)
            k_decayed(0)
            c_masked(0)
            v_scaled(0)
            with pool.Fori(0, PAIRS - 1) as k:
                turn(k, True)
            turn(PAIRS - 1, False)

        @block.vector
        def _(dve):
            own = OwnResults(dve, vec_own)

            def rsqrt(y, v, t):
                own(dve.tensor_scalar(t.bitcast(I32), v.bitcast(I32), 1, None, ALU.logical_shift_right))
                own(dve.tensor_scalar(y.bitcast(I32), t.bitcast(I32), -1, RSQRT_MAGIC, ALU.mult, ALU.add))
                for _ in range(3):
                    own(dve.tensor_tensor(t, y, y, ALU.mult))
                    own(dve.scalar_tensor_tensor(out=t, in0=t, scalar=-0.5, in1=v, op0=ALU.mult, op1=ALU.mult))
                    own(dve.scalar_tensor_tensor(out=y, in0=t, scalar=1.5, in1=y, op0=ALU.add, op1=ALU.mult))

            def conv_taps(k, j):
                after(dve, tile_out, j + 1, k, CONV_TILES)
                for m in range(TAPS - 1):
                    d = j % CONV_DEPTH
                    e = dve.scalar_tensor_tensor(out=conv[:, d, :, :], in0=raw[:, d, :, m:m + T],
                                                 scalar=wconv[:, j, m:m + 1], in1=conv[:, d, :, :],
                                                 op0=ALU.mult, op1=ALU.add)
                    if m < TAPS - 2:
                        own(e)
                    else:
                        e.then_inc(conv_done[j], 1)

            def silu(k, j):
                after(dve, tanh_done, j + 1, k, CONV_TILES)
                if not first(k):
                    if j < 3:
                        after(dve, ga_mm, 0, k, 1)
                A, N = slice(0, 64), slice(64, P)
                both = slice(0, P)
                moves = {
                    0: [(both, None, kq[:, 0:2, 1, :])],
                    1: [(both, None, kq[:, 0:2, 0, :])],
                    2: [(A, 0, kq[A, 2, 1, :]), (A, 1, kq[N, 2, 1, :]),
                        (N, 0, kq[A, 2, 0, :]), (N, 1, kq[N, 2, 0, :])],
                    3: [(both, None, v_ch[:, 0:2, 0, :])],
                    4: [(both, None, v_ch[:, 0:2, 1, :])],
                    5: [(A, 0, v_ch[A, 2, 0, :]), (A, 1, v_ch[N, 2, 0, :]),
                        (N, 0, v_ch[A, 2, 1, :]), (N, 1, v_ch[N, 2, 1, :])],
                }[j]
                for rows, b, dst in moves:
                    src = slice(0, 2) if b is None else b
                    e = dve.scalar_tensor_tensor(out=dst, in0=raw[rows, j % CONV_DEPTH, src, TAPS - 1:],
                                                 scalar=1.0, in1=conv[rows, j % CONV_DEPTH, src, :], op0=ALU.add, op1=ALU.mult)
                e.then_inc(silu_done, 1)

            def kq_to_tokens(k):
                after(dve, silu_done, 3, k, CONV_TILES)
                if not first(k):
                    after(dve, kg_done, 0, k, 1)
                    after(dve, ffn_mm, 0, k - 1, 2)
                dve.transpose(kq_tok[:, :, :, :, :].rearrange("p g k c d -> p (g k c d)"),
                              kq[:, :, :, :].rearrange("p g k t -> p (g k t)")).then_inc(kq_tok_done, 1)

            def v_to_tokens(k):
                after(dve, silu_done, CONV_TILES, k, CONV_TILES)
                if not first(k):
                    after(dve, rv_done, 0, k, 1)
                for h in range(2):
                    e = dve.transpose(v_tok[:, :, :, h, :], v_ch[:, :, h, :].rearrange("p g (c t) -> p g c t", c=NC))
                e.then_inc(v_tok_done, 1)

            def pair_parameters(k):
                if not first(k):
                    after(dve, kg_done, 0, k, 1)
                    after(dve, gm_done, 0, k, 1)
                    after(dve, rv_done, 0, k, 1)
                dve.tensor_copy(park[:, :, :], par[:, :, bass.ds(k * U, U)]).then_inc(park_done, 1)

            def factors(k):
                after(dve, sq_done, 1, k, 1)
                after(dve, park_done, 1, k, 1)
                own(dve.tensor_reduce(ss[:, :, :, :].rearrange("p g k c -> p (g k c)"),
                                      sq_tok[:, :, :, :, :].rearrange("p g k c d -> p (g k c) d"), AX.X, ALU.add))
                kk3 = kk[:, :].rearrange("p (g c) -> p g c", g=G3)
                own(dve.tensor_scalar(kk3, ss[:, :, 0, :], EPS_K, None, ALU.add))
                rsqrt(r2[:, :], kk[:, :], rt[:, :])
                own(dve.tensor_tensor(rt[:, :], r2[:, :], r2[:, :], ALU.mult))
                if not first(k):
                    after(dve, cm_done, 0, k, 1)
                    after(dve, rv_done, 0, k, 1)
                dve.scalar_tensor_tensor(out=c2[:, :], in0=rt[:, :], scalar=0.5, in1=park[:, 1, :],
                                         op0=ALU.mult, op1=ALU.mult).then_inc(c2_done, 1)
                dve.scalar_tensor_tensor(out=bv[:, :], in0=r2[:, :], scalar=0.25, in1=park[:, 1, :],
                                         op0=ALU.mult, op1=ALU.mult).then_inc(bv_done, 1)
                after(dve, c2_done, 1, k, 1)
                own(dve.scalar_tensor_tensor(out=nceg[:, :], in0=c2[:, :], scalar=-1.0, in1=park[:, 2, :],
                                             op0=ALU.mult, op1=ALU.mult))

            def scaled_operands(k):
                def rows(v, g):
                    return v[:, g * NC:(g + 1) * NC].unsqueeze(2).to_broadcast([P, NC, DK])
                for g in range(G3):
                    dve.tensor_tensor(kc_tok[:, g * NC:(g + 1) * NC, :], kq_tok[:, g, 0, :, :],
                                      rows(nceg, g), ALU.mult).then_inc(kc_part, 1)
                    dve.tensor_tensor(qe_tok[:, g * NC:(g + 1) * NC, :], kq_tok[:, g, 1, :, :],
                                      rows(park[:, 2, :], g), ALU.mult).then_inc(kc_part, 1)
                after(dve, kc_part, 2 * G3, k, 2 * G3)
                own(dve.transpose(kc_ch[:, :, :].rearrange("p u t -> p (u t)"),
                                  kc_tok[:, :, :].rearrange("p u t -> p (u t)")))
                if not first(k):
                    after(dve, abd_done, 0, k, 3)
                dve.transpose(qe_ch[:, :, :].rearrange("p u t -> p (u t)"),
                              qe_tok[:, :, :].rearrange("p u t -> p (u t)")).then_inc(qe_done, 1)

            def chunk_matrices(k):
                after(dve, dt_done, 1, k, 1)
                own(dve.transpose(d_m[:, :, :].rearrange("p u t -> p (u t)"),
                                  dt_m[:, :, :].rearrange("p u t -> p (u t)")))
                after(dve, ga_mm, 1, k, 1)
                prod = fr[:, :, :].rearrange("p g (c k t) -> p (g c) k t", c=NC, k=2)
                own(dve.tensor_tensor(gd[:, :, :], prod[:, :, 0, :], d_m[:, :, :], ALU.mult))
                if not first(k):
                    after(dve, abd_done, 0, k, 3)
                dve.tensor_tensor(a_t[:, :, :], prod[:, :, 1, :], dt_m[:, :, :], ALU.mult).then_inc(at_done, 1)
                after(dve, cm_done, 1, k, 1)
                own(dve.tensor_tensor(lo[:, :, :], gd[:, :, :], cm[:, :, :], ALU.mult))
                row_a, row_b = cst[:, C_ROWA:C_ROWA + 1], cst[:, C_ROWB:C_ROWB + 1]
                own(dve.scalar_tensor_tensor(out=l16[:, :, :], in0=lo[:, :, 0:HALF], scalar=row_a,
                                             in1=lo[:, :, HALF:CH], op0=ALU.mult, op1=ALU.add))
                own(dve.tensor_scalar(l21[:, :, 0:HALF], lo[:, :, 0:HALF], row_b, None, ALU.mult))
                for h in range(4):
                    rows = slice(32 * h, 32 * h + 32)
                    e = dve.transpose(front_bd[rows, :, 32 * h:32 * h + 32], l21[rows, :, :])
                e.then_inc(l21_done, 1)
                own(dve.tensor_copy(x16[:, :, :],
                                    cst[:, C_EYE16:C_EYE16 + HALF].unsqueeze(1).to_broadcast([P, U, HALF])), wait_apart)

            def substitute(k, i):
                n = i + 1
                own(dve.stream_shuffle(b16[:, :, 0:n], x16[:, :, 0:n], [i] * HALF + [HALF + i] * HALF))
                own(dve.tensor_tensor(p16[:, :, 0:n], b16[:, :, 0:n],
                                      l16[:, :, i:i + 1].to_broadcast([P, U, n]), ALU.mult))
                own(dve.tensor_tensor(x16[:, :, 0:n], x16[:, :, 0:n], p16[:, :, 0:n], ALU.subtract), wait_apart)

            def halves(k):
                row_a, row_b = cst[:, C_ROWA:C_ROWA + 1], cst[:, C_ROWB:C_ROWB + 1]
                if not first(k):
                    after(dve, merge_mm, 0, k, 2)
                own(dve.tensor_scalar(x32[:, :, 0:HALF], x16[:, :, :], row_a, None, ALU.mult))
                own(dve.tensor_scalar(x32[:, :, HALF:CH], x16[:, :, :], row_b, None, ALU.mult))
                dve.transpose(y32[:, :, :].rearrange("p u t -> p (u t)"),
                              x32[:, :, :].rearrange("p u t -> p (u t)")).then_inc(y32_done, 1)

            def inverse(k):
                after(dve, y32_done, 1, k, 1)
                for n in range(2):
                    after(dve, merge_mm, n + 1, k, 2)
                    units = slice(n * UH, (n + 1) * UH)
                    dve.tensor_tensor(t_t[:, units, :], y32[:, units, :],
                                      fr[:, (2, 0)[n], 0:UH * CH].rearrange("p (u t) -> p u t", u=UH),
                                      ALU.subtract).then_inc(tt_done, 1)

            def to_bd(dst, src):
                for h in range(4):
                    rows = slice(32 * h, 32 * h + 32)
                    e = dve.tensor_copy(dst[rows, :, 32 * h:32 * h + 32], src[rows, :, :])
                e.then_inc(vbd_done, 1)

            def handoff(k):
                if not first(k):
                    after(dve, o_mm, 0, k, NC)
                dve.tensor_scalar(eps_o[:, :, :], ss[:, :, 1, :], EPS_O, EPS_O * EPS_K, ALU.mult, ALU.add)
                to_bd(kc_bd, kc_ch)
                inverse(k)
                after(dve, tt_done, 2, k, 2)
                to_bd(t_bd, t_t)

            def residual(k, c):
                if c > 0:
                    after(dve, ks_mm, c, k, NC - 1)
                    after(dve, rv_done, 1, k, 1)
                    dve.tensor_tensor(r_sb[:, :, :], pc[:, 0:G3 * DV].rearrange("p (g v) -> p g v", g=G3),
                                      rv[:, :, c, :], ALU.add).then_inc(r_done, 1)

            def next_state(k, c):
                if c == NC - 1:
                    return
                after(dve, s_mm, c + 1, k, NC - 1)
                step = pc[:, 0:G3 * DV].rearrange("p (g v) -> p g v", g=G3)
                if c == 0:
                    dve.tensor_copy(s_sb[:, :, :], step).then_inc(s_done, 1)
                else:
                    after(dve, sdec_done, c, k, NC - 2)
                    dve.tensor_tensor(s_sb[:, :, :], s_dec[:, :, :], step, ALU.add).then_inc(s_done, 1)

            def gate_product(k, j):
                after(dve, gate_tanh, j + 1, k, GATE_TILES)
                dve.scalar_tensor_tensor(out=gate[:, j, :], in0=thg[:, :], scalar=1.0, in1=pg[:, :],
                                         op0=ALU.add, op1=ALU.mult).then_inc(gate_done, 1)

            def head_norm(k):
                after(dve, osq_done, 1, k, 1)
                own(dve.tensor_reduce(m_o[:, :], o_sq, AX.X, ALU.add))
                own(dve.scalar_tensor_tensor(out=v_o[:, :], in0=m_o[:, :], scalar=1.0 / DV,
                                             in1=eps_o[:, :, :].rearrange("p g c -> p (g c)"),
                                             op0=ALU.mult, op1=ALU.add))
                rsqrt(r_o[:, :], v_o[:, :], t_o[:, :])
                units = o_all[:, :, :, :].rearrange("p g c v -> p (g c) v")
                dve.tensor_tensor(units, units, r_o[:, :].unsqueeze(2).to_broadcast([P, U, DV]),
                                  ALU.mult).then_inc(on_scaled, 1)
                after(dve, on_scaled, 1, k, 1)
                if not first(k):
                    after(dve, y_mm, 0, k, 2)
                for h in range(2):
                    own(dve.transpose(
                        o_ch[:, h, :].rearrange("p (c t) -> p c t", t=CH),
                        o_all[:, 0:2, :, h * 32:(h + 1) * 32].rearrange("p g c v -> p (g c) v")))
                for h in range(2):
                    for b in range(2):
                        e = dve.transpose(
                            o_ch[64 * h:64 * h + 64, 2, b * T:(b + 1) * T].rearrange("p (c t) -> p c t", t=CH),
                            o_all[64 * b:64 * b + 64, 2, :, h * 32:(h + 1) * 32])
                e.then_inc(on_done, 1)

            def gated(k):
                after(dve, on_done, 1, k, 1)
                after(dve, gate_done, GATE_TILES, k, GATE_TILES)
                for j in range(GATE_TILES):
                    dve.scalar_tensor_tensor(out=o_ch[:, j, :], in0=o_ch[:, j, :], scalar=nwh[:, j:j + 1],
                                             in1=gate[:, j, :], op0=ALU.mult, op1=ALU.mult).then_inc(og_done, 1)

            def layer_norm_factors(src):
                for n in range(TT):
                    own(dve.bn_stats(stats[:, n, :], src[:, n, :]), wait_apart)
                for n in range(TT):
                    own(dve.bn_aggr(mv[:, n, :], stats[:, n, :]), wait_apart)
                own(dve.tensor_scalar(v_n[:, :], mv[:, :, 1], EPS_LN, None, ALU.add))
                rsqrt(r_n[:, :], v_n[:, :], t_n[:, :])

            def normalize(src, dst, done):
                for n in range(TT):
                    e = dve.tensor_scalar(dst[:, n, :], src[:, n, :], mv[:, n, 0:1], r_n[:, n:n + 1],
                                          ALU.subtract, ALU.mult)
                    if done is None:
                        own(e)
                    elif n % 2:
                        e.then_inc(done, 1)

            def first_norm(k):
                dve.wait_ge(ld_res, (k + 1) * 16)
                for n in range(2):
                    after(dve, y_mm, n + 1, k, 2)
                    dve.tensor_tensor(hid[:, 2 * n:2 * n + 2, :].rearrange("p n c -> p (n c)"), fr[:, n, :],
                                      res[:, 2 * n:2 * n + 2, :].rearrange("p n c -> p (n c)"),
                                      ALU.add).then_inc(y_in, 1)
                after(dve, y_in, 2, k, 2)
                layer_norm_factors(hid)

            def ternary(k):
                normalize(hid, x1, None)
                if not last(k):
                    after(dve, kg_done, 1, k + 1, 1)
                own(dve.tensor_scalar(pos[:, :, :], x1[:, :, :], TH_X, None, ALU.is_gt))
                dve.scalar_tensor_tensor(out=xq[:, :, :], in0=x1[:, :, :], scalar=-TH_X, in1=pos[:, :, :],
                                         op0=ALU.is_lt, op1=ALU.subtract).then_inc(xq_done, 1)

            def second_norm(k):
                for n in range(2):
                    after(dve, ffn_mm, n + 1, k, 2)
                    dve.tensor_tensor(hid[:, 2 * n:2 * n + 2, :].rearrange("p n c -> p (n c)"), fr[:, n, :],
                                      x1[:, 2 * n:2 * n + 2, :].rearrange("p n c -> p (n c)"),
                                      ALU.add).then_inc(ffn_in, 1)
                after(dve, ffn_in, 2, k, 2)
                layer_norm_factors(hid)
                normalize(hid, y_out, out_done)

            def turn(k, front, tail):
                for c in range(NC):
                    residual(k, c)
                    if tail and c == 0:
                        first_norm(k - 1)
                    if tail and c == 2:
                        second_norm(k - 1)
                    if front and c == 1:
                        conv_taps(k + 1, 1)
                        silu(k + 1, 0)
                    if front and c == 3:
                        silu(k + 1, 2)
                        kq_to_tokens(k + 1)
                        conv_taps(k + 1, 4)
                    if front and c == 4:
                        silu(k + 1, 4)
                        silu(k + 1, 5)
                        v_to_tokens(k + 1)
                    if front and c == 5:
                        scaled_operands(k + 1)
                    if front and c == 6:
                        for i in range(0, 4):
                            substitute(k + 1, i)
                    if front and c == 7:
                        for i in range(8, 12):
                            substitute(k + 1, i)
                    next_state(k, c)
                    if tail and c == 0:
                        ternary(k - 1)
                    if front and c == 0:
                        conv_taps(k + 1, 0)
                    if front and c == 1:
                        pair_parameters(k + 1)
                        conv_taps(k + 1, 2)
                        silu(k + 1, 1)
                    if front and c == 2:
                        conv_taps(k + 1, 3)
                    if front and c == 3:
                        conv_taps(k + 1, 5)
                        silu(k + 1, 3)
                    if front and c == 4:
                        factors(k + 1)
                    if front and c == 5:
                        chunk_matrices(k + 1)
                    if c >= 5:
                        gate_product(k, c - 5)
                    if front and c == 6:
                        for i in range(4, 8):
                            substitute(k + 1, i)
                    if front and c == 7:
                        for i in range(12, HALF - 1):
                            substitute(k + 1, i)
                if front:
                    halves(k + 1)
                head_norm(k)
                gated(k)
                if front:
                    handoff(k + 1)

            dve.wait_ge(ld_small, 16 * N_SMALL)
            for j in (0, 1):
                conv_taps(0, j)
            silu(0, 0)
            silu(0, 1)
            for j in range(2, CONV_TILES):
                conv_taps(0, j)
            own(dve.tensor_scalar(nwh[:, :], nw[:, :], 0.5, None, ALU.mult))
            dve.wait_ge(ab_done, 1)
            own(dve.tensor_copy(ab[:, :, :].rearrange("p n h -> p (n h)"), fr[:, 0, 0:B * T // P * 2 * H]))
            z = ab[:, :, 0:H]
            own(dve.tensor_tensor(z, z, dtb[:, :].unsqueeze(1).to_broadcast([P, B * T // P, H]), ALU.add))
            own(dve.tensor_scalar(abt[:, :, H:], z, -1.0, None, ALU.mult))
            dve.tensor_tensor(abt[:, :, 0:H], z, abt[:, :, H:], ALU.min).then_inc(abt_abs, 1)
            dve.wait_ge(soft_done, 2)
            dve.wait_ge(alog_exp, 1)
            own(dve.scalar_tensor_tensor(out=z, in0=z, scalar=0.0, in1=abt[:, :, 0:H], op0=ALU.max, op1=ALU.add))
            own(dve.scalar_tensor_tensor(out=z, in0=z, scalar=-1.0,
                                         in1=alog[:, :].unsqueeze(1).to_broadcast([P, B * T // P, H]),
                                         op0=ALU.mult, op1=ALU.mult))
            own(dve.tensor_scalar(ab[:, :, H:], abt[:, :, H:], 1.0, None, ALU.add))
            dve.wait_ge(ld_const, 16)
            for c in range(4):
                e = dve.tensor_scalar(rep_rhs[:, :, :, c], ab[:, :, :], cst[:, c:c + 1], None, ALU.mult)
                if c < 3:
                    own(e)
            e.then_inc(rep_in, 1)
            dve.wait_ge(rep_done, 1)
            for kind in range(2):
                for q in range(4):
                    rows = slice(32 * q, 32 * q + 32)
                    for n in range(2):
                        src = fr[rows, 1 + n, 0:n_tiles // 2 * 8 * H].rearrange(
                            "p (k b n h c) -> p k b n h c", k=2, b=2, n=2, c=4)
                        dst = par[rows, kind, :].rearrange("p (k g n c) -> p k g n c", k=PAIRS, g=G3, n=2)
                        for kp in range(2):
                            own(dve.tensor_copy(
                                dst[:, 2 * n + kp, 0:2, :, :].rearrange("p g n c -> p (g n) c"),
                                src[:, kp, :, :, kind * H + q, :].rearrange("p b n c -> p (b n) c")))
                        e = dve.tensor_copy(dst[:, 2 * n:2 * n + 2, 2, :, :],
                                            src[:, :, q // 2, :, kind * H + 4 + q % 2, :])
            e.then_inc(par_in, 1)
            silu(0, 2)
            kq_to_tokens(0)
            silu(0, 3)
            silu(0, 4)
            silu(0, 5)
            v_to_tokens(0)
            dve.wait_ge(par_done, 3)
            dve.wait_ge(par_in, 1)
            pair_parameters(0)
            factors(0)
            scaled_operands(0)
            dve.wait_ge(zeroed, 8)
            chunk_matrices(0)
            for i in range(HALF - 1):
                substitute(0, i)
            halves(0)
            dve.wait_ge(ld_ffn, 32)
            own(dve.tensor_scalar(wtmp[:, :, :], wf[:, :, :], TH_W, SC_W, ALU.is_gt, ALU.mult))
            own(dve.tensor_scalar(wf[:, :, :], wf[:, :, :], -TH_W, -SC_W, ALU.is_lt, ALU.mult))
            own(dve.tensor_tensor(wf[:, :, :], wf[:, :, :], wtmp[:, :, :], ALU.add))
            own(dve.tensor_tensor(wf[:, :, :], wf[:, :, :], wr[:, :, :], ALU.add))
            own(dve.tensor_scalar(wf[:, :, :], wf[:, :, :], -0.5, None, ALU.mult))
            for s in range(3):
                own(dve.tensor_copy(wsplit[:, s, :, :], wf[:, :, :]))
                if s < 2:
                    own(dve.tensor_tensor(wf[:, :, :], wf[:, :, :], wsplit[:, s, :, :], ALU.subtract))
            dve.tensor_copy(identb[:, :], cst[:, C_IDENT:C_IDENT + P]).then_inc(ffn_ready, 1)
            handoff(0)
            turn(0, True, False)
            assert own.n == VEC_OWN_FIRST, own.n
            with dve.Fori(0, PAIRS - 2) as n:
                own.start(VEC_OWN_FIRST + n * VEC_OWN_TURN)
                turn(n + 1, True, True)
                assert own.n == VEC_OWN_TURN, own.n
            own.start(VEC_OWN_FIRST + (PAIRS - 2) * VEC_OWN_TURN)
            turn(PAIRS - 1, False, True)
            first_norm(PAIRS - 1)
            ternary(PAIRS - 1)
            second_norm(PAIRS - 1)


def constants():
    import numpy as np
    p = np.arange(P)[:, None]
    q = np.arange(P)[None, :]
    same = p // CH == q // CH
    c = np.zeros((P, C_END), np.float32)
    c[:, C_QUARTER:C_QUARTER + 4] = p // CH == np.arange(4)
    c[:, C_REP:C_REP + P] = p % CH == q % CH
    c[:, C_TRI:C_TRI + P] = same & (p <= q)
    c[:, C_STRICT:C_STRICT + P] = same & (p > q)
    c[:, C_ONES:C_ONES + P] = same
    c[:, C_IDENT:C_IDENT + P] = p == q
    c[:, C_UPPER:C_UPPER + CH] = p % CH <= np.arange(CH)
    c[:, C_LOWER:C_LOWER + CH] = p % CH > np.arange(CH)
    c[:, C_EYE16:C_EYE16 + HALF] = p % HALF == np.arange(HALF)
    c[:, C_ROWA:C_ROWA + 1] = p % CH < HALF
    c[:, C_ROWB:C_ROWB + 1] = p % CH >= HALF
    return c


def kernel(L0_attn_hidden_states, L0_attn_Wq, L0_attn_Wk, L0_attn_Wv, L0_attn_Wb, L0_attn_Wa, L0_attn_A_log,
           L0_attn_dt_bias, L0_attn_conv_wq, L0_attn_conv_wk, L0_attn_conv_wv, L0_attn_Wg, L0_attn_norm_w,
           L0_attn_Wo, L0_ffn_weight, L0_ffn_rram_variation):
    import numpy as np
    import concourse.bacc as bacc
    from concourse.bass_utils import run_bass_kernel_spmd

    def whole(a):
        return np.ascontiguousarray(np.asarray(a))

    x = np.asarray(L0_attn_hidden_states)
    lo, hi = np.arange(DV // 2), np.arange(DV // 2, DV)
    v_rows = np.concatenate([h * DV + part for heads, part in
                             (((0, 1, 2, 3), lo), ((0, 1, 2, 3), hi), ((4, 5), lo), ((4, 5), hi)) for h in heads])
    a_rows, b_rows = np.arange(4 * DK), np.arange(4 * DK, H * DK)

    def tiles(q, k, v):
        q, k, v = np.asarray(q), np.asarray(k), np.asarray(v)
        return np.concatenate([q[a_rows], k[a_rows], q[b_rows], k[b_rows], v[v_rows]])

    w_proj = np.concatenate([tiles(L0_attn_Wq, L0_attn_Wk, L0_attn_Wv), np.asarray(L0_attn_Wg)[v_rows]])
    arrays = {
        "x": x,
        "x_t": x.reshape(B * T, HID).T.reshape(KT, P, B * T),
        "w_proj": w_proj.T.reshape(KT, P, -1),
        "w_conv": tiles(L0_attn_conv_wq, L0_attn_conv_wk, L0_attn_conv_wv).reshape(CONV_TILES, P, TAPS),
        "w_ab": np.concatenate([np.asarray(L0_attn_Wa), np.asarray(L0_attn_Wb)]).T.reshape(KT, P, 2 * H),
        "a_log": np.asarray(L0_attn_A_log).reshape(1, H),
        "dt_bias": np.asarray(L0_attn_dt_bias).reshape(1, H),
        "norm_w": np.asarray(L0_attn_norm_w)[v_rows % DV].reshape(GATE_TILES, P).T,
        "w_out": np.asarray(L0_attn_Wo).T[v_rows].reshape(GATE_TILES, P, HID),
        "w_ffn": np.asarray(L0_ffn_weight).T.reshape(KT, P, HID),
        "w_rram": np.asarray(L0_ffn_rram_variation).T.reshape(KT, P, HID),
        "consts": constants(),
    }
    arrays = {name: whole(a) for name, a in arrays.items()}
    nc = bacc.Bacc("TRN2", target_bir_lowering=False, num_devices=1)
    aps = {name: nc.dram_tensor(name, a.shape, mybir.dt.from_np(a.dtype), kind="ExternalInput").ap()
           for name, a in arrays.items()}
    out = nc.dram_tensor("out", (B, T, HID), F32, kind="ExternalOutput").ap()
    program(nc, **aps, out=out)
    return run_bass_kernel_spmd(nc, [arrays], core_ids=[0]).results[0]["out"]
```

```python
from contextlib import ExitStack

import concourse.bass as bass
from concourse import mybir

ALU = mybir.AluOpType
ACT = mybir.ActivationFunctionType
AX = mybir.AxisListType
F32 = mybir.dt.float32
I32 = mybir.dt.int32
BF16 = mybir.dt.bfloat16

P = 128
B, T, HID = 8, 256, 256
H, DK, DV, TAPS = 6, 32, 64, 4
CH = 32
NC = T // CH
PAIRS = B // 2
G3 = 3
U = G3 * NC
TOK = 2 * T
TT = TOK // P
KT = HID // P
CONV_TILES, GATE_TILES = 6, 3
VTILE_LO, VTILE_HI, VTILE_B = 3, 4, 5
HALF = CH // 2
CONV_DEPTH = 4
SLOT = [(j + CONV_DEPTH - 1) % CONV_DEPTH for j in range(CONV_TILES)]
UH = U // 2

EPS_K = 4e-6
EPS_O = 1e-5 * DK
EPS_LN = 1e-5
TH_X, TH_W, SC_W = 0.33, 0.2, 0.6
RSQRT_MAGIC = 0x5F3759DF

C_QUARTER, C_REP, C_TRI, C_STRICT, C_ONES, C_IDENT = 0, 4, 132, 260, 388, 516
C_UPPER, C_LOWER, C_EYE16, C_ROWA, C_ROWB, C_END = 644, 676, 708, 724, 725, 726

VEC_OWN_FIRST, VEC_OWN_TURN = 282, 174


class OwnResults:

    def __init__(self, eng, sem):
        self.eng, self.sem, self.base, self.n = eng, sem, 0, 0

    def start(self, base):
        self.base, self.n = base, 0

    def counted(self, instruction):
        self.n += 1
        instruction.then_inc(self.sem, 1)
        return self.n

    def until(self, n, wait=None):
        if wait:
            wait(self.eng, self.sem, self.base + n)
        else:
            self.eng.wait_ge(self.sem, self.base + n)

    def __call__(self, instruction, wait=None):
        self.until(self.counted(instruction), wait)


def program(nc, x, x_t, w_proj, w_conv, w_ab, a_log, dt_bias, norm_w, w_out, w_ffn, w_rram, consts, out):
    ctx = ExitStack()
    with ctx:
        def sb(name, shape, dt=F32):
            return ctx.enter_context(nc.sbuf_tensor(name, shape, dt))

        def pb(name, shape, dt=F32):
            return ctx.enter_context(nc.psum_tensor(name, shape, dt))

        def sem(name):
            return ctx.enter_context(nc.semaphore(name))

        def view(flat, start, *sizes, dt=F32):
            n = 1
            for size in sizes:
                n *= size
            words = n if dt == F32 else n // 2
            v = flat[:, start:start + words]
            if dt != F32:
                v = v.bitcast(dt)
            names = "abcde"[:len(sizes)]
            return v.rearrange(f"p ({' '.join(names)}) -> p {' '.join(names)}",
                               **dict(zip(names[1:], sizes[1:])))

        cst = sb("cst", [P, C_END])
        xt = sb("xt", [P, KT, B * T])
        wproj = sb("wproj", [P, KT, (CONV_TILES + GATE_TILES) * P])
        wconv = sb("wconv", [P, CONV_TILES, TAPS])
        wab = sb("wab", [P, KT, 2 * H])
        alog = sb("alog", [P, H])
        dtb = sb("dtb", [P, H])
        nw = sb("nw", [P, GATE_TILES])
        nwh = sb("nwh", [P, GATE_TILES])
        wout = sb("wout", [P, GATE_TILES, HID])
        wsplit = sb("wsplit", [P, 3, KT, HID], BF16)
        identb = sb("identb", [P, P], BF16)
        par = sb("par", [P, 5, PAIRS * U])
        park = sb("park", [P, 5, U])
        conv_buf = sb("conv_buf", [P, CONV_DEPTH * TOK])
        tok_buf = sb("tok_buf", [P, G3 * 2 * T])
        gate_buf = sb("gate_buf", [P, GATE_TILES * TOK])
        chunk_buf = sb("chunk_buf", [P, U * CH])
        sub_buf = sb("sub_buf", [P, U * CH])
        hid_buf = sb("hid_buf", [P, TT * HID])
        x1_buf = sb("x1_buf", [P, G3 * 2 * T])
        n_tiles = B * T // P
        rep_rhs = view(gate_buf, 0, n_tiles, 2 * H, 4)
        ab = view(x1_buf, 512, n_tiles, 2 * H)
        abt = view(x1_buf, 512 + n_tiles * 2 * H, n_tiles, 2 * H)
        wf = view(hid_buf, 0, KT, HID)
        wr = view(hid_buf, KT * HID, KT, HID)
        wtmp = view(x1_buf, 0, KT, HID)
        raw = sb("raw", [P, CONV_DEPTH, 2, T + TAPS - 1])
        conv = view(conv_buf, 0, CONV_DEPTH, 2, T)
        kq = sb("kq", [P, G3, 2, T])
        kq_tok = view(tok_buf, 0, G3, 2, NC, DK)
        sq_tok = view(gate_buf, 0, G3, 2, NC, DK)
        ss = sb("ss", [P, G3, 2, NC])
        v_ch = view(x1_buf, 0, G3, 2, T)
        v_tok = sb("v_tok", [P, G3, NC, 2, DV // 2])
        kk = sb("kk", [P, U])
        r2 = sb("r2", [P, U])
        rt = sb("rt", [P, U])
        c2 = sb("c2", [P, U])
        bv = sb("bv", [P, U])
        nceg = sb("nceg", [P, U])
        kc_tok = view(chunk_buf, 0, U, DK)
        qe_tok = view(sub_buf, 0, U, DK)
        kg_tok = sb("kg_tok", [P, U, DK])
        kc_ch = sb("kc_ch", [P, U, CH])
        qe_ch = sb("qe_ch", [P, U, CH])
        gm = sb("gm", [P, U, CH])
        dexp = gm
        dt_m = sb("dt_m", [P, U, CH])
        d_m = view(chunk_buf, 0, U, CH)
        cm = gm
        gd = d_m
        lo = d_m
        a_t = sb("a_t", [P, U, CH])
        l16 = sb("l16", [P, U, HALF])
        l21 = sb("l21", [P, U, CH])
        x16 = sb("x16", [P, U, HALF])
        b16 = view(sub_buf, 0, U, HALF)
        p16 = view(sub_buf, U * HALF, U, HALF)
        x32 = dt_m
        y32 = gm
        t_t = view(chunk_buf, 0, U, CH)
        front_bd = sb("front_bd", [P, U, P])
        p_bd = front_bd
        kc_bd = sb("kc_bd", [P, U, P])
        qe_bd = sb("qe_bd", [P, U, P])
        kg_bd = sb("kg_bd", [P, U, P])
        t_bd = sb("t_bd", [P, U, P])
        a_bd = sb("a_bd", [P, U, P])
        rv = sb("rv", [P, G3, NC, DV])
        decay = sb("decay", [P, G3, NC])
        eps_o = sb("eps_o", [P, G3, NC])
        r_sb = sb("r_sb", [P, G3, DV])
        u_sb = sb("u_sb", [P, G3, DV])
        s_sb = sb("s_sb", [P, G3, DV])
        s_dec = sb("s_dec", [P, G3, DV])
        o_all = sb("o_all", [P, G3, NC, DV])
        o_sq = view(x1_buf, 0, U, DV)
        thg = view(x1_buf, 0, TOK)
        gate = view(gate_buf, 0, GATE_TILES, TOK)
        m_o = sb("m_o", [P, U])
        v_all = sb("v_all", [P, U + TT])
        r_all = sb("r_all", [P, U + TT])
        t_all = sb("t_all", [P, U + TT])
        (v_o, v_n), (r_o, r_n), (t_o, t_n) = ((t[:, 0:U], t[:, U:]) for t in (v_all, r_all, t_all))
        o_ch = view(conv_buf, 0, GATE_TILES, TOK)
        hid = view(hid_buf, 0, TT, HID)
        x1 = view(x1_buf, 0, TT, HID)
        res = x1
        pos = view(tok_buf, 0, TT, HID, dt=BF16)
        xq = view(tok_buf, TT * HID // 2, TT, HID, dt=BF16)
        xq_t = view(tok_buf, TT * HID, TT, KT, P, dt=BF16)
        stats = sb("stats", [P, TT, 6])
        mv = sb("mv", [P, TT, 2])
        y_out = hid

        pj = pb("pj", [P, 2, 512])
        fr = pb("fr", [P, 3, 512])
        pc = pb("pc", [P, 512])
        po = pb("po", [P, 512])
        pg = pb("pg", [P, 512])
        y_bank = (pg, pj[:, 1, :])

        ld_const, ld_x0, ld_x, ld_wproj, ld_small, ld_wout, ld_ffn, ld_res, st_out = (
            sem(n) for n in ("ld_const", "ld_x0", "ld_x", "ld_wproj", "ld_small", "ld_wout", "ld_ffn",
                             "ld_res", "st_out"))
        zeroed, vec_own, act_own, ffn_ready = (sem(n) for n in ("zeroed", "vec_own", "act_own", "ffn_ready"))
        proj_done, tile_out, tanh_done, silu_done, kc_part, on_scaled = (
            sem(n) for n in ("proj_done", "tile_out", "tanh_done", "silu_done", "kc_part", "on_scaled"))
        conv_done = [sem(f"conv_done{j}") for j in range(CONV_TILES)]
        ab_done, ab_in, abt_pos, abt_abs, soft_done, alog_exp, rep_in, rep_done, par_in, cum_done, par_done = (
            sem(n) for n in ("ab_done", "ab_in", "abt_pos", "abt_abs", "soft_done", "alog_exp", "rep_in",
                             "rep_done", "par_in", "cum_done", "par_done"))
        kq_tok_done, sq_done, park_done, gm_done, dexp_mm, dexp_done, dt_done, c2_done, cm_done, bv_done = (
            sem(n) for n in ("kq_tok_done", "sq_done", "park_done", "gm_done", "dexp_mm", "dexp_done",
                             "dt_done", "c2_done", "cm_done", "bv_done"))
        v_tok_done, qe_done, kg_done, kbd_done, ga_mm, at_done, l21_done, y32_done = (
            sem(n) for n in ("v_tok_done", "qe_done", "kg_done", "kbd_done", "ga_mm", "at_done",
                             "l21_done", "y32_done"))
        x32_done, p_mm, pbd_done, merge_mm, tt_done = (
            sem(n) for n in ("x32_done", "p_mm", "pbd_done", "merge_mm", "tt_done"))
        rv_done, vbd_done, abd_done = (sem(n) for n in ("rv_done", "vbd_done", "abd_done"))
        ks_mm, r_done, u_mm, u_done, s_mm, s_done, sdec_done, o_mm, o_out = (
            sem(n) for n in ("ks_mm", "r_done", "u_mm", "u_done", "s_mm", "s_done", "sdec_done", "o_mm",
                             "o_out"))
        gate_mm, gate_tanh, gate_done = (sem(n) for n in ("gate_mm", "gate_tanh", "gate_done"))
        osq_done, on_done, og_done, y_mm, y_in, xq_done, xqt_mm, xqt_done, ffn_mm, ffn_in, out_done = (
            sem(n) for n in ("osq_done", "on_done", "og_done", "y_mm", "y_in", "xq_done", "xqt_mm",
                             "xqt_done", "ffn_mm", "ffn_in", "out_done"))

        N_SMALL = 5
        block = ctx.enter_context(nc.Block())

        def per_unit(t):
            return t.unsqueeze(2)

        def after(eng, semaphore, count, k, per_pair):
            eng.wait_ge(semaphore, k * per_pair + count)

        def wait_apart(eng, semaphore, value):
            if not isinstance(value, int):
                eng.compute_val(value)
                eng.wait_ge(ld_const, 16)
            eng.wait_ge(semaphore, value)

        def first(k):
            return isinstance(k, int) and k == 0

        def last(k):
            return isinstance(k, int) and k == PAIRS - 1

        @block.sync
        def _(sp):
            sp.dma_start(wproj[:, :, 0:P], w_proj.rearrange("k p n -> p k n")[:, :, 0:P]).then_inc(ld_wproj, 16)
            sp.dma_start(xt[:, :, 0:TOK], x_t.rearrange("k p n -> p k n")[:, :, 0:TOK]).then_inc(ld_x0, 16)
            sp.dma_start(wproj[:, :, P:], w_proj.rearrange("k p n -> p k n")[:, :, P:]).then_inc(ld_wproj, 16)
            sp.dma_start(wab[:, :, :], w_ab.rearrange("k p n -> p k n")).then_inc(ld_small, 16)
            sp.dma_start(xt[:, :, TOK:], x_t.rearrange("k p n -> p k n")[:, :, TOK:]).then_inc(ld_x, 16)
            sp.dma_start(wf[:, :, :], w_ffn.rearrange("k p n -> p k n")).then_inc(ld_ffn, 16)
            sp.dma_start(wr[:, :, :], w_rram.rearrange("k p n -> p k n")).then_inc(ld_ffn, 16)
            sp.dma_start(wout[:, :, :], w_out.rearrange("k p n -> p k n")).then_inc(ld_wout, 16)
            x_pairs = x.rearrange("(q b) t c -> q (b t) c", b=2)
            out_pairs = out.rearrange("(q b) t c -> q (b t) c", b=2)

            def load_residual(k):
                after(sp, on_scaled, 1, k, 1)
                sp.dma_start(res[:, :, :], x_pairs[bass.ds(k, 1), :, :].rearrange(
                    "q (n p) c -> p (q n) c", p=P)).then_inc(ld_res, 16)
            def store(k):
                for n in range(2):
                    after(sp, out_done, n + 1, k, 2)
                    sp.dma_start(out_pairs[bass.ds(k, 1), n * T:(n + 1) * T, :].rearrange(
                        "q (n p) c -> p (q n) c", p=P), y_out[:, 2 * n:2 * n + 2, :]).then_inc(st_out, 16)

            load_residual(0)
            with sp.Fori(1, PAIRS) as k:
                load_residual(k)
                store(k - 1)
            store(PAIRS - 1)
            sp.wait_ge(st_out, 16 * 2 * PAIRS)

        @block.tensor
        def _(pe):
            def project(k, j):
                if not first(k):
                    if j < 2:
                        after(pe, dexp_done, 0, k, 1)
                    if j == 1:
                        after(pe, y_in, 0, k - 1, 2)
                if not (first(k) and j < 2):
                    after(pe, tile_out, j - 1, k, CONV_TILES)
                for t in range(KT):
                    mm = pe.matmul(pj[:, j % 2, :], wproj[:, t, j * P:(j + 1) * P],
                                   xt[:, t, bass.ds(k * TOK, TOK)], start=(t == 0), stop=(t == KT - 1))
                mm.then_inc(proj_done, 1)

            def gates(k, j):
                if not first(k) or j > 0:
                    after(pe, gate_done, j, k, GATE_TILES)
                if not first(k) and j == 0:
                    after(pe, xqt_done, 0, k, 1)
                for t in range(KT):
                    w = CONV_TILES + j
                    mm = pe.matmul(pg[:, :], wproj[:, t, w * P:(w + 1) * P],
                                   xt[:, t, bass.ds(k * TOK, TOK)], start=(t == 0), stop=(t == KT - 1))
                mm.then_inc(gate_mm, 1)

            def exponents(k):
                after(pe, gm_done, 1, k, 1)
                after(pe, tile_out, CONV_TILES, k, CONV_TILES)
                for n in range(2):
                    mm = pe.matmul(pj[:, n, 0:UH * CH], cst[:, C_STRICT:C_STRICT + P],
                                   gm[:, n * UH:(n + 1) * UH, :].rearrange("p u t -> p (u t)"),
                                   start=True, stop=True)
                mm.then_inc(dexp_mm, 1)

            def chunk_products(k, g):
                if g == 0:
                    after(pe, kbd_done, 1, k, 1)
                    after(pe, silu_done, 3, k, CONV_TILES)
                    if not first(k):
                        after(pe, tt_done, 0, k, 2)
                        after(pe, ffn_in, 0, k - 1, 2)
                for c in range(NC):
                    mm = pe.matmul(fr[:, g, c * 2 * CH:(c + 1) * 2 * CH], front_bd[:, g * NC + c, :],
                                   kq[:, g, :, c * CH:(c + 1) * CH], start=True, stop=True)
                if g == G3 - 1:
                    mm.then_inc(ga_mm, 1)

            def merge(k):
                after(pe, l21_done, 1, k, 1)
                after(pe, x32_done, 1, k, 1)
                after(pe, at_done, 1, k, 1)
                for n in range(2):
                    for u in range(UH):
                        mm = pe.matmul(fr[:, n, u * CH:(u + 1) * CH], front_bd[:, n * UH + u, :],
                                       x32[:, n * UH + u, :], start=True, stop=True)
                    mm.then_inc(p_mm, 1)

            def merge_second(k, n):
                if n == 0:
                    after(pe, y32_done, 1, k, 1)
                after(pe, pbd_done, n + 1, k, 2)
                for u in range(UH):
                    mm = pe.matmul(fr[:, (2, 0)[n], u * CH:(u + 1) * CH], p_bd[:, n * UH + u, :],
                                   y32[:, n * UH + u, :], start=True, stop=True)
                mm.then_inc(merge_mm, 1)

            def from_state(k, c):
                if c == 0:
                    return
                after(pe, s_done, c, k, NC - 1)
                for g in range(G3):
                    mm = pe.matmul(pc[:, g * DV:(g + 1) * DV], kc_bd[:, g * NC + c, :], s_sb[:, g, :],
                                   start=True, stop=True)
                mm.then_inc(ks_mm, 1)
                after(pe, o_out, c, k, NC)
                for g in range(G3):
                    pe.matmul(po[:, g * DV:(g + 1) * DV], qe_bd[:, g * NC + c, :], s_sb[:, g, :],
                              start=(g == 0), stop=False, skip_group_check=True)

            def solve(k, c):
                if c == 0:
                    after(pe, vbd_done, 2, k, 2)
                    after(pe, rv_done, 1, k, 1)
                else:
                    after(pe, r_done, c, k, NC - 1)
                for g in range(G3):
                    mm = pe.matmul(pc[:, g * DV:(g + 1) * DV], t_bd[:, g * NC + c, :],
                                   rv[:, g, 0, :] if c == 0 else r_sb[:, g, :], start=True, stop=True)
                mm.then_inc(u_mm, 1)

            def to_state(k, c):
                after(pe, u_done, c + 1, k, NC)
                if c == 0:
                    after(pe, abd_done, 3, k, 3)
                if c < NC - 1:
                    for g in range(G3):
                        mm = pe.matmul(pc[:, g * DV:(g + 1) * DV], kg_bd[:, g * NC + c, :], u_sb[:, g, :],
                                       start=True, stop=True)
                    mm.then_inc(s_mm, 1)
                if c == 0 and not first(k):
                    after(pe, o_out, 0, k, NC)
                for g in range(G3):
                    mm = pe.matmul(po[:, g * DV:(g + 1) * DV], a_bd[:, g * NC + c, :], u_sb[:, g, :],
                                   start=(c == 0 and g == 0), stop=True, skip_group_check=True)
                mm.then_inc(o_mm, 1)

            def project_out(k, part):
                if part == 0:
                    after(pe, og_done, GATE_TILES, k, GATE_TILES)
                for n in range(2 * part, 2 * part + 2):
                    for j in range(GATE_TILES):
                        mm = pe.matmul(y_bank[part][:, (n % 2) * HID:(n % 2 + 1) * HID],
                                       o_ch[:, j, n * P:(n + 1) * P], wout[:, j, :],
                                       start=(j == 0), stop=(j == GATE_TILES - 1))
                    if n % 2:
                        mm.then_inc(y_mm, 1)

            def feed_forward(k):
                after(pe, xq_done, 1, k, 1)
                after(pe, gate_done, GATE_TILES, k, GATE_TILES)
                for n in range(TT):
                    for t in range(KT):
                        mm = pe.transpose(pg[:, :].bitcast(BF16)[:, (n * KT + t) * P:(n * KT + t + 1) * P],
                                          xq[:, n, t * P:(t + 1) * P], identb[:, :])
                mm.then_inc(xqt_mm, 1)

            def feed_forward_products(k, part):
                if part == 0:
                    after(pe, xqt_done, 1, k, 1)
                    if not last(k):
                        after(pe, tt_done, 2, k + 1, 2)
                for n in range(2 * part, 2 * part + 2):
                    for t in range(KT):
                        for w in range(3):
                            mm = pe.matmul(fr[:, n // 2, (n % 2) * HID:(n % 2 + 1) * HID], xq_t[:, n, t, :],
                                           wsplit[:, w, t, :], start=(t == 0 and w == 0),
                                           stop=(t == KT - 1 and w == 2))
                    if n % 2:
                        mm.then_inc(ffn_mm, 1)

            def turn(k, front, tail):
                if front:
                    project(k + 1, 0)
                if tail:
                    project_out(k - 1, 0)
                merge_second(k, 0)
                if tail:
                    project_out(k - 1, 1)
                merge_second(k, 1)
                for c in range(NC):
                    from_state(k, c)
                    if front and c == 1:
                        project(k + 1, 3)
                    if tail and c == 2:
                        feed_forward_products(k - 1, 0)
                    if front and c == 5:
                        chunk_products(k + 1, 2)
                    if 6 <= c < 8:
                        gates(k, c - 5)
                    solve(k, c)
                    if front and c == 0:
                        project(k + 1, 1)
                    if tail and c == 1:
                        feed_forward(k - 1)
                    if front and c == 1:
                        project(k + 1, 4)
                    if tail and c == 2:
                        feed_forward_products(k - 1, 1)
                    if front and c == 2:
                        project(k + 1, 5)
                    if front and c == 3:
                        exponents(k + 1)
                    if front and c == 4:
                        chunk_products(k + 1, 0)
                    to_state(k, c)
                    if front and c == 4:
                        chunk_products(k + 1, 1)
                    if c == 5:
                        gates(k, 0)
                    if front and c == 0:
                        project(k + 1, 2)
                if front:
                    merge(k + 1)

            pe.wait_ge(ld_wproj, 32)
            pe.wait_ge(ld_x0, 16)
            for j in range(CONV_TILES):
                project(0, j)
            pe.wait_ge(ld_x, 16)
            pe.wait_ge(ld_small, 16 * N_SMALL)
            for n in range(B * T // P):
                for t in range(KT):
                    mm = pe.matmul(fr[:, 0, n * 2 * H:(n + 1) * 2 * H], xt[:, t, n * P:(n + 1) * P],
                                   wab[:, t, :], start=(t == 0), stop=(t == KT - 1))
            mm.then_inc(ab_done, 1)
            pe.wait_ge(ld_const, 16)
            pe.wait_ge(rep_in, 4)
            half = B * T // P // 2
            for n in range(2):
                mm = pe.matmul(fr[:, 1 + n, 0:half * 8 * H], cst[:, C_REP:C_REP + P],
                               rep_rhs[:, n * half:(n + 1) * half, :, :].rearrange("p n h c -> p (n h c)"),
                               start=True, stop=True)
            mm.then_inc(rep_done, 1)
            pe.wait_ge(par_in, 48)
            for n, col in enumerate((C_TRI, C_STRICT, C_ONES)):
                mm = pe.matmul(fr[:, 0, n * PAIRS * U:(n + 1) * PAIRS * U], cst[:, col:col + P],
                               par[:, 0, :], start=True, stop=True)
            mm.then_inc(cum_done, 1)
            exponents(0)
            pe.wait_ge(par_done, 3)
            for g in range(G3):
                chunk_products(0, g)
            merge(0)
            pe.wait_ge(ld_wout, 16)
            turn(0, True, False)
            with pe.Fori(1, PAIRS - 1) as k:
                turn(k, True, True)
            turn(PAIRS - 1, False, True)
            project_out(PAIRS - 1, 0)
            project_out(PAIRS - 1, 1)
            feed_forward(PAIRS - 1)
            feed_forward_products(PAIRS - 1, 0)
            feed_forward_products(PAIRS - 1, 1)

        @block.scalar
        def _(act):
            act.dma_start(cst[:, :], consts).then_inc(ld_const, 16)
            act.dma_start(wconv[:, :, :], w_conv.rearrange("j p m -> p j m")).then_inc(ld_small, 16)
            act.dma_start(nw[:, :], norm_w).then_inc(ld_small, 16)
            act.dma_start(alog[:, :], a_log.to_broadcast([P, H])).then_inc(ld_small, 16)
            act.dma_start(dtb[:, :], dt_bias.to_broadcast([P, H])).then_inc(ld_small, 16)

            def tile_out_of_psum(k, j):
                after(act, proj_done, j + 1, k, CONV_TILES)
                if not first(k) or j >= CONV_DEPTH:
                    after(act, silu_done, j + 1 - CONV_DEPTH if j >= CONV_DEPTH else 0, k, CONV_TILES)
                if not first(k) and j == 1:
                    after(act, y_mm, 0, k - 1, 2)
                bank = pj[:, j % 2, :].rearrange("p (b t) -> p b t", b=2)
                act.activation(raw[:, SLOT[j], :, TAPS - 1:], bank, ACT.Copy)
                act.activation(conv[:, SLOT[j], :, :], bank, ACT.Identity,
                               scale=wconv[:, j, TAPS - 1:TAPS]).then_inc(tile_out, 1)

            def tanh(k, j):
                after(act, conv_done[j], 1, k, 1)
                d = SLOT[j]
                act.activation(raw[:, d, :, TAPS - 1:], conv[:, d, :, :], ACT.Tanh, scale=0.5).then_inc(tanh_done, 1)

            def exp_d(k):
                after(act, dexp_mm, 1, k, 1)
                for n in range(2):
                    e = act.activation(dexp[:, n * UH:(n + 1) * UH, :].rearrange("p u t -> p (u t)"),
                                       pj[:, n, 0:UH * CH], ACT.Exp)
                e.then_inc(dexp_done, 1)

            def to_bd(dst, src, done):
                for h in range(4):
                    rows = slice(32 * h, 32 * h + 32)
                    e = act.activation(dst[rows, :, 32 * h:32 * h + 32], src[rows, :, :], ACT.Copy)
                e.then_inc(done, 1)

            def k_bd(k):
                after(act, silu_done, 3, k, CONV_TILES)
                if not first(k):
                    after(act, merge_mm, 0, k, 2)
                for h in range(4):
                    rows = slice(32 * h, 32 * h + 32)
                    e = act.activation(
                        front_bd[rows, :, 32 * h:32 * h + 32].rearrange("p (g c) t -> p g c t", g=G3),
                        kq[rows, :, 0, :].rearrange("p g (c t) -> p g c t", c=NC), ACT.Copy)
                e.then_inc(kbd_done, 1)

            def square(k):
                after(act, kq_tok_done, 1, k, 1)
                if not first(k):
                    after(act, og_done, 0, k - 1, GATE_TILES)
                act.activation(sq_tok[:, :, :, :, :].rearrange("p g k c d -> p (g k c d)"),
                               kq_tok[:, :, :, :, :].rearrange("p g k c d -> p (g k c d)"),
                               ACT.Square).then_inc(sq_done, 1)

            def merge_bd(k):
                for n in range(2):
                    after(act, p_mm, n + 1, k, 2)
                    units = slice(n * UH, (n + 1) * UH)
                    for h in range(4):
                        rows = slice(32 * h, 32 * h + 32)
                        e = act.activation(p_bd[rows, units, 32 * h:32 * h + 32],
                                           fr[rows, n, 0:UH * CH].rearrange("p (u t) -> p u t", u=UH), ACT.Copy)
                    e.then_inc(pbd_done, 1)

            def handoff(k, front):
                if not first(k):
                    after(act, o_mm, 0, k, NC)
                after(act, at_done, 1, k, 1)
                to_bd(a_bd, a_t, abd_done)
                merge_bd(k)
                if front:
                    tile_out_of_psum(k + 1, 0)
                after(act, kg_done, 1, k, 1)
                to_bd(kg_bd, kg_tok, abd_done)
                after(act, qe_done, 1, k, 1)
                to_bd(qe_bd, qe_ch, abd_done)

            def u_out(k, c):
                after(act, u_mm, c + 1, k, NC)
                act.activation(u_sb[:, :, :].rearrange("p g v -> p (g v)"), pc[:, 0:G3 * DV],
                               ACT.Copy).then_inc(u_done, 1)

            def o_out_of_psum(k, c):
                after(act, o_mm, c + 1, k, NC)
                if c == 0 and not first(k):
                    after(act, on_done, 0, k, 1)
                act.activation(o_all[:, :, c, :], po[:, 0:G3 * DV].rearrange("p (g v) -> p g v", g=G3),
                               ACT.Copy).then_inc(o_out, 1)

            def gate_tanh_(k, j):
                after(act, gate_mm, j + 1, k, GATE_TILES)
                if not first(k) and j == 0:
                    after(act, ffn_in, 0, k, 2)
                act.activation(thg[:, :], pg[:, :], ACT.Tanh, scale=0.5).then_inc(gate_tanh, 1)

            def o_square(k, front):
                after(act, o_out, NC, k, NC)
                after(act, gate_done, GATE_TILES, k, GATE_TILES)
                if front:
                    after(act, v_tok_done, 1, k + 1, 1)
                act.activation(o_sq.rearrange("p u v -> p (u v)"),
                               o_all[:, :, :, :].rearrange("p g c v -> p (g c v)"),
                               ACT.Square).then_inc(osq_done, 1)

            def ternary_out(k):
                after(act, xqt_mm, 1, k, 1)
                act.activation(xq_t.rearrange("p n t q -> p (n t q)"),
                               pg[:, :].bitcast(BF16), ACT.Copy).then_inc(xqt_done, 1)

            def turn(k, front, tail):
                handoff(k, front)
                for c in range(NC):
                    if front and c == 2:
                        tanh(k + 1, 2)
                    if front and c == 4:
                        square(k + 1)
                    if 6 <= c < 8:
                        gate_tanh_(k, c - 5)
                    u_out(k, c)
                    if tail and c == 1:
                        ternary_out(k - 1)
                    if front and c == 0:
                        tanh(k + 1, 0)
                    if front and c == 1:
                        tanh(k + 1, 1)
                        tile_out_of_psum(k + 1, 3)
                    if front and c == 2:
                        tile_out_of_psum(k + 1, 4)
                        tanh(k + 1, 3)
                    if front and c == 3:
                        tanh(k + 1, 4)
                    o_out_of_psum(k, c)
                    if c == 5:
                        gate_tanh_(k, 0)
                    if front and c == 0:
                        tile_out_of_psum(k + 1, 1)
                        tile_out_of_psum(k + 1, 2)
                    if front and c == 2:
                        tile_out_of_psum(k + 1, 5)
                    if front and c == 3:
                        exp_d(k + 1)
                        k_bd(k + 1)
                        tanh(k + 1, 5)
                    if front and c == 4:
                        after(act, v_tok_done, 1, k + 1, 1)
                o_square(k, front)

            act.wait_ge(ld_small, 16 * N_SMALL)
            act.wait_ge(zeroed, 3)
            for j in range(CONV_DEPTH):
                tile_out_of_psum(0, j)
            for j in range(CONV_DEPTH, CONV_TILES):
                tanh(0, j - CONV_DEPTH)
                tile_out_of_psum(0, j)
            act.activation(alog[:, :], alog[:, :], ACT.Exp).then_inc(alog_exp, 1)
            act.wait_ge(abt_abs, 1)
            act.activation(abt[:, :, 0:H], abt[:, :, 0:H], ACT.Exp).then_inc(act_own, 1)
            act.wait_ge(act_own, 1)
            act.activation(abt[:, :, 0:H], abt[:, :, 0:H], ACT.Ln, bias=1.0).then_inc(soft_done, 1)
            act.activation(abt[:, :, H:2 * H], ab[:, :, H:2 * H], ACT.Tanh, scale=0.5).then_inc(soft_done, 1)
            for j in range(CONV_TILES - CONV_DEPTH, CONV_TILES):
                tanh(0, j)
            act.wait_ge(cum_done, 1)
            for n in range(3):
                act.activation(par[:, 2 + n, :], fr[:, 0, n * PAIRS * U:(n + 1) * PAIRS * U],
                               ACT.Exp).then_inc(par_done, 1)
            exp_d(0)
            square(0)
            k_bd(0)
            turn(0, True, False)
            with act.Fori(1, PAIRS - 1) as k:
                turn(k, True, True)
            turn(PAIRS - 1, False, True)
            ternary_out(PAIRS - 1)

        @block.gpsimd
        def _(pool):
            pool.memset(raw[:, :, :, 0:TAPS - 1], 0.0).then_inc(zeroed, 1)
            pool.memset(front_bd[:, :, :], 0.0).then_inc(zeroed, 1)
            pool.memset(l21[:, :, :], 0.0).then_inc(zeroed, 1)
            for t in (qe_bd, kg_bd, a_bd, kc_bd, t_bd):
                pool.memset(t[:, :, :], 0.0).then_inc(zeroed, 1)

            upper = cst[:, C_UPPER:C_UPPER + CH].unsqueeze(1).to_broadcast([P, U, CH])
            lower = cst[:, C_LOWER:C_LOWER + CH].unsqueeze(1).to_broadcast([P, U, CH])

            def units(v):
                return v.unsqueeze(2).to_broadcast([P, U, CH])

            def g_masked(k):
                after(pool, park_done, 1, k, 1)
                if not first(k):
                    after(pool, tt_done, 0, k, 2)
                pool.tensor_tensor(gm[:, :, :], units(park[:, 0, :]), upper, ALU.mult).then_inc(gm_done, 1)

            def d_masked(k):
                after(pool, dexp_done, 1, k, 1)
                pool.tensor_tensor(dt_m[:, :, :], dexp[:, :, :], upper, ALU.mult).then_inc(dt_done, 1)

            def c_masked(k):
                after(pool, dt_done, 1, k, 1)
                after(pool, c2_done, 1, k, 1)
                pool.tensor_tensor(cm[:, :, :], units(c2[:, :]), lower, ALU.mult).then_inc(cm_done, 1)

            def k_decayed(k):
                if not first(k):
                    after(pool, abd_done, 0, k, 3)
                after(pool, kq_tok_done, 1, k, 1)
                for g in range(G3):
                    e = pool.tensor_tensor(kg_tok[:, g * NC:(g + 1) * NC, :], kq_tok[:, g, 0, :, :],
                                           park[:, 3, g * NC:(g + 1) * NC].unsqueeze(2).to_broadcast([P, NC, DK]),
                                           ALU.mult)
                e.then_inc(kg_done, 1)

            def v_scaled(k):
                wait_apart(pool, bv_done, k + 1)
                after(pool, v_tok_done, 1, k, 1)
                if not first(k):
                    after(pool, r_done, 0, k, NC - 1)
                    wait_apart(pool, u_mm, k * NC)
                pool.tensor_copy(decay[:, :, :].rearrange("p g c -> p (g c)"), park[:, 4, :])
                pool.tensor_tensor(rv[:, :, :, :].rearrange("p g c v -> p (g c) v"),
                                   v_tok[:, :, :, :, :].rearrange("p g c h v -> p (g c) (h v)"),
                                   bv[:, :].unsqueeze(2).to_broadcast([P, U, DV]), ALU.mult).then_inc(rv_done, 1)

            def decay_state(k, c):
                after(pool, s_done, c, k, NC - 1)
                after(pool, rv_done, 1, k, 1)
                pool.tensor_tensor(s_dec[:, :, :], s_sb[:, :, :],
                                   decay[:, :, c:c + 1].to_broadcast([P, G3, DV]),
                                   ALU.mult).then_inc(sdec_done, 1)

            def turn(k, front):
                for c in range(NC):
                    if 1 <= c < NC - 1:
                        decay_state(k, c)
                    if front and c == 2:
                        g_masked(k + 1)
                    if front and c == 4:
                        k_decayed(k + 1)
                        d_masked(k + 1)
                        c_masked(k + 1)
                if front:
                    v_scaled(k + 1)

            pool.wait_ge(ld_const, 16)
            g_masked(0)
            d_masked(0)
            k_decayed(0)
            c_masked(0)
            v_scaled(0)
            with pool.Fori(0, PAIRS - 1) as k:
                turn(k, True)
            turn(PAIRS - 1, False)

        @block.vector
        def _(dve):
            own = OwnResults(dve, vec_own)
            x16_final = [0, 0]

            def rsqrt(y, v, t):
                own(dve.tensor_scalar(t.bitcast(I32), v.bitcast(I32), 1, None, ALU.logical_shift_right))
                own(dve.tensor_scalar(y.bitcast(I32), t.bitcast(I32), -1, RSQRT_MAGIC, ALU.mult, ALU.add))
                for _ in range(3):
                    own(dve.tensor_tensor(t, y, y, ALU.mult))
                    own(dve.scalar_tensor_tensor(out=t, in0=t, scalar=-0.5, in1=v, op0=ALU.mult, op1=ALU.mult))
                    own(dve.scalar_tensor_tensor(out=y, in0=t, scalar=1.5, in1=y, op0=ALU.add, op1=ALU.mult))

            def conv_taps(k, j):
                after(dve, tile_out, j + 1, k, CONV_TILES)
                for m in range(TAPS - 1):
                    d = SLOT[j]
                    e = dve.scalar_tensor_tensor(out=conv[:, d, :, :], in0=raw[:, d, :, m:m + T],
                                                 scalar=wconv[:, j, m:m + 1], in1=conv[:, d, :, :],
                                                 op0=ALU.mult, op1=ALU.add)
                    if m < TAPS - 2:
                        own(e)
                    else:
                        e.then_inc(conv_done[j], 1)

            def silu(k, j):
                after(dve, tanh_done, j + 1, k, CONV_TILES)
                if not first(k):
                    if j < 3:
                        after(dve, ga_mm, 0, k, 1)
                A, N = slice(0, 64), slice(64, P)
                both = slice(0, P)
                moves = {
                    0: [(both, None, kq[:, 0:2, 1, :])],
                    1: [(both, None, kq[:, 0:2, 0, :])],
                    2: [(A, 0, kq[A, 2, 1, :]), (A, 1, kq[N, 2, 1, :]),
                        (N, 0, kq[A, 2, 0, :]), (N, 1, kq[N, 2, 0, :])],
                    3: [(both, None, v_ch[:, 0:2, 0, :])],
                    4: [(both, None, v_ch[:, 0:2, 1, :])],
                    5: [(A, 0, v_ch[A, 2, 0, :]), (A, 1, v_ch[N, 2, 0, :]),
                        (N, 0, v_ch[A, 2, 1, :]), (N, 1, v_ch[N, 2, 1, :])],
                }[j]
                for rows, b, dst in moves:
                    src = slice(0, 2) if b is None else b
                    e = dve.scalar_tensor_tensor(out=dst, in0=raw[rows, SLOT[j], src, TAPS - 1:],
                                                 scalar=1.0, in1=conv[rows, SLOT[j], src, :], op0=ALU.add, op1=ALU.mult)
                e.then_inc(silu_done, 1)

            def kq_to_tokens(k):
                after(dve, silu_done, 3, k, CONV_TILES)
                if not first(k):
                    after(dve, kg_done, 0, k, 1)
                    after(dve, ffn_mm, 0, k - 1, 2)
                dve.transpose(kq_tok[:, :, :, :, :].rearrange("p g k c d -> p (g k c d)"),
                              kq[:, :, :, :].rearrange("p g k t -> p (g k t)")).then_inc(kq_tok_done, 1)

            def v_to_tokens(k):
                after(dve, silu_done, CONV_TILES, k, CONV_TILES)
                if not first(k):
                    after(dve, rv_done, 0, k, 1)
                for h in range(2):
                    e = dve.transpose(v_tok[:, :, :, h, :], v_ch[:, :, h, :].rearrange("p g (c t) -> p g c t", c=NC))
                e.then_inc(v_tok_done, 1)

            def pair_parameters(k):
                if not first(k):
                    after(dve, kg_done, 0, k, 1)
                    after(dve, gm_done, 0, k, 1)
                    after(dve, rv_done, 0, k, 1)
                dve.tensor_copy(park[:, :, :], par[:, :, bass.ds(k * U, U)]).then_inc(park_done, 1)

            def factors(k):
                after(dve, sq_done, 1, k, 1)
                after(dve, park_done, 1, k, 1)
                own(dve.tensor_reduce(ss[:, :, :, :].rearrange("p g k c -> p (g k c)"),
                                      sq_tok[:, :, :, :, :].rearrange("p g k c d -> p (g k c) d"), AX.X, ALU.add))
                kk3 = kk[:, :].rearrange("p (g c) -> p g c", g=G3)
                own(dve.tensor_scalar(kk3, ss[:, :, 0, :], EPS_K, None, ALU.add))
                rsqrt(r2[:, :], kk[:, :], rt[:, :])
                own(dve.tensor_tensor(rt[:, :], r2[:, :], r2[:, :], ALU.mult))
                if not first(k):
                    after(dve, cm_done, 0, k, 1)
                    after(dve, rv_done, 0, k, 1)
                dve.scalar_tensor_tensor(out=c2[:, :], in0=rt[:, :], scalar=0.5, in1=park[:, 1, :],
                                         op0=ALU.mult, op1=ALU.mult).then_inc(c2_done, 1)
                dve.scalar_tensor_tensor(out=bv[:, :], in0=r2[:, :], scalar=0.25, in1=park[:, 1, :],
                                         op0=ALU.mult, op1=ALU.mult).then_inc(bv_done, 1)
                after(dve, c2_done, 1, k, 1)
                own(dve.scalar_tensor_tensor(out=nceg[:, :], in0=c2[:, :], scalar=-1.0, in1=park[:, 2, :],
                                             op0=ALU.mult, op1=ALU.mult))

            def scaled_operands(k):
                def rows(v, g):
                    return v[:, g * NC:(g + 1) * NC].unsqueeze(2).to_broadcast([P, NC, DK])
                for g in range(G3):
                    dve.tensor_tensor(kc_tok[:, g * NC:(g + 1) * NC, :], kq_tok[:, g, 0, :, :],
                                      rows(nceg, g), ALU.mult).then_inc(kc_part, 1)
                    dve.tensor_tensor(qe_tok[:, g * NC:(g + 1) * NC, :], kq_tok[:, g, 1, :, :],
                                      rows(park[:, 2, :], g), ALU.mult).then_inc(kc_part, 1)
                after(dve, kc_part, 2 * G3, k, 2 * G3)
                own(dve.transpose(kc_ch[:, :, :].rearrange("p u t -> p (u t)"),
                                  kc_tok[:, :, :].rearrange("p u t -> p (u t)")))
                if not first(k):
                    after(dve, abd_done, 0, k, 3)
                dve.transpose(qe_ch[:, :, :].rearrange("p u t -> p (u t)"),
                              qe_tok[:, :, :].rearrange("p u t -> p (u t)")).then_inc(qe_done, 1)

            def chunk_matrices(k):
                after(dve, dt_done, 1, k, 1)
                own(dve.transpose(d_m[:, :, :].rearrange("p u t -> p (u t)"),
                                  dt_m[:, :, :].rearrange("p u t -> p (u t)")))
                after(dve, ga_mm, 1, k, 1)
                prod = fr[:, :, :].rearrange("p g (c k t) -> p (g c) k t", c=NC, k=2)
                own(dve.tensor_tensor(gd[:, :, :], prod[:, :, 0, :], d_m[:, :, :], ALU.mult))
                if not first(k):
                    after(dve, abd_done, 0, k, 3)
                dve.tensor_tensor(a_t[:, :, :], prod[:, :, 1, :], dt_m[:, :, :], ALU.mult).then_inc(at_done, 1)
                after(dve, cm_done, 1, k, 1)
                own(dve.tensor_tensor(lo[:, :, :], gd[:, :, :], cm[:, :, :], ALU.mult))
                row_a, row_b = cst[:, C_ROWA:C_ROWA + 1], cst[:, C_ROWB:C_ROWB + 1]
                own(dve.scalar_tensor_tensor(out=l16[:, :, :], in0=lo[:, :, 0:HALF], scalar=row_a,
                                             in1=lo[:, :, HALF:CH], op0=ALU.mult, op1=ALU.add))
                own(dve.tensor_scalar(l21[:, :, 0:HALF], lo[:, :, 0:HALF], row_b, None, ALU.mult))
                for h in range(4):
                    rows = slice(32 * h, 32 * h + 32)
                    e = dve.transpose(front_bd[rows, :, 32 * h:32 * h + 32], l21[rows, :, :])
                e.then_inc(l21_done, 1)
                own(dve.tensor_copy(x16[:, :, :],
                                    cst[:, C_EYE16:C_EYE16 + HALF].unsqueeze(1).to_broadcast([P, U, HALF])), wait_apart)

            def substitute(k, i):
                n = i + 1
                parts = [slice(0, UH), slice(UH, U)]
                done = [0, 0]
                for h, u in enumerate(parts):
                    if i > 0:
                        own.until(x16_final[h], wait_apart)
                    done[h] = own.counted(dve.stream_shuffle(b16[:, u, 0:n], x16[:, u, 0:n],
                                                            [i] * HALF + [HALF + i] * HALF))
                for h, u in enumerate(parts):
                    own.until(done[h])
                    done[h] = own.counted(dve.tensor_tensor(
                        p16[:, u, 0:n], b16[:, u, 0:n],
                        l16[:, u, i:i + 1].to_broadcast([P, UH, n]), ALU.mult))
                for h, u in enumerate(parts):
                    own.until(done[h])
                    x16_final[h] = own.counted(dve.tensor_tensor(
                        x16[:, u, 0:n], x16[:, u, 0:n], p16[:, u, 0:n], ALU.subtract))
                if i == HALF - 2:
                    own.until(x16_final[1])

            def halves(k):
                row_a, row_b = cst[:, C_ROWA:C_ROWA + 1], cst[:, C_ROWB:C_ROWB + 1]
                if not first(k):
                    after(dve, merge_mm, 0, k, 2)
                own(dve.tensor_scalar(x32[:, :, 0:HALF], x16[:, :, :], row_a, None, ALU.mult))
                dve.tensor_scalar(x32[:, :, HALF:CH], x16[:, :, :], row_b, None, ALU.mult).then_inc(x32_done, 1)
                after(dve, x32_done, 1, k, 1)
                dve.transpose(y32[:, :, :].rearrange("p u t -> p (u t)"),
                              x32[:, :, :].rearrange("p u t -> p (u t)")).then_inc(y32_done, 1)

            def inverse(k, n):
                after(dve, y32_done, 1, k, 1)
                after(dve, merge_mm, n + 1, k, 2)
                units = slice(n * UH, (n + 1) * UH)
                dve.tensor_tensor(t_t[:, units, :], y32[:, units, :],
                                  fr[:, (2, 0)[n], 0:UH * CH].rearrange("p (u t) -> p u t", u=UH),
                                  ALU.subtract).then_inc(tt_done, 1)

            def to_bd(dst, src):
                for h in range(4):
                    rows = slice(32 * h, 32 * h + 32)
                    e = dve.tensor_copy(dst[rows, :, 32 * h:32 * h + 32], src[rows, :, :])
                e.then_inc(vbd_done, 1)

            def handoff(k, front, tail):
                if not first(k):
                    after(dve, o_mm, 0, k, NC)
                dve.tensor_scalar(eps_o[:, :, :], ss[:, :, 1, :], EPS_O, EPS_O * EPS_K, ALU.mult, ALU.add)
                to_bd(kc_bd, kc_ch)
                if front:
                    conv_taps(k + 1, 0)
                if tail:
                    attention_sum(k - 1, 0)
                inverse(k, 0)
                if tail:
                    attention_sum(k - 1, 1)
                inverse(k, 1)
                after(dve, tt_done, 2, k, 2)
                to_bd(t_bd, t_t)

            def residual(k, c):
                if c > 0:
                    after(dve, ks_mm, c, k, NC - 1)
                    after(dve, rv_done, 1, k, 1)
                    dve.tensor_tensor(r_sb[:, :, :], pc[:, 0:G3 * DV].rearrange("p (g v) -> p g v", g=G3),
                                      rv[:, :, c, :], ALU.add).then_inc(r_done, 1)

            def next_state(k, c):
                if c == NC - 1:
                    return
                after(dve, s_mm, c + 1, k, NC - 1)
                step = pc[:, 0:G3 * DV].rearrange("p (g v) -> p g v", g=G3)
                if c == 0:
                    dve.tensor_copy(s_sb[:, :, :], step).then_inc(s_done, 1)
                else:
                    after(dve, sdec_done, c, k, NC - 2)
                    dve.tensor_tensor(s_sb[:, :, :], s_dec[:, :, :], step, ALU.add).then_inc(s_done, 1)

            def gate_product(k, j):
                after(dve, gate_tanh, j + 1, k, GATE_TILES)
                dve.scalar_tensor_tensor(out=gate[:, j, :], in0=thg[:, :], scalar=1.0, in1=pg[:, :],
                                         op0=ALU.add, op1=ALU.mult).then_inc(gate_done, 1)

            def second_norm(k):
                after(dve, ffn_in, 2, k, 2)
                moments(hid)
                rsqrt(r_n, v_n, t_n)
                normalize(hid, y_out, out_done)

            def head_norm(k, tail):
                if tail:
                    after(dve, ffn_in, 2, k - 1, 2)
                    moments(hid)
                after(dve, osq_done, 1, k, 1)
                own(dve.tensor_reduce(m_o[:, :], o_sq, AX.X, ALU.add))
                own(dve.scalar_tensor_tensor(out=v_o, in0=m_o[:, :], scalar=1.0 / DV,
                                             in1=eps_o[:, :, :].rearrange("p g c -> p (g c)"),
                                             op0=ALU.mult, op1=ALU.add))
                if tail:
                    rsqrt(r_all[:, :], v_all[:, :], t_all[:, :])
                else:
                    rsqrt(r_o, v_o, t_o)
                units = o_all[:, :, :, :].rearrange("p g c v -> p (g c) v")
                dve.tensor_tensor(units, units, r_o.unsqueeze(2).to_broadcast([P, U, DV]),
                                  ALU.mult).then_inc(on_scaled, 1)
                after(dve, on_scaled, 1, k, 1)
                if not first(k):
                    after(dve, y_mm, 0, k, 2)
                for h in range(2):
                    own(dve.transpose(
                        o_ch[:, h, :].rearrange("p (c t) -> p c t", t=CH),
                        o_all[:, 0:2, :, h * 32:(h + 1) * 32].rearrange("p g c v -> p (g c) v")))
                for h in range(2):
                    for b in range(2):
                        e = dve.transpose(
                            o_ch[64 * h:64 * h + 64, 2, b * T:(b + 1) * T].rearrange("p (c t) -> p c t", t=CH),
                            o_all[64 * b:64 * b + 64, 2, :, h * 32:(h + 1) * 32])
                e.then_inc(on_done, 1)

            def gated(k):
                after(dve, on_done, 1, k, 1)
                after(dve, gate_done, GATE_TILES, k, GATE_TILES)
                for j in range(GATE_TILES):
                    dve.scalar_tensor_tensor(out=o_ch[:, j, :], in0=o_ch[:, j, :], scalar=nwh[:, j:j + 1],
                                             in1=gate[:, j, :], op0=ALU.mult, op1=ALU.mult).then_inc(og_done, 1)

            def moments(src):
                for n in range(TT):
                    read = own.counted(dve.bn_stats(stats[:, n, :], src[:, n, :]))
                own.until(read, wait_apart)
                for n in range(TT):
                    read = own.counted(dve.bn_aggr(mv[:, n, :], stats[:, n, :]))
                own.until(read)
                own(dve.tensor_scalar(v_n, mv[:, :, 1], EPS_LN, None, ALU.add))

            def normalize(src, dst, done):
                for n in range(TT):
                    e = dve.tensor_scalar(dst[:, n, :], src[:, n, :], mv[:, n, 0:1], r_n[:, n:n + 1],
                                          ALU.subtract, ALU.mult)
                    if done is None:
                        own(e)
                    elif n % 2:
                        e.then_inc(done, 1)

            def attention_sum(k, n):
                if n == 0:
                    dve.wait_ge(ld_res, (k + 1) * 16)
                    if not first(k):
                        after(dve, st_out, 0, k, 32)
                after(dve, y_mm, n + 1, k, 2)
                dve.tensor_tensor(hid[:, 2 * n:2 * n + 2, :].rearrange("p n c -> p (n c)"), y_bank[n][:, :],
                                  res[:, 2 * n:2 * n + 2, :].rearrange("p n c -> p (n c)"),
                                  ALU.add).then_inc(y_in, 1)

            def first_norm(k):
                after(dve, y_in, 2, k, 2)
                moments(hid)
                rsqrt(r_n, v_n, t_n)

            def ternary(k):
                normalize(hid, x1, None)
                if not last(k):
                    after(dve, kg_done, 1, k + 1, 1)
                own(dve.tensor_scalar(pos[:, :, :], x1[:, :, :], TH_X, None, ALU.is_gt))
                dve.scalar_tensor_tensor(out=xq[:, :, :], in0=x1[:, :, :], scalar=-TH_X, in1=pos[:, :, :],
                                         op0=ALU.is_lt, op1=ALU.subtract).then_inc(xq_done, 1)

            def feed_forward_sum(k):
                for n in range(2):
                    after(dve, ffn_mm, n + 1, k, 2)
                    dve.tensor_tensor(hid[:, 2 * n:2 * n + 2, :].rearrange("p n c -> p (n c)"), fr[:, n, :],
                                      x1[:, 2 * n:2 * n + 2, :].rearrange("p n c -> p (n c)"),
                                      ALU.add).then_inc(ffn_in, 1)

            def turn(k, front, tail):
                handoff(k, front, tail)
                for c in range(NC):
                    residual(k, c)
                    if tail and c == 0:
                        first_norm(k - 1)
                    if front and c == 1:
                        conv_taps(k + 1, 2)
                    if tail and c == 2:
                        feed_forward_sum(k - 1)
                    if front and c == 2:
                        conv_taps(k + 1, 3)
                    if front and c == 3:
                        conv_taps(k + 1, 4)
                    if front and c == 4:
                        silu(k + 1, 4)
                        silu(k + 1, 5)
                        v_to_tokens(k + 1)
                    if front and c == 5:
                        scaled_operands(k + 1)
                    if front and c == 6:
                        for i in range(0, 4):
                            substitute(k + 1, i)
                    if front and c == 7:
                        for i in range(8, 12):
                            substitute(k + 1, i)
                    next_state(k, c)
                    if front and c == 0:
                        silu(k + 1, 0)
                    if tail and c == 0:
                        ternary(k - 1)
                    if front and c == 0:
                        conv_taps(k + 1, 1)
                    if front and c == 1:
                        pair_parameters(k + 1)
                        silu(k + 1, 1)
                    if front and c == 2:
                        silu(k + 1, 2)
                        kq_to_tokens(k + 1)
                    if front and c == 3:
                        silu(k + 1, 3)
                        conv_taps(k + 1, 5)
                    if front and c == 4:
                        factors(k + 1)
                    if front and c == 5:
                        chunk_matrices(k + 1)
                    if c >= 5:
                        gate_product(k, c - 5)
                    if front and c == 6:
                        for i in range(4, 8):
                            substitute(k + 1, i)
                    if front and c == 7:
                        for i in range(12, HALF - 1):
                            substitute(k + 1, i)
                if front:
                    halves(k + 1)
                head_norm(k, tail)
                gated(k)
                if tail:
                    normalize(hid, y_out, out_done)

            dve.wait_ge(ld_small, 16 * N_SMALL)
            for j in (0, 1):
                conv_taps(0, j)
            silu(0, 0)
            silu(0, 1)
            for j in range(2, CONV_TILES):
                conv_taps(0, j)
            own(dve.tensor_scalar(nwh[:, :], nw[:, :], 0.5, None, ALU.mult))
            dve.wait_ge(ab_done, 1)
            own(dve.tensor_copy(ab[:, :, :].rearrange("p n h -> p (n h)"), fr[:, 0, 0:B * T // P * 2 * H]))
            z = ab[:, :, 0:H]
            own(dve.tensor_tensor(z, z, dtb[:, :].unsqueeze(1).to_broadcast([P, B * T // P, H]), ALU.add))
            own(dve.tensor_scalar(abt[:, :, H:], z, -1.0, None, ALU.mult))
            dve.tensor_tensor(abt[:, :, 0:H], z, abt[:, :, H:], ALU.min).then_inc(abt_abs, 1)
            dve.wait_ge(soft_done, 2)
            dve.wait_ge(alog_exp, 1)
            own(dve.scalar_tensor_tensor(out=z, in0=z, scalar=0.0, in1=abt[:, :, 0:H], op0=ALU.max, op1=ALU.add))
            own(dve.scalar_tensor_tensor(out=z, in0=z, scalar=-1.0,
                                         in1=alog[:, :].unsqueeze(1).to_broadcast([P, B * T // P, H]),
                                         op0=ALU.mult, op1=ALU.mult))
            own(dve.tensor_scalar(ab[:, :, H:], abt[:, :, H:], 1.0, None, ALU.add))
            dve.wait_ge(ld_const, 16)
            for c in range(4):
                e = dve.tensor_scalar(rep_rhs[:, :, :, c], ab[:, :, :], cst[:, c:c + 1], None, ALU.mult)
                e.then_inc(rep_in, 1)
            dve.wait_ge(rep_done, 1)
            for kind in range(2):
                for q in range(4):
                    rows = slice(32 * q, 32 * q + 32)
                    for n in range(2):
                        src = fr[rows, 1 + n, 0:n_tiles // 2 * 8 * H].rearrange(
                            "p (k b n h c) -> p k b n h c", k=2, b=2, n=2, c=4)
                        dst = par[rows, kind, :].rearrange("p (k g n c) -> p k g n c", k=PAIRS, g=G3, n=2)
                        for kp in range(2):
                            dve.tensor_copy(
                                dst[:, 2 * n + kp, 0:2, :, :].rearrange("p g n c -> p (g n) c"),
                                src[:, kp, :, :, kind * H + q, :].rearrange("p b n c -> p (b n) c")
                                ).then_inc(par_in, 1)
                        e = dve.tensor_copy(dst[:, 2 * n:2 * n + 2, 2, :, :],
                                            src[:, :, q // 2, :, kind * H + 4 + q % 2, :])
                        e.then_inc(par_in, 1)
            silu(0, 2)
            kq_to_tokens(0)
            silu(0, 3)
            silu(0, 4)
            silu(0, 5)
            v_to_tokens(0)
            dve.wait_ge(par_done, 3)
            dve.wait_ge(par_in, 48)
            pair_parameters(0)
            factors(0)
            scaled_operands(0)
            dve.wait_ge(zeroed, 8)
            chunk_matrices(0)
            for i in range(HALF - 1):
                substitute(0, i)
            halves(0)
            dve.wait_ge(ld_ffn, 32)
            own(dve.tensor_scalar(wtmp[:, :, :], wf[:, :, :], TH_W, SC_W, ALU.is_gt, ALU.mult))
            own(dve.tensor_scalar(wf[:, :, :], wf[:, :, :], -TH_W, -SC_W, ALU.is_lt, ALU.mult))
            own(dve.tensor_tensor(wf[:, :, :], wf[:, :, :], wtmp[:, :, :], ALU.add))
            own(dve.tensor_tensor(wf[:, :, :], wf[:, :, :], wr[:, :, :], ALU.add))
            own(dve.tensor_scalar(wf[:, :, :], wf[:, :, :], -0.5, None, ALU.mult))
            for s in range(3):
                own(dve.tensor_copy(wsplit[:, s, :, :], wf[:, :, :]))
                if s < 2:
                    own(dve.tensor_tensor(wf[:, :, :], wf[:, :, :], wsplit[:, s, :, :], ALU.subtract))
            dve.tensor_copy(identb[:, :], cst[:, C_IDENT:C_IDENT + P]).then_inc(ffn_ready, 1)
            turn(0, True, False)
            assert own.n == VEC_OWN_FIRST, own.n
            with dve.Fori(0, PAIRS - 2) as n:
                own.start(VEC_OWN_FIRST + n * VEC_OWN_TURN)
                turn(n + 1, True, True)
                assert own.n == VEC_OWN_TURN, own.n
            own.start(VEC_OWN_FIRST + (PAIRS - 2) * VEC_OWN_TURN)
            turn(PAIRS - 1, False, True)
            attention_sum(PAIRS - 1, 0)
            attention_sum(PAIRS - 1, 1)
            first_norm(PAIRS - 1)
            ternary(PAIRS - 1)
            feed_forward_sum(PAIRS - 1)
            second_norm(PAIRS - 1)


def constants():
    import numpy as np
    p = np.arange(P)[:, None]
    q = np.arange(P)[None, :]
    same = p // CH == q // CH
    c = np.zeros((P, C_END), np.float32)
    c[:, C_QUARTER:C_QUARTER + 4] = p // CH == np.arange(4)
    c[:, C_REP:C_REP + P] = p % CH == q % CH
    c[:, C_TRI:C_TRI + P] = same & (p <= q)
    c[:, C_STRICT:C_STRICT + P] = same & (p > q)
    c[:, C_ONES:C_ONES + P] = same
    c[:, C_IDENT:C_IDENT + P] = p == q
    c[:, C_UPPER:C_UPPER + CH] = p % CH <= np.arange(CH)
    c[:, C_LOWER:C_LOWER + CH] = p % CH > np.arange(CH)
    c[:, C_EYE16:C_EYE16 + HALF] = p % HALF == np.arange(HALF)
    c[:, C_ROWA:C_ROWA + 1] = p % CH < HALF
    c[:, C_ROWB:C_ROWB + 1] = p % CH >= HALF
    return c


def kernel(L0_attn_hidden_states, L0_attn_Wq, L0_attn_Wk, L0_attn_Wv, L0_attn_Wb, L0_attn_Wa, L0_attn_A_log,
           L0_attn_dt_bias, L0_attn_conv_wq, L0_attn_conv_wk, L0_attn_conv_wv, L0_attn_Wg, L0_attn_norm_w,
           L0_attn_Wo, L0_ffn_weight, L0_ffn_rram_variation):
    import numpy as np
    import concourse.bacc as bacc
    from concourse.bass_utils import run_bass_kernel_spmd

    def whole(a):
        return np.ascontiguousarray(np.asarray(a))

    x = np.asarray(L0_attn_hidden_states)
    lo, hi = np.arange(DV // 2), np.arange(DV // 2, DV)
    v_rows = np.concatenate([h * DV + part for heads, part in
                             (((0, 1, 2, 3), lo), ((0, 1, 2, 3), hi), ((4, 5), lo), ((4, 5), hi)) for h in heads])
    a_rows, b_rows = np.arange(4 * DK), np.arange(4 * DK, H * DK)

    def tiles(q, k, v):
        q, k, v = np.asarray(q), np.asarray(k), np.asarray(v)
        return np.concatenate([q[a_rows], k[a_rows], q[b_rows], k[b_rows], v[v_rows]])

    w_proj = np.concatenate([tiles(L0_attn_Wq, L0_attn_Wk, L0_attn_Wv), np.asarray(L0_attn_Wg)[v_rows]])
    arrays = {
        "x": x,
        "x_t": x.reshape(B * T, HID).T.reshape(KT, P, B * T),
        "w_proj": w_proj.T.reshape(KT, P, -1),
        "w_conv": tiles(L0_attn_conv_wq, L0_attn_conv_wk, L0_attn_conv_wv).reshape(CONV_TILES, P, TAPS),
        "w_ab": np.concatenate([np.asarray(L0_attn_Wa), np.asarray(L0_attn_Wb)]).T.reshape(KT, P, 2 * H),
        "a_log": np.asarray(L0_attn_A_log).reshape(1, H),
        "dt_bias": np.asarray(L0_attn_dt_bias).reshape(1, H),
        "norm_w": np.asarray(L0_attn_norm_w)[v_rows % DV].reshape(GATE_TILES, P).T,
        "w_out": np.asarray(L0_attn_Wo).T[v_rows].reshape(GATE_TILES, P, HID),
        "w_ffn": np.asarray(L0_ffn_weight).T.reshape(KT, P, HID),
        "w_rram": np.asarray(L0_ffn_rram_variation).T.reshape(KT, P, HID),
        "consts": constants(),
    }
    arrays = {name: whole(a) for name, a in arrays.items()}
    nc = bacc.Bacc("TRN2", target_bir_lowering=False, num_devices=1)
    aps = {name: nc.dram_tensor(name, a.shape, mybir.dt.from_np(a.dtype), kind="ExternalInput").ap()
           for name, a in arrays.items()}
    out = nc.dram_tensor("out", (B, T, HID), F32, kind="ExternalOutput").ap()
    program(nc, **aps, out=out)
    return run_bass_kernel_spmd(nc, [arrays], core_ids=[0]).results[0]["out"]
```

```python
from contextlib import ExitStack

import concourse.bass as bass
from concourse import mybir

ALU = mybir.AluOpType
ACT = mybir.ActivationFunctionType
AX = mybir.AxisListType
F32 = mybir.dt.float32
I32 = mybir.dt.int32
BF16 = mybir.dt.bfloat16

P = 128
B, T, HID = 8, 256, 256
H, DK, DV, TAPS = 6, 32, 64, 4
CH = 32
NC = T // CH
PAIRS = B // 2
G3 = 3
U = G3 * NC
TOK = 2 * T
TT = TOK // P
KT = HID // P
CONV_TILES, GATE_TILES = 6, 3
VTILE_LO, VTILE_HI, VTILE_B = 3, 4, 5
HALF = CH // 2
CONV_DEPTH = 4
SLOT = [(j + CONV_DEPTH - 1) % CONV_DEPTH for j in range(CONV_TILES)]
UH = U // 2

EPS_K = 4e-6
EPS_O = 1e-5 * DK
EPS_LN = 1e-5
TH_X, TH_W, SC_W = 0.33, 0.2, 0.6
RSQRT_MAGIC = 0x5F3759DF

C_QUARTER, C_REP, C_TRI, C_STRICT, C_ONES, C_IDENT = 0, 4, 132, 260, 388, 516
C_UPPER, C_LOWER, C_EYE16, C_ROWA, C_ROWB, C_END = 644, 676, 708, 724, 725, 726

VEC_OWN_FIRST, VEC_OWN_TURN = 282, 174


class OwnResults:

    def __init__(self, eng, sem):
        self.eng, self.sem, self.base, self.n = eng, sem, 0, 0

    def start(self, base):
        self.base, self.n = base, 0

    def counted(self, instruction):
        self.n += 1
        instruction.then_inc(self.sem, 1)
        return self.n

    def until(self, n, wait=None):
        if wait:
            wait(self.eng, self.sem, self.base + n)
        else:
            self.eng.wait_ge(self.sem, self.base + n)

    def __call__(self, instruction, wait=None):
        self.until(self.counted(instruction), wait)


def program(nc, x, x_t, w_proj, w_conv, w_ab, a_log, dt_bias, norm_w, w_out, w_ffn, w_rram, consts, out):
    ctx = ExitStack()
    with ctx:
        def sb(name, shape, dt=F32):
            return ctx.enter_context(nc.sbuf_tensor(name, shape, dt))

        def pb(name, shape, dt=F32):
            return ctx.enter_context(nc.psum_tensor(name, shape, dt))

        def sem(name):
            return ctx.enter_context(nc.semaphore(name))

        def view(flat, start, *sizes, dt=F32):
            n = 1
            for size in sizes:
                n *= size
            words = n if dt == F32 else n // 2
            v = flat[:, start:start + words]
            if dt != F32:
                v = v.bitcast(dt)
            names = "abcde"[:len(sizes)]
            return v.rearrange(f"p ({' '.join(names)}) -> p {' '.join(names)}",
                               **dict(zip(names[1:], sizes[1:])))

        cst = sb("cst", [P, C_END])
        xt = sb("xt", [P, KT, B * T])
        wproj = sb("wproj", [P, KT, (CONV_TILES + GATE_TILES) * P])
        wconv = sb("wconv", [P, CONV_TILES, TAPS])
        wab = sb("wab", [P, KT, 2 * H])
        alog = sb("alog", [P, H])
        dtb = sb("dtb", [P, H])
        nw = sb("nw", [P, GATE_TILES])
        nwh = sb("nwh", [P, GATE_TILES])
        wout = sb("wout", [P, GATE_TILES, HID])
        wsplit = sb("wsplit", [P, 3, KT, HID], BF16)
        identb = sb("identb", [P, P], BF16)
        par = sb("par", [P, 5, PAIRS * U])
        park = sb("park", [P, 5, U])
        conv_buf = sb("conv_buf", [P, CONV_DEPTH * TOK])
        tok_buf = sb("tok_buf", [P, G3 * 2 * T])
        gate_buf = sb("gate_buf", [P, GATE_TILES * TOK])
        chunk_buf = sb("chunk_buf", [P, U * CH])
        sub_buf = sb("sub_buf", [P, U * CH])
        hid_buf = sb("hid_buf", [P, TT * HID])
        x1_buf = sb("x1_buf", [P, G3 * 2 * T])
        n_tiles = B * T // P
        rep_rhs = view(gate_buf, 0, n_tiles, 2 * H, 4)
        ab = view(x1_buf, 512, n_tiles, 2 * H)
        abt = view(x1_buf, 512 + n_tiles * 2 * H, n_tiles, 2 * H)
        wf = view(hid_buf, 0, KT, HID)
        wr = view(hid_buf, KT * HID, KT, HID)
        wtmp = view(x1_buf, 0, KT, HID)
        raw = sb("raw", [P, CONV_DEPTH, 2, T + TAPS - 1])
        conv = view(conv_buf, 0, CONV_DEPTH, 2, T)
        kq = sb("kq", [P, G3, 2, T])
        kq_tok = view(tok_buf, 0, G3, 2, NC, DK)
        sq_tok = view(gate_buf, 0, G3, 2, NC, DK)
        ss = sb("ss", [P, G3, 2, NC])
        v_ch = view(x1_buf, 0, G3, 2, T)
        v_tok = sb("v_tok", [P, G3, NC, 2, DV // 2])
        kk = sb("kk", [P, U])
        r2 = sb("r2", [P, U])
        rt = sb("rt", [P, U])
        c2 = sb("c2", [P, U])
        bv = sb("bv", [P, U])
        nceg = sb("nceg", [P, U])
        kc_tok = view(chunk_buf, 0, U, DK)
        qe_tok = view(sub_buf, 0, U, DK)
        kg_tok = sb("kg_tok", [P, U, DK])
        kc_ch = sb("kc_ch", [P, U, CH])
        qe_ch = sb("qe_ch", [P, U, CH])
        gm = sb("gm", [P, U, CH])
        dexp = gm
        dt_m = sb("dt_m", [P, U, CH])
        d_m = view(chunk_buf, 0, U, CH)
        cm = gm
        gd = d_m
        lo = d_m
        l21_t = d_m
        a_t = sb("a_t", [P, U, CH])
        l16 = sb("l16", [P, U, HALF])
        l21 = sb("l21", [P, U, CH])
        x16 = sb("x16", [P, U, HALF])
        b16 = view(sub_buf, 0, U, HALF)
        p16 = view(sub_buf, U * HALF, U, HALF)
        x32 = dt_m
        y32 = gm
        t_t = view(chunk_buf, 0, U, CH)
        front_bd = sb("front_bd", [P, U, P])
        p_bd = front_bd
        kc_bd = sb("kc_bd", [P, U, P])
        qe_bd = sb("qe_bd", [P, U, P])
        kg_bd = sb("kg_bd", [P, U, P])
        t_bd = sb("t_bd", [P, U, P])
        a_bd = sb("a_bd", [P, U, P])
        rv = sb("rv", [P, G3, NC, DV])
        decay = sb("decay", [P, G3, NC])
        eps_o = sb("eps_o", [P, G3, NC])
        r_sb = sb("r_sb", [P, G3, DV])
        u_sb = sb("u_sb", [P, G3, DV])
        s_sb = sb("s_sb", [P, G3, DV])
        s_dec = sb("s_dec", [P, G3, DV])
        o_all = sb("o_all", [P, G3, NC, DV])
        o_sq = view(x1_buf, 0, U, DV)
        thg = view(x1_buf, 0, TOK)
        gate = view(gate_buf, 0, GATE_TILES, TOK)
        m_o = sb("m_o", [P, U])
        v_all = sb("v_all", [P, U + TT])
        r_all = sb("r_all", [P, U + TT])
        t_all = sb("t_all", [P, U + TT])
        (v_o, v_n), (r_o, r_n), (t_o, t_n) = ((t[:, 0:U], t[:, U:]) for t in (v_all, r_all, t_all))
        o_ch = view(conv_buf, 0, GATE_TILES, TOK)
        hid = view(hid_buf, 0, TT, HID)
        x1 = view(x1_buf, 0, TT, HID)
        res = x1
        pos = view(tok_buf, 0, TT, HID, dt=BF16)
        xq = view(tok_buf, TT * HID // 2, TT, HID, dt=BF16)
        xq_t = view(tok_buf, TT * HID, TT, KT, P, dt=BF16)
        stats = sb("stats", [P, TT, 6])
        mv = sb("mv", [P, TT, 2])
        y_out = hid
        UF = U // 2
        end_sq = front_bd[:, 0:U // 2, :].rearrange("p u t -> p (u t)").rearrange("p (g c v) -> p g c v", g=G3, c=NC)
        end_hid = v_tok[:, :, :, :, :].rearrange("p g c h v -> p (g c h v)")[:, 0:TT * HID].rearrange(
            "p (b s c) -> p b s c", b=2, s=2)
        end_x1 = kq[:, :, :, :].rearrange("p g k t -> p (g k t)")[:, 0:TT * HID].rearrange(
            "p (b s c) -> p b s c", b=2, s=2)
        end_pos = view(tok_buf, 0, 2, 2, HID, dt=BF16)
        end_xq = view(tok_buf, TT * HID // 2, 2, 2, HID, dt=BF16)
        end_xq_t = view(tok_buf, TT * HID, 2, 2 * KT * P, dt=BF16)

        pj = pb("pj", [P, 2, 512])
        fr = pb("fr", [P, 3, 512])
        pc = pb("pc", [P, 512])
        po = pb("po", [P, 512])
        pg = pb("pg", [P, 512])
        y_bank = (pg, pj[:, 1, :])
        turn_bank = (fr[:, 2, :], pj[:, 0, :])

        ld_const, ld_conv, ld_x0, ld_x, ld_wproj, ld_wrest, ld_small, ld_wout, ld_res, hid_moved = (
            sem(n) for n in ("ld_const", "ld_conv", "ld_x0", "ld_x", "ld_wproj", "ld_wrest", "ld_small",
                             "ld_wout", "ld_res", "hid_moved"))
        zeroed, vec_own, act_own, ffn_ready = (sem(n) for n in ("zeroed", "vec_own", "act_own", "ffn_ready"))
        proj_done, tile_out, tanh_done, silu_done, kc_part, on_scaled = (
            sem(n) for n in ("proj_done", "tile_out", "tanh_done", "silu_done", "kc_part", "on_scaled"))
        conv_done = [sem(f"conv_done{j}") for j in range(CONV_TILES)]
        ab_done, abt_abs, soft_done, alog_exp, rep_in, rep_done, g_in, beta_in, cum_done, par_done = (
            sem(n) for n in ("ab_done", "abt_abs", "soft_done", "alog_exp", "rep_in",
                             "rep_done", "g_in", "beta_in", "cum_done", "par_done"))
        kq_tok_done, sq_done, park_done, gm_done, dexp_mm, dexp_done, dt_done, c2_done, cm_done, bv_done = (
            sem(n) for n in ("kq_tok_done", "sq_done", "park_done", "gm_done", "dexp_mm", "dexp_done",
                             "dt_done", "c2_done", "cm_done", "bv_done"))
        v_tok_done, qe_done, kg_done, kbd_done, ga_mm, at_done, l21_done, y32_done = (
            sem(n) for n in ("v_tok_done", "qe_done", "kg_done", "kbd_done", "ga_mm", "at_done",
                             "l21_done", "y32_done"))
        lbd_done, x32_done, p_mm, pbd_done, merge_mm, tt_done = (
            sem(n) for n in ("lbd_done", "x32_done", "p_mm", "pbd_done", "merge_mm", "tt_done"))
        rv_done, vbd_done, abd_done = (sem(n) for n in ("rv_done", "vbd_done", "abd_done"))
        ks_mm, r_done, u_mm, u_done, s_mm, s_done, sdec_done, o_mm, o_out = (
            sem(n) for n in ("ks_mm", "r_done", "u_mm", "u_done", "s_mm", "s_done", "sdec_done", "o_mm",
                             "o_out"))
        gate_mm, gate_tanh, gate_done = (sem(n) for n in ("gate_mm", "gate_tanh", "gate_done"))
        osq_done, on_done, og_done, y_mm, y_in, xq_done, xqt_mm, xqt_done, ffn_mm, ffn_in, out_done = (
            sem(n) for n in ("osq_done", "on_done", "og_done", "y_mm", "y_in", "xq_done", "xqt_mm",
                             "xqt_done", "ffn_mm", "ffn_in", "out_done"))

        end_x, end_squared, end_gated, end_y, end_ternary = (
            sem(n) for n in ("end_x", "end_squared", "end_gated", "end_y", "end_ternary"))
        end_turned, end_moved, end_ffn, end_out, end_stored = (
            sem(n) for n in ("end_turned", "end_moved", "end_ffn", "end_out", "end_stored"))

        N_SMALL = 4
        block = ctx.enter_context(nc.Block())

        def after(eng, semaphore, count, k, per_pair):
            eng.wait_ge(semaphore, k * per_pair + count)

        def wait_apart(eng, semaphore, value):
            if not isinstance(value, int):
                eng.compute_val(value)
                eng.wait_ge(ld_const, 16)
            eng.wait_ge(semaphore, value)

        def spread(kind, n):
            moves = []
            for q in range(4):
                rows = slice(32 * q, 32 * q + 32)
                src = fr[rows, 1 + n, 0:n_tiles // 2 * 8 * H].rearrange(
                    "p (k b n h c) -> p k b n h c", k=2, b=2, n=2, c=4)
                dst = par[rows, kind, :].rearrange("p (k g n c) -> p k g n c", k=PAIRS, g=G3, n=2)
                for kp in range(2):
                    moves.append((dst[:, 2 * n + kp, 0:2, :, :].rearrange("p g n c -> p (g n) c"),
                                  src[:, kp, :, :, kind * H + q, :].rearrange("p b n c -> p (b n) c")))
                moves.append((dst[:, 2 * n:2 * n + 2, 2, :, :], src[:, :, q // 2, :, kind * H + 4 + q % 2, :]))
            return moves

        def first(k):
            return isinstance(k, int) and k == 0

        def last(k):
            return isinstance(k, int) and k == PAIRS - 1

        @block.sync
        def _(sp):
            sp.dma_start(wproj[:, :, 0:P], w_proj.rearrange("k p n -> p k n")[:, :, 0:P]).then_inc(ld_wproj, 16)
            sp.dma_start(xt[:, :, 0:TOK], x_t.rearrange("k p n -> p k n")[:, :, 0:TOK]).then_inc(ld_x0, 16)
            sp.dma_start(wproj[:, :, P:], w_proj.rearrange("k p n -> p k n")[:, :, P:]).then_inc(ld_wrest, 16)
            sp.dma_start(wab[:, :, :], w_ab.rearrange("k p n -> p k n")).then_inc(ld_small, 16)
            sp.dma_start(nw[:, :], norm_w).then_inc(ld_small, 16)
            sp.dma_start(alog[:, :], a_log.to_broadcast([P, H])).then_inc(ld_small, 16)
            sp.dma_start(dtb[:, :], dt_bias.to_broadcast([P, H])).then_inc(ld_small, 16)
            sp.dma_start(xt[:, :, TOK:], x_t.rearrange("k p n -> p k n")[:, :, TOK:]).then_inc(ld_x, 16)
            sp.dma_start(wf[:, :, :], w_ffn.rearrange("k p n -> p k n")).then_inc(hid_moved, 16)
            sp.dma_start(wr[:, :, :], w_rram.rearrange("k p n -> p k n")).then_inc(hid_moved, 16)
            sp.dma_start(wout[:, :, :], w_out.rearrange("k p n -> p k n")).then_inc(ld_wout, 16)
            x_pairs = x.rearrange("(q b) t c -> q (b t) c", b=2)
            out_pairs = out.rearrange("(q b) t c -> q (b t) c", b=2)

            def load_residual(k):
                after(sp, on_scaled, 1, k, 1)
                sp.dma_start(res[:, :, :], x_pairs[bass.ds(k, 1), :, :].rearrange(
                    "q (n p) c -> p (q n) c", p=P)).then_inc(ld_res, 16)
            def store(k):
                for n in range(2):
                    after(sp, out_done, n + 1, k, 2)
                    sp.dma_start(out_pairs[bass.ds(k, 1), n * T:(n + 1) * T, :].rearrange(
                        "q (n p) c -> p (q n) c", p=P), y_out[:, 2 * n:2 * n + 2, :]).then_inc(hid_moved, 16)

            load_residual(0)
            with sp.Fori(1, PAIRS - 1) as k:
                load_residual(k)
                store(k - 1)
            sp.wait_ge(vbd_done, 3 * PAIRS)
            sp.dma_start(end_x1.rearrange("p b s c -> p (b s) c"), x_pairs[PAIRS - 1, :, :].rearrange(
                "(n p) c -> p n c", p=P)).then_inc(end_x, 16)
            out_last = out_pairs[PAIRS - 1, :, :].rearrange("(b s p) c -> p b s c", b=2, s=2)
            store(PAIRS - 2)
            for s in range(2):
                sp.wait_ge(end_out, 2 * (s + 1))
                sp.dma_start(out_last[:, :, s, :], end_hid[:, :, s, :]).then_inc(end_stored, 16)
            sp.wait_ge(hid_moved, 16 * 2 * PAIRS)
            sp.wait_ge(end_stored, 32)

        @block.tensor
        def _(pe):
            def project(k, j):
                if not first(k):
                    if j < 2:
                        after(pe, dexp_done, 0, k, 1)
                    if j == 1:
                        after(pe, y_in, 0, k - 1, 2)
                if not (first(k) and j < 2):
                    after(pe, tile_out, j - 1, k, CONV_TILES)
                for t in range(KT):
                    mm = pe.matmul(pj[:, j % 2, :], wproj[:, t, j * P:(j + 1) * P],
                                   xt[:, t, bass.ds(k * TOK, TOK)], start=(t == 0), stop=(t == KT - 1))
                mm.then_inc(proj_done, 1)

            def gates(k, j):
                if not first(k) or j > 0:
                    after(pe, gate_done, j, k, GATE_TILES)
                if not first(k) and j == 0:
                    after(pe, xqt_done, 0, k, 1)
                for t in range(KT):
                    w = CONV_TILES + j
                    mm = pe.matmul(pg[:, :], wproj[:, t, w * P:(w + 1) * P],
                                   xt[:, t, bass.ds(k * TOK, TOK)], start=(t == 0), stop=(t == KT - 1))
                mm.then_inc(gate_mm, 1)

            def exponents(k):
                after(pe, gm_done, 1, k, 1)
                after(pe, tile_out, CONV_TILES, k, CONV_TILES)
                for n in range(2):
                    mm = pe.matmul(pj[:, n, 0:UH * CH], cst[:, C_STRICT:C_STRICT + P],
                                   gm[:, n * UH:(n + 1) * UH, :].rearrange("p u t -> p (u t)"),
                                   start=True, stop=True)
                mm.then_inc(dexp_mm, 1)

            def chunk_products(k, g):
                if g == 0:
                    after(pe, kbd_done, 1, k, 1)
                    after(pe, silu_done, 3, k, CONV_TILES)
                    if not first(k):
                        after(pe, tt_done, 0, k, 2)
                        after(pe, ffn_in, 0, k - 1, 2)
                for c in range(NC):
                    mm = pe.matmul(fr[:, g, c * 2 * CH:(c + 1) * 2 * CH], front_bd[:, g * NC + c, :],
                                   kq[:, g, :, c * CH:(c + 1) * CH], start=True, stop=True)
                mm.then_inc(ga_mm, 1)

            def merge(k):
                after(pe, lbd_done, 1, k, 1)
                after(pe, x32_done, 1, k, 1)
                after(pe, at_done, 1, k, 1)
                for n in range(2):
                    for u in range(UH):
                        mm = pe.matmul(fr[:, n, u * CH:(u + 1) * CH], front_bd[:, n * UH + u, :],
                                       x32[:, n * UH + u, :], start=True, stop=True)
                    mm.then_inc(p_mm, 1)

            def merge_second(k, n):
                if n == 0:
                    after(pe, y32_done, 1, k, 1)
                after(pe, pbd_done, n + 1, k, 2)
                for u in range(UH):
                    mm = pe.matmul(fr[:, (2, 0)[n], u * CH:(u + 1) * CH], p_bd[:, n * UH + u, :],
                                   y32[:, n * UH + u, :], start=True, stop=True)
                mm.then_inc(merge_mm, 1)

            def from_state(k, c):
                if c == 0:
                    return
                after(pe, s_done, c, k, NC - 1)
                for g in range(G3):
                    mm = pe.matmul(pc[:, g * DV:(g + 1) * DV], kc_bd[:, g * NC + c, :], s_sb[:, g, :],
                                   start=True, stop=True)
                mm.then_inc(ks_mm, 1)
                after(pe, o_out, c, k, NC)
                for g in range(G3):
                    pe.matmul(po[:, g * DV:(g + 1) * DV], qe_bd[:, g * NC + c, :], s_sb[:, g, :],
                              start=(g == 0), stop=False, skip_group_check=True)

            def solve(k, c):
                if c == 0:
                    after(pe, vbd_done, 3, k, 3)
                    after(pe, rv_done, 1, k, 1)
                else:
                    after(pe, r_done, c, k, NC - 1)
                for g in range(G3):
                    mm = pe.matmul(pc[:, g * DV:(g + 1) * DV], t_bd[:, g * NC + c, :],
                                   rv[:, g, 0, :] if c == 0 else r_sb[:, g, :], start=True, stop=True)
                mm.then_inc(u_mm, 1)

            def to_state(k, c):
                after(pe, u_done, c + 1, k, NC)
                if c == 0:
                    after(pe, abd_done, 3, k, 3)
                if c < NC - 1:
                    for g in range(G3):
                        mm = pe.matmul(pc[:, g * DV:(g + 1) * DV], kg_bd[:, g * NC + c, :], u_sb[:, g, :],
                                       start=True, stop=True)
                    mm.then_inc(s_mm, 1)
                if c == 0 and not first(k):
                    after(pe, o_out, 0, k, NC)
                for g in range(G3):
                    mm = pe.matmul(po[:, g * DV:(g + 1) * DV], a_bd[:, g * NC + c, :], u_sb[:, g, :],
                                   start=(c == 0 and g == 0), stop=True, skip_group_check=True)
                mm.then_inc(o_mm, 1)

            def project_out(k, part):
                if part == 0:
                    after(pe, og_done, GATE_TILES, k, GATE_TILES)
                for n in range(2 * part, 2 * part + 2):
                    for j in range(GATE_TILES):
                        mm = pe.matmul(y_bank[part][:, (n % 2) * HID:(n % 2 + 1) * HID],
                                       o_ch[:, j, n * P:(n + 1) * P], wout[:, j, :],
                                       start=(j == 0), stop=(j == GATE_TILES - 1))
                    if n % 2:
                        mm.then_inc(y_mm, 1)

            def feed_forward(k):
                after(pe, xq_done, 1, k, 1)
                after(pe, gate_done, GATE_TILES, k, GATE_TILES)
                for n in range(TT):
                    for t in range(KT):
                        mm = pe.transpose(pg[:, :].bitcast(BF16)[:, (n * KT + t) * P:(n * KT + t + 1) * P],
                                          xq[:, n, t * P:(t + 1) * P], identb[:, :])
                mm.then_inc(xqt_mm, 1)

            def feed_forward_products(k, part):
                if part == 0:
                    after(pe, xqt_done, 1, k, 1)
                    if not last(k):
                        after(pe, tt_done, 2, k + 1, 2)
                for n in range(2 * part, 2 * part + 2):
                    for t in range(KT):
                        for w in range(3):
                            mm = pe.matmul(fr[:, n // 2, (n % 2) * HID:(n % 2 + 1) * HID], xq_t[:, n, t, :],
                                           wsplit[:, w, t, :], start=(t == 0 and w == 0),
                                           stop=(t == KT - 1 and w == 2))
                    if n % 2:
                        mm.then_inc(ffn_mm, 1)

            def end_project_out(s):
                pe.wait_ge(end_gated, GATE_TILES * (s + 1))
                for b in range(2):
                    for j in range(GATE_TILES):
                        mm = pe.matmul(y_bank[s][:, b * HID:(b + 1) * HID],
                                       o_ch[:, j, b * T + s * P:b * T + (s + 1) * P], wout[:, j, :],
                                       start=(j == 0), stop=(j == GATE_TILES - 1))
                mm.then_inc(end_y, 1)

            def end_transposes(s):
                pe.wait_ge(end_ternary, s + 1)
                for b in range(2):
                    for t in range(KT):
                        mm = pe.transpose(turn_bank[s].bitcast(BF16)[:, (b * KT + t) * P:(b * KT + t + 1) * P],
                                          end_xq[:, b, s, t * P:(t + 1) * P], identb[:, :])
                mm.then_inc(end_turned, 1)

            def end_feed_forward(s):
                pe.wait_ge(end_moved, s + 1)
                for b in range(2):
                    for t in range(KT):
                        for w in range(3):
                            mm = pe.matmul(fr[:, s, b * HID:(b + 1) * HID],
                                           end_xq_t[:, s, (b * KT + t) * P:(b * KT + t + 1) * P],
                                           wsplit[:, w, t, :], start=(t == 0 and w == 0),
                                           stop=(t == KT - 1 and w == 2))
                mm.then_inc(end_ffn, 1)

            def turn(k, front, tail):
                if front and not first(k):
                    project(k + 1, 0)
                if tail:
                    project_out(k - 1, 0)
                merge_second(k, 0)
                if tail:
                    project_out(k - 1, 1)
                merge_second(k, 1)
                for c in range(NC):
                    from_state(k, c)
                    if front and c == 1:
                        project(k + 1, 3)
                    if tail and c == 2:
                        feed_forward_products(k - 1, 0)
                    if front and 6 <= c < 8:
                        gates(k, c - 5)
                    solve(k, c)
                    if front and c == 0:
                        project(k + 1, 1)
                    if tail and c == 1:
                        feed_forward(k - 1)
                    if front and c == 1:
                        project(k + 1, 4)
                    if tail and c == 2:
                        feed_forward_products(k - 1, 1)
                    if front and c == 2:
                        project(k + 1, 5)
                    if front and c == 3:
                        exponents(k + 1)
                    if front and c == 4:
                        chunk_products(k + 1, 0)
                    to_state(k, c)
                    if front and c == 4:
                        chunk_products(k + 1, 1)
                    if front and c == 5:
                        chunk_products(k + 1, 2)
                    if front and c == 5:
                        gates(k, 0)
                    if not front and 2 <= c < 5:
                        gates(k, c - 2)
                    if front and c == 0:
                        project(k + 1, 2)
                if front:
                    merge(k + 1)

            pe.wait_ge(ld_wproj, 16)
            pe.wait_ge(ld_x0, 16)
            project(0, 0)
            pe.wait_ge(ld_wrest, 16)
            for j in range(1, CONV_TILES):
                project(0, j)
            pe.wait_ge(ld_x, 16)
            pe.wait_ge(ld_small, 16 * N_SMALL)
            for n in range(B * T // P):
                for t in range(KT):
                    mm = pe.matmul(fr[:, 0, n * 2 * H:(n + 1) * 2 * H], xt[:, t, n * P:(n + 1) * P],
                                   wab[:, t, :], start=(t == 0), stop=(t == KT - 1))
            mm.then_inc(ab_done, 1)
            pe.wait_ge(ld_const, 16)
            pe.wait_ge(rep_in, 4)
            half = B * T // P // 2
            for n in range(2):
                mm = pe.matmul(fr[:, 1 + n, 0:half * 8 * H], cst[:, C_REP:C_REP + P],
                               rep_rhs[:, n * half:(n + 1) * half, :, :].rearrange("p n h c -> p (n h c)"),
                               start=True, stop=True)
            mm.then_inc(rep_done, 1)
            pe.wait_ge(g_in, 24)
            for n, col in enumerate((C_TRI, C_STRICT, C_ONES)):
                mm = pe.matmul(fr[:, 0, n * PAIRS * U:(n + 1) * PAIRS * U], cst[:, col:col + P],
                               par[:, 0, :], start=True, stop=True)
            mm.then_inc(cum_done, 1)
            pe.wait_ge(beta_in, 24)
            pe.wait_ge(kbd_done, 1)
            chunk_products(0, 1)
            exponents(0)
            chunk_products(0, 2)
            pe.wait_ge(par_done, 3)
            chunk_products(0, 0)
            project(1, 0)
            merge(0)
            pe.wait_ge(ld_wout, 16)
            turn(0, True, False)
            with pe.Fori(1, PAIRS - 1) as k:
                turn(k, True, True)
            turn(PAIRS - 1, False, True)
            end_project_out(0)
            end_project_out(1)
            end_transposes(0)
            end_feed_forward(0)
            end_transposes(1)
            end_feed_forward(1)

        @block.scalar
        def _(act):
            act.dma_start(wconv[:, :, :], w_conv.rearrange("j p m -> p j m")).then_inc(ld_conv, 16)
            act.dma_start(cst[:, :], consts).then_inc(ld_const, 16)

            def tile_out_of_psum(k, j):
                after(act, proj_done, j + 1, k, CONV_TILES)
                if not first(k) or j >= CONV_DEPTH:
                    after(act, silu_done, j + 1 - CONV_DEPTH if j >= CONV_DEPTH else 0, k, CONV_TILES)
                if not first(k) and j == 1:
                    after(act, y_mm, 0, k - 1, 2)
                bank = pj[:, j % 2, :].rearrange("p (b t) -> p b t", b=2)
                act.activation(raw[:, SLOT[j], :, TAPS - 1:], bank, ACT.Copy)
                act.activation(conv[:, SLOT[j], :, :], bank, ACT.Identity,
                               scale=wconv[:, j, TAPS - 1:TAPS]).then_inc(tile_out, 1)

            def tanh(k, j):
                after(act, conv_done[j], 1, k, 1)
                d = SLOT[j]
                act.activation(raw[:, d, :, TAPS - 1:], conv[:, d, :, :], ACT.Tanh, scale=0.5).then_inc(tanh_done, 1)

            def exp_d(k):
                after(act, dexp_mm, 1, k, 1)
                for n in range(2):
                    e = act.activation(dexp[:, n * UH:(n + 1) * UH, :].rearrange("p u t -> p (u t)"),
                                       pj[:, n, 0:UH * CH], ACT.Exp)
                e.then_inc(dexp_done, 1)

            def to_bd(dst, src, done):
                for h in range(4):
                    rows = slice(32 * h, 32 * h + 32)
                    e = act.activation(dst[rows, :, 32 * h:32 * h + 32], src[rows, :, :], ACT.Copy)
                e.then_inc(done, 1)

            def k_bd(k):
                after(act, silu_done, 3, k, CONV_TILES)
                if not first(k):
                    after(act, merge_mm, 0, k, 2)
                for h in range(4):
                    rows = slice(32 * h, 32 * h + 32)
                    e = act.activation(
                        front_bd[rows, :, 32 * h:32 * h + 32].rearrange("p (g c) t -> p g c t", g=G3),
                        kq[rows, :, 0, :].rearrange("p g (c t) -> p g c t", c=NC), ACT.Copy)
                e.then_inc(kbd_done, 1)

            def l21_bd(k):
                after(act, l21_done, 1, k, 1)
                after(act, ga_mm, G3, k, G3)
                to_bd(front_bd, l21_t, lbd_done)

            def square(k):
                after(act, kq_tok_done, 1, k, 1)
                if not first(k):
                    after(act, og_done, 0, k - 1, GATE_TILES)
                act.activation(sq_tok[:, :, :, :, :].rearrange("p g k c d -> p (g k c d)"),
                               kq_tok[:, :, :, :, :].rearrange("p g k c d -> p (g k c d)"),
                               ACT.Square).then_inc(sq_done, 1)

            def merge_bd(k):
                for n in range(2):
                    after(act, p_mm, n + 1, k, 2)
                    units = slice(n * UH, (n + 1) * UH)
                    for h in range(4):
                        rows = slice(32 * h, 32 * h + 32)
                        e = act.activation(p_bd[rows, units, 32 * h:32 * h + 32],
                                           fr[rows, n, 0:UH * CH].rearrange("p (u t) -> p u t", u=UH), ACT.Copy)
                    e.then_inc(pbd_done, 1)

            def handoff(k, front):
                if not first(k):
                    after(act, o_mm, 0, k, NC)
                after(act, at_done, 1, k, 1)
                if front and first(k):
                    tile_out_of_psum(k + 1, 0)
                to_bd(a_bd, a_t, abd_done)
                merge_bd(k)
                if front and not first(k):
                    tile_out_of_psum(k + 1, 0)
                after(act, kg_done, 1, k, 1)
                to_bd(kg_bd, kg_tok, abd_done)
                after(act, qe_done, 1, k, 1)
                to_bd(qe_bd, qe_ch, abd_done)

            def u_out(k, c):
                after(act, u_mm, c + 1, k, NC)
                act.activation(u_sb[:, :, :].rearrange("p g v -> p (g v)"), pc[:, 0:G3 * DV],
                               ACT.Copy).then_inc(u_done, 1)

            def o_out_of_psum(k, c):
                after(act, o_mm, c + 1, k, NC)
                if c == 0 and not first(k):
                    after(act, on_done, 0, k, 1)
                act.activation(o_all[:, :, c, :], po[:, 0:G3 * DV].rearrange("p (g v) -> p g v", g=G3),
                               ACT.Copy).then_inc(o_out, 1)

            def gate_tanh_(k, j):
                after(act, gate_mm, j + 1, k, GATE_TILES)
                if not first(k) and j == 0:
                    after(act, ffn_in, 0, k, 2)
                act.activation(thg[:, :], pg[:, :], ACT.Tanh, scale=0.5).then_inc(gate_tanh, 1)

            def o_square(k, front):
                after(act, o_out, NC, k, NC)
                after(act, gate_done, GATE_TILES, k, GATE_TILES)
                if front:
                    after(act, v_tok_done, 1, k + 1, 1)
                act.activation(o_sq.rearrange("p u v -> p (u v)"),
                               o_all[:, :, :, :].rearrange("p g c v -> p (g c v)"),
                               ACT.Square).then_inc(osq_done, 1)

            def end_square(s):
                act.wait_ge(o_out, (PAIRS - 1) * NC + (s + 1) * NC // 2)
                if s == 0:
                    act.wait_ge(merge_mm, 2 * PAIRS)
                chunks = slice(s * NC // 2, (s + 1) * NC // 2)
                act.activation(end_sq[:, :, chunks, :], o_all[:, :, chunks, :], ACT.Square).then_inc(end_squared, 1)

            def end_move(s):
                act.wait_ge(end_turned, s + 1)
                act.activation(end_xq_t[:, s, :], turn_bank[s].bitcast(BF16)[:, 0:2 * KT * P],
                               ACT.Copy).then_inc(end_moved, 1)

            def ternary_out(k):
                after(act, xqt_mm, 1, k, 1)
                act.activation(xq_t.rearrange("p n t q -> p (n t q)"),
                               pg[:, :].bitcast(BF16), ACT.Copy).then_inc(xqt_done, 1)

            def turn(k, front, tail):
                handoff(k, front)
                for c in range(NC):
                    if front and c == 2:
                        tanh(k + 1, 2)
                    if front and c == 4:
                        square(k + 1)
                    if front and 6 <= c < 8:
                        gate_tanh_(k, c - 5)
                    if not front and 3 <= c < 6:
                        gate_tanh_(k, c - 3)
                    u_out(k, c)
                    if front and c == 6:
                        l21_bd(k + 1)
                    if tail and c == 1:
                        ternary_out(k - 1)
                    if front and c == 0:
                        tanh(k + 1, 0)
                    if front and c == 1:
                        tanh(k + 1, 1)
                        tile_out_of_psum(k + 1, 3)
                    if front and c == 2:
                        tile_out_of_psum(k + 1, 4)
                        tanh(k + 1, 3)
                    if front and c == 3:
                        tanh(k + 1, 4)
                    o_out_of_psum(k, c)
                    if front and c == 5:
                        gate_tanh_(k, 0)
                    if not front and c == 3:
                        end_square(0)
                    if front and c == 0:
                        tile_out_of_psum(k + 1, 1)
                        tile_out_of_psum(k + 1, 2)
                    if front and c == 2:
                        tile_out_of_psum(k + 1, 5)
                    if front and c == 3:
                        exp_d(k + 1)
                        k_bd(k + 1)
                        tanh(k + 1, 5)
                    if front and c == 4:
                        after(act, v_tok_done, 1, k + 1, 1)
                if front:
                    o_square(k, front)
                else:
                    end_square(1)

            act.wait_ge(ld_conv, 16)
            act.wait_ge(zeroed, 1)
            for j in range(CONV_DEPTH):
                tile_out_of_psum(0, j)
            for j in range(CONV_DEPTH, CONV_TILES):
                tanh(0, j - CONV_DEPTH)
                tile_out_of_psum(0, j)
            for j in range(CONV_TILES - CONV_DEPTH, CONV_TILES):
                tanh(0, j)
            act.wait_ge(ld_small, 16 * N_SMALL)
            act.activation(alog[:, :], alog[:, :], ACT.Exp).then_inc(alog_exp, 1)
            act.wait_ge(abt_abs, 1)
            act.activation(abt[:, :, 0:H], abt[:, :, 0:H], ACT.Exp).then_inc(act_own, 1)
            act.wait_ge(act_own, 1)
            act.activation(abt[:, :, 0:H], abt[:, :, 0:H], ACT.Ln, bias=1.0).then_inc(soft_done, 1)
            act.activation(abt[:, :, H:2 * H], ab[:, :, H:2 * H], ACT.Tanh, scale=0.5).then_inc(soft_done, 1)
            act.wait_ge(rep_done, 1)
            for dst, src in spread(1, 1):
                act.activation(dst, src, ACT.Copy).then_inc(beta_in, 1)
            act.wait_ge(g_in, 12)
            for dst, src in spread(1, 0):
                act.activation(dst, src, ACT.Copy).then_inc(beta_in, 1)
            square(0)
            act.wait_ge(zeroed, 8)
            k_bd(0)
            act.wait_ge(cum_done, 1)
            for n in range(3):
                act.activation(par[:, 2 + n, :], fr[:, 0, n * PAIRS * U:(n + 1) * PAIRS * U],
                               ACT.Exp).then_inc(par_done, 1)
            exp_d(0)
            l21_bd(0)
            turn(0, True, False)
            with act.Fori(1, PAIRS - 1) as k:
                turn(k, True, True)
            turn(PAIRS - 1, False, True)
            for s in range(2):
                end_move(s)

        @block.gpsimd
        def _(pool):
            pool.memset(raw[:, :, :, 0:TAPS - 1], 0.0).then_inc(zeroed, 1)
            pool.memset(front_bd[:, :, :], 0.0).then_inc(zeroed, 1)
            pool.memset(l21[:, :, :], 0.0).then_inc(zeroed, 1)
            for t in (qe_bd, kg_bd, a_bd, kc_bd, t_bd):
                pool.memset(t[:, :, :], 0.0).then_inc(zeroed, 1)

            upper = cst[:, C_UPPER:C_UPPER + CH].unsqueeze(1).to_broadcast([P, U, CH])
            lower = cst[:, C_LOWER:C_LOWER + CH].unsqueeze(1).to_broadcast([P, U, CH])

            def units(v):
                return v.unsqueeze(2).to_broadcast([P, U, CH])

            def g_masked(k):
                after(pool, park_done, 1, k, 1)
                if not first(k):
                    after(pool, tt_done, 0, k, 2)
                pool.tensor_tensor(gm[:, :, :], units(park[:, 0, :]), upper, ALU.mult).then_inc(gm_done, 1)

            def d_masked(k):
                after(pool, dexp_done, 1, k, 1)
                pool.tensor_tensor(dt_m[:, :, :], dexp[:, :, :], upper, ALU.mult).then_inc(dt_done, 1)

            def c_masked(k):
                after(pool, dt_done, 1, k, 1)
                after(pool, c2_done, 1, k, 1)
                pool.tensor_tensor(cm[:, :, :], units(c2[:, :]), lower, ALU.mult).then_inc(cm_done, 1)

            def k_decayed(k):
                if not first(k):
                    after(pool, abd_done, 0, k, 3)
                after(pool, kq_tok_done, 1, k, 1)
                for g in range(G3):
                    e = pool.tensor_tensor(kg_tok[:, g * NC:(g + 1) * NC, :], kq_tok[:, g, 0, :, :],
                                           park[:, 3, g * NC:(g + 1) * NC].unsqueeze(2).to_broadcast([P, NC, DK]),
                                           ALU.mult)
                e.then_inc(kg_done, 1)

            def v_scaled(k):
                wait_apart(pool, bv_done, k + 1)
                after(pool, v_tok_done, 1, k, 1)
                if not first(k):
                    after(pool, r_done, 0, k, NC - 1)
                    wait_apart(pool, u_mm, k * NC)
                pool.tensor_copy(decay[:, :, :].rearrange("p g c -> p (g c)"), park[:, 4, :])
                pool.tensor_tensor(rv[:, :, :, :].rearrange("p g c v -> p (g c) v"),
                                   v_tok[:, :, :, :, :].rearrange("p g c h v -> p (g c) (h v)"),
                                   bv[:, :].unsqueeze(2).to_broadcast([P, U, DV]), ALU.mult).then_inc(rv_done, 1)

            def decay_state(k, c):
                after(pool, s_done, c, k, NC - 1)
                after(pool, rv_done, 1, k, 1)
                pool.tensor_tensor(s_dec[:, :, :], s_sb[:, :, :],
                                   decay[:, :, c:c + 1].to_broadcast([P, G3, DV]),
                                   ALU.mult).then_inc(sdec_done, 1)

            def turn(k, front):
                for c in range(NC):
                    if 1 <= c < NC - 1:
                        decay_state(k, c)
                    if front and c == 2:
                        g_masked(k + 1)
                    if front and c == 4:
                        k_decayed(k + 1)
                        d_masked(k + 1)
                        c_masked(k + 1)
                if front:
                    v_scaled(k + 1)

            pool.wait_ge(ld_const, 16)
            g_masked(0)
            d_masked(0)
            k_decayed(0)
            c_masked(0)
            v_scaled(0)
            with pool.Fori(0, PAIRS - 1) as k:
                turn(k, True)
            turn(PAIRS - 1, False)

        @block.vector
        def _(dve):
            own = OwnResults(dve, vec_own)
            x16_final = [0, 0]

            def rsqrt_estimate(y, v, t):
                own(dve.tensor_scalar(t.bitcast(I32), v.bitcast(I32), 1, None, ALU.logical_shift_right))
                own(dve.tensor_scalar(y.bitcast(I32), t.bitcast(I32), -1, RSQRT_MAGIC, ALU.mult, ALU.add))

            def rsqrt_newton(y, v, t):
                own(dve.tensor_tensor(t, y, y, ALU.mult))
                own(dve.scalar_tensor_tensor(out=t, in0=t, scalar=-0.5, in1=v, op0=ALU.mult, op1=ALU.mult))
                own(dve.scalar_tensor_tensor(out=y, in0=t, scalar=1.5, in1=y, op0=ALU.add, op1=ALU.mult))

            def rsqrt(y, v, t):
                rsqrt_estimate(y, v, t)
                for _ in range(3):
                    rsqrt_newton(y, v, t)

            def conv_taps(k, j):
                after(dve, tile_out, j + 1, k, CONV_TILES)
                for m in range(TAPS - 1):
                    d = SLOT[j]
                    e = dve.scalar_tensor_tensor(out=conv[:, d, :, :], in0=raw[:, d, :, m:m + T],
                                                 scalar=wconv[:, j, m:m + 1], in1=conv[:, d, :, :],
                                                 op0=ALU.mult, op1=ALU.add)
                    if m < TAPS - 2:
                        own(e)
                    else:
                        e.then_inc(conv_done[j], 1)

            def silu(k, j):
                after(dve, tanh_done, j + 1, k, CONV_TILES)
                if not first(k):
                    if j < 3:
                        after(dve, ga_mm, 0, k, G3)
                A, N = slice(0, 64), slice(64, P)
                both = slice(0, P)
                moves = {
                    0: [(both, None, kq[:, 0:2, 1, :])],
                    1: [(both, None, kq[:, 0:2, 0, :])],
                    2: [(A, 0, kq[A, 2, 1, :]), (A, 1, kq[N, 2, 1, :]),
                        (N, 0, kq[A, 2, 0, :]), (N, 1, kq[N, 2, 0, :])],
                    3: [(both, None, v_ch[:, 0:2, 0, :])],
                    4: [(both, None, v_ch[:, 0:2, 1, :])],
                    5: [(A, 0, v_ch[A, 2, 0, :]), (A, 1, v_ch[N, 2, 0, :]),
                        (N, 0, v_ch[A, 2, 1, :]), (N, 1, v_ch[N, 2, 1, :])],
                }[j]
                for rows, b, dst in moves:
                    src = slice(0, 2) if b is None else b
                    e = dve.scalar_tensor_tensor(out=dst, in0=raw[rows, SLOT[j], src, TAPS - 1:],
                                                 scalar=1.0, in1=conv[rows, SLOT[j], src, :], op0=ALU.add, op1=ALU.mult)
                e.then_inc(silu_done, 1)

            def kq_to_tokens(k):
                after(dve, silu_done, 3, k, CONV_TILES)
                if not first(k):
                    after(dve, kg_done, 0, k, 1)
                    after(dve, ffn_mm, 0, k - 1, 2)
                dve.transpose(kq_tok[:, :, :, :, :].rearrange("p g k c d -> p (g k c d)"),
                              kq[:, :, :, :].rearrange("p g k t -> p (g k t)")).then_inc(kq_tok_done, 1)

            def v_to_tokens(k):
                after(dve, silu_done, CONV_TILES, k, CONV_TILES)
                if not first(k):
                    after(dve, rv_done, 0, k, 1)
                for h in range(2):
                    e = dve.transpose(v_tok[:, :, :, h, :], v_ch[:, :, h, :].rearrange("p g (c t) -> p g c t", c=NC))
                e.then_inc(v_tok_done, 1)

            def pair_parameters(k):
                if not first(k):
                    after(dve, kg_done, 0, k, 1)
                    after(dve, gm_done, 0, k, 1)
                    after(dve, rv_done, 0, k, 1)
                dve.tensor_copy(park[:, :, :], par[:, :, bass.ds(k * U, U)]).then_inc(park_done, 1)

            def factors(k):
                after(dve, sq_done, 1, k, 1)
                after(dve, park_done, 1, k, 1)
                own(dve.tensor_reduce(ss[:, :, :, :].rearrange("p g k c -> p (g k c)"),
                                      sq_tok[:, :, :, :, :].rearrange("p g k c d -> p (g k c) d"), AX.X, ALU.add))
                kk3 = kk[:, :].rearrange("p (g c) -> p g c", g=G3)
                own(dve.tensor_scalar(kk3, ss[:, :, 0, :], EPS_K, None, ALU.add))
                rsqrt(r2[:, :], kk[:, :], rt[:, :])
                own(dve.tensor_tensor(rt[:, :], r2[:, :], r2[:, :], ALU.mult))
                if not first(k):
                    after(dve, cm_done, 0, k, 1)
                    after(dve, rv_done, 0, k, 1)
                dve.scalar_tensor_tensor(out=c2[:, :], in0=rt[:, :], scalar=0.5, in1=park[:, 1, :],
                                         op0=ALU.mult, op1=ALU.mult).then_inc(c2_done, 1)
                dve.scalar_tensor_tensor(out=bv[:, :], in0=r2[:, :], scalar=0.25, in1=park[:, 1, :],
                                         op0=ALU.mult, op1=ALU.mult).then_inc(bv_done, 1)
                after(dve, c2_done, 1, k, 1)
                own(dve.scalar_tensor_tensor(out=nceg[:, :], in0=c2[:, :], scalar=-1.0, in1=park[:, 2, :],
                                             op0=ALU.mult, op1=ALU.mult))

            def scaled_operands(k):
                def rows(v, g):
                    return v[:, g * NC:(g + 1) * NC].unsqueeze(2).to_broadcast([P, NC, DK])
                for g in range(G3):
                    dve.tensor_tensor(kc_tok[:, g * NC:(g + 1) * NC, :], kq_tok[:, g, 0, :, :],
                                      rows(nceg, g), ALU.mult).then_inc(kc_part, 1)
                    dve.tensor_tensor(qe_tok[:, g * NC:(g + 1) * NC, :], kq_tok[:, g, 1, :, :],
                                      rows(park[:, 2, :], g), ALU.mult).then_inc(kc_part, 1)
                after(dve, kc_part, 2 * G3, k, 2 * G3)
                own(dve.transpose(kc_ch[:, :, :].rearrange("p u t -> p (u t)"),
                                  kc_tok[:, :, :].rearrange("p u t -> p (u t)")))
                if not first(k):
                    after(dve, abd_done, 0, k, 3)
                dve.transpose(qe_ch[:, :, :].rearrange("p u t -> p (u t)"),
                              qe_tok[:, :, :].rearrange("p u t -> p (u t)")).then_inc(qe_done, 1)

            def chunk_matrices(k):
                after(dve, dt_done, 1, k, 1)
                own(dve.transpose(d_m[:, :, :].rearrange("p u t -> p (u t)"),
                                  dt_m[:, :, :].rearrange("p u t -> p (u t)")))
                after(dve, ga_mm, G3, k, G3)
                prod = fr[:, :, :].rearrange("p g (c k t) -> p (g c) k t", c=NC, k=2)
                own(dve.tensor_tensor(gd[:, :, :], prod[:, :, 0, :], d_m[:, :, :], ALU.mult))
                if not first(k):
                    after(dve, abd_done, 0, k, 3)
                dve.tensor_tensor(a_t[:, :, :], prod[:, :, 1, :], dt_m[:, :, :], ALU.mult).then_inc(at_done, 1)
                after(dve, cm_done, 1, k, 1)
                own(dve.tensor_tensor(lo[:, :, :], gd[:, :, :], cm[:, :, :], ALU.mult))
                row_a, row_b = cst[:, C_ROWA:C_ROWA + 1], cst[:, C_ROWB:C_ROWB + 1]
                own(dve.scalar_tensor_tensor(out=l16[:, :, :], in0=lo[:, :, 0:HALF], scalar=row_a,
                                             in1=lo[:, :, HALF:CH], op0=ALU.mult, op1=ALU.add))
                own(dve.tensor_scalar(l21[:, :, 0:HALF], lo[:, :, 0:HALF], row_b, None, ALU.mult))
                dve.transpose(l21_t[:, :, :].rearrange("p u t -> p (u t)"),
                              l21[:, :, :].rearrange("p u t -> p (u t)")).then_inc(l21_done, 1)
                own(dve.tensor_copy(x16[:, :, :],
                                    cst[:, C_EYE16:C_EYE16 + HALF].unsqueeze(1).to_broadcast([P, U, HALF])), wait_apart)

            def substitute(k, i):
                n = i + 1
                parts = [slice(0, UH), slice(UH, U)]
                done = [0, 0]
                for h, u in enumerate(parts):
                    if i > 0:
                        own.until(x16_final[h], wait_apart)
                    done[h] = own.counted(dve.stream_shuffle(b16[:, u, 0:n], x16[:, u, 0:n],
                                                            [i] * HALF + [HALF + i] * HALF))
                for h, u in enumerate(parts):
                    own.until(done[h])
                    done[h] = own.counted(dve.tensor_tensor(
                        p16[:, u, 0:n], b16[:, u, 0:n],
                        l16[:, u, i:i + 1].to_broadcast([P, UH, n]), ALU.mult))
                for h, u in enumerate(parts):
                    own.until(done[h])
                    x16_final[h] = own.counted(dve.tensor_tensor(
                        x16[:, u, 0:n], x16[:, u, 0:n], p16[:, u, 0:n], ALU.subtract))
                if i == HALF - 2:
                    own.until(x16_final[1])

            def halves(k):
                row_a, row_b = cst[:, C_ROWA:C_ROWA + 1], cst[:, C_ROWB:C_ROWB + 1]
                if not first(k):
                    after(dve, merge_mm, 0, k, 2)
                own(dve.tensor_scalar(x32[:, :, 0:HALF], x16[:, :, :], row_a, None, ALU.mult))
                dve.tensor_scalar(x32[:, :, HALF:CH], x16[:, :, :], row_b, None, ALU.mult).then_inc(x32_done, 1)
                after(dve, x32_done, 1, k, 1)
                dve.transpose(y32[:, :, :].rearrange("p u t -> p (u t)"),
                              x32[:, :, :].rearrange("p u t -> p (u t)")).then_inc(y32_done, 1)

            def inverse(k, n):
                after(dve, y32_done, 1, k, 1)
                after(dve, merge_mm, n + 1, k, 2)
                units = slice(n * UH, (n + 1) * UH)
                dve.tensor_tensor(t_t[:, units, :], y32[:, units, :],
                                  fr[:, (2, 0)[n], 0:UH * CH].rearrange("p (u t) -> p u t", u=UH),
                                  ALU.subtract).then_inc(tt_done, 1)

            def to_bd(dst, src, units):
                for h in range(4):
                    rows = slice(32 * h, 32 * h + 32)
                    e = dve.tensor_copy(dst[rows, units, 32 * h:32 * h + 32], src[rows, units, :])
                e.then_inc(vbd_done, 1)

            def handoff(k, front, tail):
                if not first(k):
                    after(dve, o_mm, 0, k, NC)
                dve.tensor_scalar(eps_o[:, :, :], ss[:, :, 1, :], EPS_O, EPS_O * EPS_K, ALU.mult, ALU.add)
                to_bd(kc_bd, kc_ch, slice(0, U))
                if front:
                    conv_taps(k + 1, 0)
                if tail:
                    attention_sum(k - 1, 0)
                inverse(k, 0)
                after(dve, tt_done, 1, k, 2)
                to_bd(t_bd, t_t, slice(0, UH))
                if tail:
                    attention_sum(k - 1, 1)
                inverse(k, 1)
                after(dve, tt_done, 2, k, 2)
                to_bd(t_bd, t_t, slice(UH, U))

            def residual(k, c):
                if c > 0:
                    after(dve, ks_mm, c, k, NC - 1)
                    after(dve, rv_done, 1, k, 1)
                    dve.tensor_tensor(r_sb[:, :, :], pc[:, 0:G3 * DV].rearrange("p (g v) -> p g v", g=G3),
                                      rv[:, :, c, :], ALU.add).then_inc(r_done, 1)

            def next_state(k, c):
                if c == NC - 1:
                    return
                after(dve, s_mm, c + 1, k, NC - 1)
                step = pc[:, 0:G3 * DV].rearrange("p (g v) -> p g v", g=G3)
                if c == 0:
                    dve.tensor_copy(s_sb[:, :, :], step).then_inc(s_done, 1)
                else:
                    after(dve, sdec_done, c, k, NC - 2)
                    dve.tensor_tensor(s_sb[:, :, :], s_dec[:, :, :], step, ALU.add).then_inc(s_done, 1)

            def gate_product(k, j):
                after(dve, gate_tanh, j + 1, k, GATE_TILES)
                dve.scalar_tensor_tensor(out=gate[:, j, :], in0=thg[:, :], scalar=1.0, in1=pg[:, :],
                                         op0=ALU.add, op1=ALU.mult).then_inc(gate_done, 1)

            def head_norm(k, tail):
                after(dve, osq_done, 1, k, 1)
                own(dve.tensor_reduce(m_o[:, :], o_sq, AX.X, ALU.add))
                own(dve.scalar_tensor_tensor(out=v_o, in0=m_o[:, :], scalar=1.0 / DV,
                                             in1=eps_o[:, :, :].rearrange("p g c -> p (g c)"),
                                             op0=ALU.mult, op1=ALU.add))
                if tail:
                    rsqrt(r_all[:, :], v_all[:, :], t_all[:, :])
                else:
                    rsqrt(r_o, v_o, t_o)
                units = o_all[:, :, :, :].rearrange("p g c v -> p (g c) v")
                dve.tensor_tensor(units, units, r_o.unsqueeze(2).to_broadcast([P, U, DV]),
                                  ALU.mult).then_inc(on_scaled, 1)
                after(dve, on_scaled, 1, k, 1)
                if not first(k):
                    after(dve, y_mm, 0, k, 2)
                for h in range(2):
                    own(dve.transpose(
                        o_ch[:, h, :].rearrange("p (c t) -> p c t", t=CH),
                        o_all[:, 0:2, :, h * 32:(h + 1) * 32].rearrange("p g c v -> p (g c) v")))
                for h in range(2):
                    for b in range(2):
                        e = dve.transpose(
                            o_ch[64 * h:64 * h + 64, 2, b * T:(b + 1) * T].rearrange("p (c t) -> p c t", t=CH),
                            o_all[64 * b:64 * b + 64, 2, :, h * 32:(h + 1) * 32])
                e.then_inc(on_done, 1)

            def gated(k):
                after(dve, on_done, 1, k, 1)
                after(dve, gate_done, GATE_TILES, k, GATE_TILES)
                for j in range(GATE_TILES):
                    dve.scalar_tensor_tensor(out=o_ch[:, j, :], in0=o_ch[:, j, :], scalar=nwh[:, j:j + 1],
                                             in1=gate[:, j, :], op0=ALU.mult, op1=ALU.mult).then_inc(og_done, 1)

            def moments(src):
                for n in range(TT):
                    read = own.counted(dve.bn_stats(stats[:, n, :], src[:, n, :]))
                own.until(read, wait_apart)
                for n in range(TT):
                    read = own.counted(dve.bn_aggr(mv[:, n, :], stats[:, n, :]))
                own.until(read)
                own(dve.tensor_scalar(v_n, mv[:, :, 1], EPS_LN, None, ALU.add))

            def normalize(src, dst, done):
                for n in range(TT):
                    e = dve.tensor_scalar(dst[:, n, :], src[:, n, :], mv[:, n, 0:1], r_n[:, n:n + 1],
                                          ALU.subtract, ALU.mult)
                    if done is None:
                        own(e)
                    elif n % 2:
                        e.then_inc(done, 1)

            def attention_sum(k, n):
                if n == 0:
                    dve.wait_ge(ld_res, (k + 1) * 16)
                    after(dve, hid_moved, 32, k, 32)
                after(dve, y_mm, n + 1, k, 2)
                dve.tensor_tensor(hid[:, 2 * n:2 * n + 2, :].rearrange("p n c -> p (n c)"), y_bank[n][:, :],
                                  res[:, 2 * n:2 * n + 2, :].rearrange("p n c -> p (n c)"),
                                  ALU.add).then_inc(y_in, 1)

            def first_norm(k):
                after(dve, y_in, 2, k, 2)
                moments(hid)
                rsqrt(r_n, v_n, t_n)

            def ternary(k):
                normalize(hid, x1, None)
                if not last(k):
                    after(dve, kg_done, 1, k + 1, 1)
                own(dve.tensor_scalar(pos[:, :, :], x1[:, :, :], TH_X, None, ALU.is_gt))
                dve.scalar_tensor_tensor(out=xq[:, :, :], in0=x1[:, :, :], scalar=-TH_X, in1=pos[:, :, :],
                                         op0=ALU.is_lt, op1=ALU.subtract).then_inc(xq_done, 1)

            def feed_forward_sum(k):
                for n in range(2):
                    after(dve, ffn_mm, n + 1, k, 2)
                    dve.tensor_tensor(hid[:, 2 * n:2 * n + 2, :].rearrange("p n c -> p (n c)"), fr[:, n, :],
                                      x1[:, 2 * n:2 * n + 2, :].rearrange("p n c -> p (n c)"),
                                      ALU.add).then_inc(ffn_in, 1)

            head_v, head_r = ([a[:, UF:U], a[:, 0:UF]] for a in (v_all, r_all))

            def end_head_sums(s):
                chunks = slice(s * NC // 2, (s + 1) * NC // 2)
                m = m_o[:, 0:UF].rearrange("p (g c) -> p g c", g=G3)
                dve.wait_ge(end_squared, s + 1)
                own(dve.tensor_reduce(m, end_sq[:, :, chunks, :], AX.X, ALU.add))
                own(dve.scalar_tensor_tensor(out=head_v[s].rearrange("p (g c) -> p g c", g=G3), in0=m,
                                             scalar=1.0 / DV, in1=eps_o[:, :, chunks], op0=ALU.mult, op1=ALU.add))

            def end_head_scale(s):
                part = o_all[:, :, s * NC // 2:(s + 1) * NC // 2, :]
                factor = head_r[s].rearrange("p (g c) -> p g c", g=G3).unsqueeze(3)
                own(dve.tensor_tensor(part, part, factor.to_broadcast([P, G3, NC // 2, DV]), ALU.mult))

            def end_to_channels(s):
                chunks = slice(s * NC // 2, (s + 1) * NC // 2)
                dve.wait_ge(y_mm, 2 * (PAIRS - 1))
                for h in range(2):
                    for b in range(2):
                        cols = slice(b * T + s * P, b * T + (s + 1) * P)
                        own.counted(dve.transpose(o_ch[:, h, cols].rearrange("p (c t) -> p c t", t=CH),
                                                  o_all[:, b, chunks, h * 32:(h + 1) * 32]))
                        e = own.counted(dve.transpose(
                            o_ch[64 * h:64 * h + 64, 2, cols].rearrange("p (c t) -> p c t", t=CH),
                            o_all[64 * b:64 * b + 64, 2, chunks, h * 32:(h + 1) * 32]))
                own.until(e)

            def end_gate(s):
                dve.wait_ge(gate_done, GATE_TILES * PAIRS)
                for j in range(GATE_TILES):
                    o_half, g_half = (a[:, j, :].rearrange("p (b s t) -> p b s t", b=2, s=2)[:, :, s, :]
                                      for a in (o_ch, gate))
                    dve.scalar_tensor_tensor(out=o_half, in0=o_half, scalar=nwh[:, j:j + 1], in1=g_half,
                                             op0=ALU.mult, op1=ALU.mult).then_inc(end_gated, 1)

            def end_factors(s):
                for b in range(2):
                    e = own.counted(dve.bn_stats(stats[:, b, :], end_hid[:, b, s, :]))
                own.until(e, wait_apart)
                for b in range(2):
                    e = own.counted(dve.bn_aggr(mv[:, b, :], stats[:, b, :]))
                own.until(e)
                own(dve.tensor_scalar(v_n[:, 0:2], mv[:, 0:2, 1], EPS_LN, None, ALU.add))
                rsqrt(r_n[:, 0:2], v_n[:, 0:2], t_n[:, 0:2])

            def end_first_norm(s):
                dve.wait_ge(end_x, 16)
                dve.wait_ge(end_y, s + 1)
                own(dve.tensor_tensor(end_hid[:, :, s, :], y_bank[s].rearrange("p (b c) -> p b c", b=2)
                                      if s else pg[:, :].rearrange("p (b c) -> p b c", b=2),
                                      end_x1[:, :, s, :], ALU.add), wait_apart)
                end_factors(s)
                for b in range(2):
                    e = own.counted(dve.tensor_scalar(end_x1[:, b, s, :], end_hid[:, b, s, :], mv[:, b, 0:1],
                                                      r_n[:, b:b + 1], ALU.subtract, ALU.mult))
                own.until(e)
                own(dve.tensor_scalar(end_pos[:, :, s, :], end_x1[:, :, s, :], TH_X, None, ALU.is_gt))
                dve.scalar_tensor_tensor(out=end_xq[:, :, s, :], in0=end_x1[:, :, s, :], scalar=-TH_X,
                                         in1=end_pos[:, :, s, :], op0=ALU.is_lt,
                                         op1=ALU.subtract).then_inc(end_ternary, 1)

            def end_second_norm(s):
                dve.wait_ge(end_ffn, s + 1)
                own(dve.tensor_tensor(end_hid[:, :, s, :], fr[:, s, :].rearrange("p (b c) -> p b c", b=2),
                                      end_x1[:, :, s, :], ALU.add), wait_apart)
                end_factors(s)
                for b in range(2):
                    dve.tensor_scalar(end_hid[:, b, s, :], end_hid[:, b, s, :], mv[:, b, 0:1], r_n[:, b:b + 1],
                                      ALU.subtract, ALU.mult).then_inc(end_out, 1)

            def turn(k, front, tail):
                handoff(k, front, tail)
                for c in range(NC):
                    residual(k, c)
                    if tail and c == 0:
                        first_norm(k - 1)
                    if front and c == 1:
                        conv_taps(k + 1, 2)
                    if tail and c == 2:
                        feed_forward_sum(k - 1)
                    if front and c == 2:
                        conv_taps(k + 1, 3)
                    if front and c == 3:
                        conv_taps(k + 1, 4)
                    if front and c == 4:
                        silu(k + 1, 4)
                        silu(k + 1, 5)
                        v_to_tokens(k + 1)
                    if not front and 3 <= c < 6:
                        gate_product(k, c - 3)
                    if not front and c == 4:
                        end_head_sums(0)
                    if tail and c == 3:
                        moments(hid)
                    both = (r_all[:, UF:], v_all[:, UF:], t_all[:, UF:])
                    if not front and c == 5:
                        rsqrt_estimate(*both)
                        rsqrt_newton(*both)
                    if not front and c == 6:
                        rsqrt_newton(*both)
                        rsqrt_newton(*both)
                        end_head_scale(0)
                    if not front and c == 7:
                        end_to_channels(0)
                        end_gate(0)
                        normalize(hid, y_out, out_done)
                    if front and c == 5:
                        scaled_operands(k + 1)
                    if front and c == 6:
                        for i in range(0, 4):
                            substitute(k + 1, i)
                    if front and c == 7:
                        for i in range(8, 12):
                            substitute(k + 1, i)
                    next_state(k, c)
                    if front and c == 0:
                        silu(k + 1, 0)
                    if tail and c == 0:
                        ternary(k - 1)
                    if front and c == 0:
                        conv_taps(k + 1, 1)
                    if front and c == 1:
                        pair_parameters(k + 1)
                        silu(k + 1, 1)
                    if front and c == 2:
                        silu(k + 1, 2)
                        kq_to_tokens(k + 1)
                    if front and c == 3:
                        silu(k + 1, 3)
                        conv_taps(k + 1, 5)
                    if front and c == 4:
                        factors(k + 1)
                    if front and c == 5:
                        chunk_matrices(k + 1)
                    if front and 5 <= c < NC - 1:
                        gate_product(k, c - 5)
                    if front and c == 6:
                        for i in range(4, 8):
                            substitute(k + 1, i)
                    if front and c == 7:
                        for i in range(12, HALF - 1):
                            substitute(k + 1, i)
                if front:
                    halves(k + 1)
                    gate_product(k, 2)
                    head_norm(k, tail)
                    gated(k)
                    if tail:
                        normalize(hid, y_out, out_done)

            dve.wait_ge(ld_conv, 16)
            for j in (0, 1):
                conv_taps(0, j)
            silu(0, 0)
            silu(0, 1)
            for j in range(2, CONV_TILES):
                conv_taps(0, j)
            dve.wait_ge(ld_small, 16 * N_SMALL)
            own(dve.tensor_scalar(nwh[:, :], nw[:, :], 0.5, None, ALU.mult))
            dve.wait_ge(ab_done, 1)
            own(dve.tensor_copy(ab[:, :, :].rearrange("p n h -> p (n h)"), fr[:, 0, 0:B * T // P * 2 * H]))
            z = ab[:, :, 0:H]
            own(dve.tensor_tensor(z, z, dtb[:, :].unsqueeze(1).to_broadcast([P, B * T // P, H]), ALU.add))
            own(dve.tensor_scalar(abt[:, :, H:], z, -1.0, None, ALU.mult))
            dve.tensor_tensor(abt[:, :, 0:H], z, abt[:, :, H:], ALU.min).then_inc(abt_abs, 1)
            silu(0, 2)
            kq_to_tokens(0)
            dve.wait_ge(soft_done, 2)
            dve.wait_ge(alog_exp, 1)
            own(dve.scalar_tensor_tensor(out=z, in0=z, scalar=0.0, in1=abt[:, :, 0:H], op0=ALU.max, op1=ALU.add))
            own(dve.scalar_tensor_tensor(out=z, in0=z, scalar=-1.0,
                                         in1=alog[:, :].unsqueeze(1).to_broadcast([P, B * T // P, H]),
                                         op0=ALU.mult, op1=ALU.mult))
            own(dve.tensor_scalar(ab[:, :, H:], abt[:, :, H:], 1.0, None, ALU.add))
            dve.wait_ge(ld_const, 16)
            for c in range(4):
                e = dve.tensor_scalar(rep_rhs[:, :, :, c], ab[:, :, :], cst[:, c:c + 1], None, ALU.mult)
                e.then_inc(rep_in, 1)
            dve.wait_ge(rep_in, 4)
            silu(0, 3)
            silu(0, 4)
            silu(0, 5)
            dve.wait_ge(rep_done, 1)
            for dst, src in spread(0, 0):
                dve.tensor_copy(dst, src).then_inc(g_in, 1)
            dve.wait_ge(beta_in, 12)
            for dst, src in spread(0, 1):
                dve.tensor_copy(dst, src).then_inc(g_in, 1)
            v_to_tokens(0)
            dve.wait_ge(par_done, 3)
            dve.wait_ge(g_in, 24)
            dve.wait_ge(beta_in, 24)
            pair_parameters(0)
            factors(0)
            scaled_operands(0)
            dve.wait_ge(zeroed, 8)
            chunk_matrices(0)
            for i in range(HALF - 1):
                substitute(0, i)
            halves(0)
            dve.wait_ge(hid_moved, 32)
            own(dve.tensor_scalar(wtmp[:, :, :], wf[:, :, :], TH_W, SC_W, ALU.is_gt, ALU.mult))
            own(dve.tensor_scalar(wf[:, :, :], wf[:, :, :], -TH_W, -SC_W, ALU.is_lt, ALU.mult))
            own(dve.tensor_tensor(wf[:, :, :], wf[:, :, :], wtmp[:, :, :], ALU.add))
            own(dve.tensor_tensor(wf[:, :, :], wf[:, :, :], wr[:, :, :], ALU.add))
            own(dve.tensor_scalar(wf[:, :, :], wf[:, :, :], -0.5, None, ALU.mult))
            for s in range(3):
                own(dve.tensor_copy(wsplit[:, s, :, :], wf[:, :, :]))
                if s < 2:
                    own(dve.tensor_tensor(wf[:, :, :], wf[:, :, :], wsplit[:, s, :, :], ALU.subtract))
            dve.tensor_copy(identb[:, :], cst[:, C_IDENT:C_IDENT + P]).then_inc(ffn_ready, 1)
            turn(0, True, False)
            assert own.n == VEC_OWN_FIRST, own.n
            with dve.Fori(0, PAIRS - 2) as n:
                own.start(VEC_OWN_FIRST + n * VEC_OWN_TURN)
                turn(n + 1, True, True)
                assert own.n == VEC_OWN_TURN, own.n
            own.start(VEC_OWN_FIRST + (PAIRS - 2) * VEC_OWN_TURN)
            turn(PAIRS - 1, False, True)
            end_head_sums(1)
            rsqrt(head_r[1], head_v[1], t_all[:, 0:UF])
            end_head_scale(1)
            end_to_channels(1)
            end_gate(1)
            end_first_norm(0)
            end_first_norm(1)
            end_second_norm(0)
            end_second_norm(1)


def constants():
    import numpy as np
    p = np.arange(P)[:, None]
    q = np.arange(P)[None, :]
    same = p // CH == q // CH
    c = np.zeros((P, C_END), np.float32)
    c[:, C_QUARTER:C_QUARTER + 4] = p // CH == np.arange(4)
    c[:, C_REP:C_REP + P] = p % CH == q % CH
    c[:, C_TRI:C_TRI + P] = same & (p <= q)
    c[:, C_STRICT:C_STRICT + P] = same & (p > q)
    c[:, C_ONES:C_ONES + P] = same
    c[:, C_IDENT:C_IDENT + P] = p == q
    c[:, C_UPPER:C_UPPER + CH] = p % CH <= np.arange(CH)
    c[:, C_LOWER:C_LOWER + CH] = p % CH > np.arange(CH)
    c[:, C_EYE16:C_EYE16 + HALF] = p % HALF == np.arange(HALF)
    c[:, C_ROWA:C_ROWA + 1] = p % CH < HALF
    c[:, C_ROWB:C_ROWB + 1] = p % CH >= HALF
    return c


def kernel(L0_attn_hidden_states, L0_attn_Wq, L0_attn_Wk, L0_attn_Wv, L0_attn_Wb, L0_attn_Wa, L0_attn_A_log,
           L0_attn_dt_bias, L0_attn_conv_wq, L0_attn_conv_wk, L0_attn_conv_wv, L0_attn_Wg, L0_attn_norm_w,
           L0_attn_Wo, L0_ffn_weight, L0_ffn_rram_variation):
    import numpy as np
    import concourse.bacc as bacc
    from concourse.bass_utils import run_bass_kernel_spmd

    def whole(a):
        return np.ascontiguousarray(np.asarray(a))

    x = np.asarray(L0_attn_hidden_states)
    lo, hi = np.arange(DV // 2), np.arange(DV // 2, DV)
    v_rows = np.concatenate([h * DV + part for heads, part in
                             (((0, 1, 2, 3), lo), ((0, 1, 2, 3), hi), ((4, 5), lo), ((4, 5), hi)) for h in heads])
    a_rows, b_rows = np.arange(4 * DK), np.arange(4 * DK, H * DK)

    def tiles(q, k, v):
        q, k, v = np.asarray(q), np.asarray(k), np.asarray(v)
        return np.concatenate([q[a_rows], k[a_rows], q[b_rows], k[b_rows], v[v_rows]])

    w_proj = np.concatenate([tiles(L0_attn_Wq, L0_attn_Wk, L0_attn_Wv), np.asarray(L0_attn_Wg)[v_rows]])
    arrays = {
        "x": x,
        "x_t": x.reshape(B * T, HID).T.reshape(KT, P, B * T),
        "w_proj": w_proj.T.reshape(KT, P, -1),
        "w_conv": tiles(L0_attn_conv_wq, L0_attn_conv_wk, L0_attn_conv_wv).reshape(CONV_TILES, P, TAPS),
        "w_ab": np.concatenate([np.asarray(L0_attn_Wa), np.asarray(L0_attn_Wb)]).T.reshape(KT, P, 2 * H),
        "a_log": np.asarray(L0_attn_A_log).reshape(1, H),
        "dt_bias": np.asarray(L0_attn_dt_bias).reshape(1, H),
        "norm_w": np.asarray(L0_attn_norm_w)[v_rows % DV].reshape(GATE_TILES, P).T,
        "w_out": np.asarray(L0_attn_Wo).T[v_rows].reshape(GATE_TILES, P, HID),
        "w_ffn": np.asarray(L0_ffn_weight).T.reshape(KT, P, HID),
        "w_rram": np.asarray(L0_ffn_rram_variation).T.reshape(KT, P, HID),
        "consts": constants(),
    }
    arrays = {name: whole(a) for name, a in arrays.items()}
    nc = bacc.Bacc("TRN2", target_bir_lowering=False, num_devices=1)
    aps = {name: nc.dram_tensor(name, a.shape, mybir.dt.from_np(a.dtype), kind="ExternalInput").ap()
           for name, a in arrays.items()}
    out = nc.dram_tensor("out", (B, T, HID), F32, kind="ExternalOutput").ap()
    program(nc, **aps, out=out)
    return run_bass_kernel_spmd(nc, [arrays], core_ids=[0]).results[0]["out"]
```
